# Optimizing a Trainium2 kernel written in Bass

```python
import numpy as np
import jax
import jax.numpy as jnp

def _softmax(x, axis=-1):
    return jax.nn.softmax(x, axis=axis)

def _gelu(x):
    return jax.nn.gelu(x, approximate=True)

def _silu(x):
    return jax.nn.silu(x)

def _sigmoid(x):
    return jax.nn.sigmoid(x)

def _layernorm(x, axis=-1, eps=1e-05):
    m = jnp.mean(x, axis=axis, keepdims=True)
    v = jnp.var(x, axis=axis, keepdims=True)
    return (x - m) / jnp.sqrt(v + eps)

def _scatter_add(tgt, idx, src, axis=0):
    return tgt.at[idx].add(src)

def _segment_sum(src, seg, n):
    return jax.ops.segment_sum(src, seg, n)
kernel_name = 'mk_lm_tower_d2_tok_ids768_r4_5f30a1'

def setup_inputs(seed: int=0):
    np.random.seed(seed)
    _w = jnp.asarray

    def _rec_inputs():
        import jax
        import jax.numpy as jnp
        _rk = jax.random.key(seed)
        x = jax.random.randint(jax.random.fold_in(_rk, 1), (1, 2048), 0, 70, jnp.int32)
        return x
    x = _rec_inputs()

    def _L0_tok_setup():
        import jax, jax.numpy as jnp
        import numpy as np
        import math
        D_MODEL = 192
        BASE = D_MODEL // 3

        def positional_encoding(seq_length, d_model, dtype=jnp.float32):
            pos = jnp.arange(seq_length, dtype=dtype)[:, None]
            i_even = jnp.arange(0, d_model, 2, dtype=dtype)
            inv = jnp.exp(-(i_even / d_model) * math.log(10000.0))
            ang = pos * inv
            pe = jnp.stack([jnp.sin(ang), jnp.cos(ang)], axis=-1)
            return pe.reshape(seq_length, d_model)
        key = jax.random.key(seed)
        k_tok, k_c, k_s, k_q, k_sp = jax.random.split(key, 5)
        tokens = jax.random.randint(k_tok, (64, 512), 0, 70, dtype=jnp.int64)
        scale = 1.0
        color_W = jax.random.normal(k_c, (4, BASE), dtype=jnp.float32) * scale
        shape_W = jax.random.normal(k_s, (4, BASE), dtype=jnp.float32) * scale
        quantity_W = jax.random.normal(k_q, (4, BASE), dtype=jnp.float32) * scale
        special_W = jax.random.normal(k_sp, (6, D_MODEL), dtype=jnp.float32) * scale
        return {'tokens': tokens, 'color_W': color_W, 'shape_W': shape_W, 'quantity_W': quantity_W, 'special_W': special_W}
    _L0_tok_all = _L0_tok_setup()
    _L0_tok_in = {k: v for k, v in _L0_tok_all.items() if k in ('color_W', 'shape_W', 'quantity_W', 'special_W')}
    del _L0_tok_all

    def _L0_attn_setup():
        import jax, jax.numpy as jnp
        import numpy as np
        B, S, D, H = (2, 512, 192, 12)
        DK = D // H

        def _split_heads(t):
            b, s, _ = t.shape
            return t.reshape(b, s, H, DK).transpose(0, 2, 1, 3)
        key = jax.random.key(seed)
        ks = jax.random.split(key, 5)
        sigma = (2.0 / (D + D)) ** 0.5

        def w(k):
            return jnp.clip(jax.random.normal(k, (D, D), dtype=jnp.float32) * sigma, -3 * sigma, 3 * sigma)
        return {'x': jax.random.normal(ks[0], (B, S, D), dtype=jnp.float32), 'Wq': w(ks[1]), 'Wk': w(ks[2]), 'Wv': w(ks[3]), 'Wo': w(ks[4])}
    _L0_attn_all = _L0_attn_setup()
    _L0_attn_in = {k: v for k, v in _L0_attn_all.items() if k in ('Wq', 'Wk', 'Wv', 'Wo')}
    del _L0_attn_all

    def _L0_ffn_setup():
        import jax, jax.numpy as jnp
        import numpy as np
        EPS = 1e-06

        def l2_normalize(x, axis):
            norm = jnp.sqrt(jnp.square(x).sum(axis=axis, keepdims=True))
            return x * (1.0 / (norm + EPS))
        key = jax.random.key(seed)
        ks = jax.random.split(key, 8)
        b, m, d = (32, 256, 192)
        n, p = (8, 4)
        h = d // 8
        X = jax.random.normal(ks[0], (b, m, d), dtype=jnp.float32)
        std_slot = float(np.sqrt(2.0 / (d + n * p)))
        slot_params = jax.random.normal(ks[1], (d, n, p), dtype=jnp.float32) * std_slot
        scale = jnp.ones((), dtype=jnp.float32)
        W_down = jax.random.normal(ks[2], (n, d, h), dtype=jnp.float32) * float(np.sqrt(1.0 / d))
        b_down = jnp.zeros((n, h), dtype=jnp.float32)
        W_up = jax.random.normal(ks[3], (n, h, d), dtype=jnp.float32) * float(np.sqrt(1.0 / h))
        b_up = jnp.zeros((n, d), dtype=jnp.float32)
        return {'X': X, 'slot_params': slot_params, 'scale': scale, 'W_down': W_down, 'b_down': b_down, 'W_up': W_up, 'b_up': b_up}
    _L0_ffn_all = _L0_ffn_setup()
    _L0_ffn_in = {k: v for k, v in _L0_ffn_all.items() if k in ('slot_params', 'scale', 'W_down', 'b_down', 'W_up', 'b_up')}
    del _L0_ffn_all

    def _L1_attn_setup():
        import jax, jax.numpy as jnp
        import numpy as np
        B, T, DM = (4, 512, 192)
        H, D = (4, 64)
        DIM = H * D

        def _feature_map(x):
            return jax.nn.elu(x) + 1.0
        key = jax.random.key(seed)
        kx, kq, kk, kv, ko, kg = jax.random.split(key, 6)
        s = 0.02
        return {'x': jax.random.normal(kx, (B, T, DM), jnp.float32), 'Wq': jax.random.normal(kq, (DM, DIM), jnp.float32) * s, 'Wk': jax.random.normal(kk, (DM, DIM), jnp.float32) * s, 'Wv': jax.random.normal(kv, (DM, DIM), jnp.float32) * s, 'Wo': jax.random.normal(ko, (DIM, DM), jnp.float32) * s, 'Wg': jax.random.normal(kg, (DM, DM), jnp.float32) * s}
    _L1_attn_all = _L1_attn_setup()
    _L1_attn_in = {k: v for k, v in _L1_attn_all.items() if k in ('Wq', 'Wk', 'Wv', 'Wo', 'Wg')}
    del _L1_attn_all

    def _L1_ffn_setup():
        import jax, jax.numpy as jnp
        import numpy as np
        NUM_EXPERTS = 8
        TOP_K = 2
        CAPACITY_FACTOR = 1.25
        MAX_GROUP_SIZE = 1024
        MIN_EXPERT_CAPACITY = 4

        def _moe_forward(x, w_router, wi, wo):
            B, T, D = x.shape
            E = NUM_EXPERTS
            num_tokens = B * T
            G = max(num_tokens // MAX_GROUP_SIZE, E)
            while num_tokens % G != 0 or G % E != 0:
                G += 1
            S = num_tokens // G
            C = max(int(TOP_K * CAPACITY_FACTOR * S / E), MIN_EXPERT_CAPACITY)
            xg = x.reshape(G, S, D)
            logits = jnp.einsum('gsd,de->gse', xg.astype(jnp.float32), w_router.astype(jnp.float32))
            probs = jax.nn.softmax(logits, axis=-1)
            gate, idx = jax.lax.top_k(probs, TOP_K)
            idx_kf = jnp.swapaxes(idx, 1, 2).reshape(G, TOP_K * S)
            mask = jax.nn.one_hot(idx_kf, E, dtype=jnp.int32)
            prio = jnp.cumsum(mask, axis=1) * mask - 1
            prio = jnp.swapaxes(prio.reshape(G, TOP_K, S, E), 1, 2)
            prio_se = prio.max(axis=2)
            gate_se = jnp.einsum('gsk,gske->gse', gate, jax.nn.one_hot(idx, E, dtype=gate.dtype))
            dispatch = jax.nn.one_hot(prio_se, C, dtype=x.dtype)
            combine = dispatch * gate_se[..., None].astype(x.dtype)
            expert_in = jnp.einsum('gsec,gsd->egcd', dispatch, xg)
            h = jax.nn.relu(jnp.einsum('egcd,edf->egcf', expert_in, wi))
            expert_out = jnp.einsum('egcf,efd->egcd', h, wo)
            out = jnp.einsum('gsec,egcd->gsd', combine, expert_out)
            return out.reshape(B, T, D)
        key = jax.random.key(seed)
        k1, k2, k3, k4 = jax.random.split(key, 4)
        B, T, D, F = (8, 256, 192, 768)
        x = jax.random.normal(k1, (B, T, D), jnp.float32)
        w_router = jax.random.normal(k2, (D, NUM_EXPERTS), jnp.float32) * D ** (-0.5)
        wi = jax.random.normal(k3, (NUM_EXPERTS, D, F), jnp.float32) * D ** (-0.5)
        wo = jax.random.normal(k4, (NUM_EXPERTS, F, D), jnp.float32) * F ** (-0.5)
        return {'x': x, 'w_router': w_router, 'wi': wi, 'wo': wo}
    _L1_ffn_all = _L1_ffn_setup()
    _L1_ffn_in = {k: v for k, v in _L1_ffn_all.items() if k in ('w_router', 'wi', 'wo')}
    del _L1_ffn_all
    return {'x': x, 'L0_tok_color_W': _L0_tok_in['color_W'], 'L0_tok_shape_W': _L0_tok_in['shape_W'], 'L0_tok_quantity_W': _L0_tok_in['quantity_W'], 'L0_tok_special_W': _L0_tok_in['special_W'], 'L0_attn_Wq': _L0_attn_in['Wq'], 'L0_attn_Wk': _L0_attn_in['Wk'], 'L0_attn_Wv': _L0_attn_in['Wv'], 'L0_attn_Wo': _L0_attn_in['Wo'], 'L0_ffn_slot_params': _L0_ffn_in['slot_params'], 'L0_ffn_scale': _L0_ffn_in['scale'], 'L0_ffn_W_down': _L0_ffn_in['W_down'], 'L0_ffn_b_down': _L0_ffn_in['b_down'], 'L0_ffn_W_up': _L0_ffn_in['W_up'], 'L0_ffn_b_up': _L0_ffn_in['b_up'], 'L1_attn_Wq': _L1_attn_in['Wq'], 'L1_attn_Wk': _L1_attn_in['Wk'], 'L1_attn_Wv': _L1_attn_in['Wv'], 'L1_attn_Wo': _L1_attn_in['Wo'], 'L1_attn_Wg': _L1_attn_in['Wg'], 'L1_ffn_w_router': _L1_ffn_in['w_router'], 'L1_ffn_wi': _L1_ffn_in['wi'], 'L1_ffn_wo': _L1_ffn_in['wo']}

def reference(x, L0_tok_color_W, L0_tok_shape_W, L0_tok_quantity_W, L0_tok_special_W, L0_attn_Wq, L0_attn_Wk, L0_attn_Wv, L0_attn_Wo, L0_ffn_slot_params, L0_ffn_scale, L0_ffn_W_down, L0_ffn_b_down, L0_ffn_W_up, L0_ffn_b_up, L1_attn_Wq, L1_attn_Wk, L1_attn_Wv, L1_attn_Wo, L1_attn_Wg, L1_ffn_w_router, L1_ffn_wi, L1_ffn_wo):
    import jax
    import jax.numpy as jnp

    def _L0_tok_ref(tokens, color_W, shape_W, quantity_W, special_W):
        import jax, jax.numpy as jnp
        import numpy as np
        import math
        D_MODEL = 192
        BASE = D_MODEL // 3

        def positional_encoding(seq_length, d_model, dtype=jnp.float32):
            pos = jnp.arange(seq_length, dtype=dtype)[:, None]
            i_even = jnp.arange(0, d_model, 2, dtype=dtype)
            inv = jnp.exp(-(i_even / d_model) * math.log(10000.0))
            ang = pos * inv
            pe = jnp.stack([jnp.sin(ang), jnp.cos(ang)], axis=-1)
            return pe.reshape(seq_length, d_model)
        B, S = tokens.shape
        d_model = special_W.shape[1]
        t = jnp.minimum(tokens, 63)
        color = t // 16
        shape = t % 16 // 4
        quantity = t % 4
        feat_emb = jnp.concatenate([color_W[color], shape_W[shape], quantity_W[quantity]], axis=-1)
        sp_idx = jnp.clip(tokens - 64, 0, special_W.shape[0] - 1)
        spec_emb = special_W[sp_idx]
        emb = jnp.where((tokens < 64)[..., None], feat_emb, spec_emb)
        pe = positional_encoding(S, d_model, dtype=emb.dtype)
        out = emb * jnp.asarray(math.sqrt(d_model), emb.dtype) + pe[None, :, :]
        return out

    def _L0_attn_ref(x, Wq, Wk, Wv, Wo):
        import jax, jax.numpy as jnp
        import numpy as np
        B, S, D, H = (2, 512, 192, 12)
        DK = D // H

        def _split_heads(t):
            b, s, _ = t.shape
            return t.reshape(b, s, H, DK).transpose(0, 2, 1, 3)
        q = _split_heads(jnp.einsum('bsd,od->bso', x, Wq))
        k = _split_heads(jnp.einsum('bsd,od->bso', x, Wk))
        v = _split_heads(jnp.einsum('bsd,od->bso', x, Wv))
        norm = jax.lax.rsqrt(jnp.asarray(DK, dtype=x.dtype))
        scores = jnp.einsum('bhid,bhjd->bhij', q, k) * norm
        s = x.shape[-2]
        causal = jnp.tril(jnp.ones((s, s), dtype=bool))
        scores = jnp.where(causal, scores, -jnp.inf)
        attn = jax.nn.softmax(scores, axis=-1)
        out = jnp.einsum('bhij,bhjd->bhid', attn, v)
        out = out.transpose(0, 2, 1, 3).reshape(x.shape[0], s, D)
        return jnp.einsum('bsd,od->bso', out, Wo)

    def _L0_ffn_ref(X, slot_params, scale, W_down, b_down, W_up, b_up):
        import jax, jax.numpy as jnp
        import numpy as np
        EPS = 1e-06

        def l2_normalize(x, axis):
            norm = jnp.sqrt(jnp.square(x).sum(axis=axis, keepdims=True))
            return x * (1.0 / (norm + EPS))
        b, m, d = X.shape
        _, n, p = slot_params.shape
        Xn = l2_normalize(X, axis=-1)
        sp = l2_normalize(slot_params, axis=1) * scale
        logits = jnp.einsum('bmd,dnp->bmnp', Xn, sp)
        D = jax.nn.softmax(logits, axis=1)
        C = jax.nn.softmax(logits.reshape(b, m, n * p), axis=2).reshape(b, m, n, p)
        X_tilde = jnp.einsum('bmd,bmnp->bnpd', Xn, D)
        H = jax.nn.gelu(jnp.einsum('bnpd,ndh->bnph', X_tilde, W_down) + b_down[None, :, None, :], approximate=False)
        Y_tilde = jnp.einsum('bnph,nhd->bnpd', H, W_up) + b_up[None, :, None, :]
        Y = jnp.einsum('bnpd,bmnp->bmd', Y_tilde, C)
        return Y

    def _L1_attn_ref(x, Wq, Wk, Wv, Wo, Wg):
        import jax, jax.numpy as jnp
        import numpy as np
        B, T, DM = (4, 512, 192)
        H, D = (4, 64)
        DIM = H * D

        def _feature_map(x):
            return jax.nn.elu(x) + 1.0
        Bx, Tx, _ = x.shape
        q = _feature_map((x @ Wq).reshape(Bx, Tx, H, D))
        k = _feature_map((x @ Wk).reshape(Bx, Tx, H, D))
        v = (x @ Wv).reshape(Bx, Tx, H, D)
        qT = q.transpose(1, 0, 2, 3)
        kT = k.transpose(1, 0, 2, 3)
        vT = v.transpose(1, 0, 2, 3)
        S0 = jnp.zeros((Bx, H, D, D), x.dtype)
        z0 = jnp.zeros((Bx, H, D), x.dtype)

        def step(carry, inp):
            S, z = carry
            qi, ki, vi = inp
            S = S + ki[..., :, None] * vi[..., None, :]
            z = z + ki
            num = jnp.einsum('bhd,bhde->bhe', qi, S)
            den = jnp.maximum(jnp.sum(qi * z, axis=-1), 1e-06)
            return ((S, z), num / den[..., None])
        (_, _), outT = jax.lax.scan(step, (S0, z0), (qT, kT, vT))
        out = outT.transpose(1, 0, 2, 3).reshape(Bx, Tx, DIM)
        gate = jax.nn.sigmoid(x @ Wg)
        return out @ Wo * gate

    def _L1_ffn_ref(x, w_router, wi, wo):
        import jax, jax.numpy as jnp
        import numpy as np
        NUM_EXPERTS = 8
        TOP_K = 2
        CAPACITY_FACTOR = 1.25
        MAX_GROUP_SIZE = 1024
        MIN_EXPERT_CAPACITY = 4

        def _moe_forward(x, w_router, wi, wo):
            B, T, D = x.shape
            E = NUM_EXPERTS
            num_tokens = B * T
            G = max(num_tokens // MAX_GROUP_SIZE, E)
            while num_tokens % G != 0 or G % E != 0:
                G += 1
            S = num_tokens // G
            C = max(int(TOP_K * CAPACITY_FACTOR * S / E), MIN_EXPERT_CAPACITY)
            xg = x.reshape(G, S, D)
            logits = jnp.einsum('gsd,de->gse', xg.astype(jnp.float32), w_router.astype(jnp.float32))
            probs = jax.nn.softmax(logits, axis=-1)
            gate, idx = jax.lax.top_k(probs, TOP_K)
            idx_kf = jnp.swapaxes(idx, 1, 2).reshape(G, TOP_K * S)
            mask = jax.nn.one_hot(idx_kf, E, dtype=jnp.int32)
            prio = jnp.cumsum(mask, axis=1) * mask - 1
            prio = jnp.swapaxes(prio.reshape(G, TOP_K, S, E), 1, 2)
            prio_se = prio.max(axis=2)
            gate_se = jnp.einsum('gsk,gske->gse', gate, jax.nn.one_hot(idx, E, dtype=gate.dtype))
            dispatch = jax.nn.one_hot(prio_se, C, dtype=x.dtype)
            combine = dispatch * gate_se[..., None].astype(x.dtype)
            expert_in = jnp.einsum('gsec,gsd->egcd', dispatch, xg)
            h = jax.nn.relu(jnp.einsum('egcd,edf->egcf', expert_in, wi))
            expert_out = jnp.einsum('egcf,efd->egcd', h, wo)
            out = jnp.einsum('gsec,egcd->gsd', combine, expert_out)
            return out.reshape(B, T, D)
        return _moe_forward(x, w_router, wi, wo)
    h = _L0_tok_ref(x, L0_tok_color_W, L0_tok_shape_W, L0_tok_quantity_W, L0_tok_special_W)
    h = h + _L0_attn_ref(_layernorm(h, axis=-1), L0_attn_Wq, L0_attn_Wk, L0_attn_Wv, L0_attn_Wo)
    h = h + _L0_ffn_ref(_layernorm(h, axis=-1), L0_ffn_slot_params, L0_ffn_scale, L0_ffn_W_down, L0_ffn_b_down, L0_ffn_W_up, L0_ffn_b_up)
    h = h + _L1_attn_ref(_layernorm(h, axis=-1), L1_attn_Wq, L1_attn_Wk, L1_attn_Wv, L1_attn_Wo, L1_attn_Wg)
    h = h + _L1_ffn_ref(_layernorm(h, axis=-1), L1_ffn_w_router, L1_ffn_wi, L1_ffn_wo)
    return h

_drawn_inputs = setup_inputs


def setup_inputs(seed=0):
    import zlib

    import numpy as np

    out = dict(_drawn_inputs(seed))
    spreads = {'L0_ffn_b_down': (0.0, 0.8), 'L0_ffn_b_up': (0.0, 2.0)}
    factors = {'L0_attn_Wq': 3.081,
     'L0_attn_Wk': 2.891,
     'L0_ffn_slot_params': 8.0,
     'L0_ffn_W_down': 8.0,
     'L0_ffn_W_up': 8.0,
     'L1_attn_Wq': 52.703,
     'L1_attn_Wk': 38.226,
     'L1_attn_Wv': 8.0,
     'L1_attn_Wo': 8.0,
     'L1_attn_Wg': 8.0,
     'L1_ffn_w_router': 2.803,
     'L1_ffn_wi': 2.839}
    for name, (base, spread) in spreads.items():
        noise = np.random.default_rng([zlib.crc32(name.encode()), seed]).standard_normal(out[name].shape)
        drawn = base * np.exp(spread * noise) if base else spread * noise
        out[name] = jnp.asarray(drawn.astype(out[name].dtype))
    for name, factor in factors.items():
        out[name] = (out[name] * factor).astype(out[name].dtype)
    return out
```

```python
import math
from contextlib import ExitStack, contextmanager

import numpy as np
import concourse.bass as bass
from concourse import mybir

F32 = mybir.dt.float32
BF16 = mybir.dt.bfloat16
I32 = mybir.dt.int32
ALU = mybir.AluOpType
ACT = mybir.ActivationFunctionType
AX = mybir.AxisListType

P = 128
S = 2048
D = 192
NT = S // P
KH = D // 2
QW = 512
NQ = S // QW
TPQ = QW // P
VOCAB = 70

H0 = 12
DK0 = D // H0
HG = 4
NG = H0 // HG
HROW = P // HG
STACK = 6 * DK0
PARTS_Q = (0, 0, 0, 1, 1, 2)
PARTS_K = (0, 1, 2, 0, 1, 0)

NSLOT, PSLOT, HDOWN = 8, 4, 24
NP = NSLOT * PSLOT

H1, D1 = 4, 64
DIM1 = H1 * D1
NPAIR = H1 // 2

E = 8
F = 768
NF = F // P
GRP = 8
SG = S // GRP
CAP = 80
TPG = SG // P
SLOTS = GRP * CAP
EHALF = E * CAP // 2

MASKED = -1.0e30
C_ID, C_TRI, C_MQK, C_MKQ, C_SEL, C_ONE, C_IOTA, C_PIDX, C_RANK = 0, 128, 256, 384, 512, 640, 768, 848, 849
C_ALL = 857


def constants():
    p, f = np.arange(P)[:, None], np.arange(P)[None, :]
    c = np.zeros((P, C_ALL), np.float32)
    c[:, C_ID:C_ID + P] = p == f
    c[:, C_TRI:C_TRI + P] = p <= f
    c[:, C_MQK:C_MQK + P] = np.where(f > p, MASKED, 0)
    c[:, C_MKQ:C_MKQ + P] = np.where(p > f, MASKED, 0)
    c[:, C_SEL:C_SEL + P] = p == HROW * (f // HROW) + DK0
    c[:, C_ONE:C_ONE + P] = 1
    c[:, C_IOTA:C_IOTA + CAP] = np.arange(CAP)
    c[:, C_PIDX] = np.arange(P)
    c[:, C_RANK:C_RANK + E] = np.arange(E, 0, -1)
    pos = np.arange(S, dtype=np.float32)[:, None]
    even = np.arange(0, D, 2, dtype=np.float32)
    exponent = -(even / np.float32(D)) * np.float32(math.log(10000.0))
    angle = pos * np.exp(exponent.astype(np.float64)).astype(np.float32)
    pe = np.stack([np.sin(angle), np.cos(angle)], axis=-1).reshape(S, D).astype(np.float32)
    return c, pe


class Core:

    def __init__(self, nc, ctx):
        self.nc = nc
        self.ctx = ctx
        self.sems = ctx
        self.h = self.sb("h", [P, NT, D])
        self.xn = self.sb("xn", [P, NT, D])
        self.xnT = self.sb("xnT", [KH, 2, S])
        self.cst = self.sb("cst", [P, C_ALL])
        self.identb = self.sb("identb", [P, P], BF16)
        self.mqkb = self.sb("mqkb", [P, P], BF16)
        self.mkqb = self.sb("mkqb", [P, P], BF16)
        self.trib = self.sb("trib", [P, P], BF16)
        self.oneb = self.sb("oneb", [P, P], BF16)
        self.stats = self.sb("stats", [P, NT, 6])
        self.mv = self.sb("mv", [P, NT, 2])
        self.ve = self.sb("ve", [P, NT])
        self.sd = self.sb("sd", [P, NT])
        self.rstd = self.sb("rstd", [P, NT])
        self.PS = ctx.enter_context(nc.psum_tensor("PS", [P, 8, 512], F32))
        self.ident = self.cst[:, C_ID:C_ID + P]
        self.tri = self.cst[:, C_TRI:C_TRI + P]

    def sb(self, name, shape, dt=F32):
        return self.ctx.enter_context(self.nc.sbuf_tensor(name, shape, dt))

    def sem(self, name):
        return self.sems.enter_context(self.nc.semaphore(name))

    @contextmanager
    def room(self):
        outer = self.ctx
        with ExitStack() as self.ctx:
            yield
        self.ctx = outer


def embed(nc, k, a):
    tok = k.sb("tok", [VOCAB, S], I32)
    onehot = k.xnT[0:VOCAB, 0, :]
    table = k.sb("table", [VOCAB, D])
    pe = k.xn
    landed = k.sem("emb_landed")
    pe_landed = k.sem("pe_landed")
    onehot_made = k.sem("onehot_made")
    rows_made = k.sem("rows_made")
    h_made = k.sem("h_made")
    base = D // 3
    with nc.Block() as block:
        @block.sync
        def _(sp):
            sp.dma_start(k.cst[:, :], a["consts"]).then_inc(landed, 16)
            sp.dma_start(tok[:, :], a["x"].to_broadcast([VOCAB, S])).then_inc(landed, 16)
            sp.dma_start(table[0:64, 0:base], a["L0_tok_color_W"].unsqueeze(1).to_broadcast([4, 16, base])).then_inc(landed, 16)
            for c in range(4):
                sp.dma_start(table[16 * c:16 * c + 16, base:2 * base],
                             a["L0_tok_shape_W"].unsqueeze(1).to_broadcast([4, 4, base])).then_inc(landed, 16)
            sp.dma_start(table[0:64, 2 * base:D], a["L0_tok_quantity_W"].unsqueeze(0).to_broadcast([16, 4, base])).then_inc(landed, 16)
            sp.dma_start(table[64:VOCAB, :], a["L0_tok_special_W"]).then_inc(landed, 16)
            sp.dma_start(pe[:, :, :], a["pe"].rearrange("(t p) d -> p t d", p=P)).then_inc(pe_landed, 16)

        @block.vector
        def _(dve):
            dve.wait_ge(landed, 16 * 9)
            nc.vector.tensor_scalar(onehot, tok[:, :], float(VOCAB - 1), k.cst[0:VOCAB, C_PIDX:C_PIDX + 1],
                                    ALU.min, ALU.is_equal).then_inc(onehot_made, 1)
            for dst, c in ((k.identb, C_ID), (k.mqkb, C_MQK), (k.mkqb, C_MKQ), (k.trib, C_TRI), (k.oneb, C_ONE)):
                nc.vector.tensor_copy(dst[:, :], k.cst[:, c:c + P])
            dve.wait_ge(pe_landed, 16)
            for t in range(NT):
                dve.wait_ge(rows_made, t + 1)
                nc.vector.scalar_tensor_tensor(k.h[:, t, :], k.PS[:, t % 8, 0:D], math.sqrt(D),
                                               pe[:, t, :], ALU.mult, ALU.add).then_inc(h_made, 1)

        @block.tensor
        def _(te):
            te.wait_ge(onehot_made, 1)
            for t in range(NT):
                if t >= 8:
                    te.wait_ge(h_made, t - 7)
                nc.tensor.matmul(k.PS[:, t % 8, 0:D], onehot[:, t * P:(t + 1) * P], table[:, :],
                                 start=True, stop=True).then_inc(rows_made, 1)


def layernorm(nc, k, name, l2=False):
    stats_made = k.sem(name + "_stats_made")
    mv_made = k.sem(name + "_mv_made")
    small = k.sem(name + "_small")
    rooted = k.sem(name + "_rooted")
    xn_made = k.sem(name + "_xn_made")
    turned = k.sem(name + "_turned")
    with nc.Block() as block:
        @block.vector
        def _(dve):
            for t in range(NT):
                nc.vector.bn_stats(k.stats[:, t, :], k.h[:, t, :]).then_inc(stats_made, 1)
            for t in range(NT):
                dve.wait_ge(stats_made, t + 1)
                nc.vector.bn_aggr(k.mv[:, t, :], k.stats[:, t, :]).then_inc(mv_made, 1)
            dve.wait_ge(mv_made, NT)
            nc.vector.tensor_scalar(k.ve[:, :], k.mv[:, :, 1], 1e-5, None, ALU.add).then_inc(small, 1)
            dve.wait_ge(rooted, 1)
            nc.vector.reciprocal(k.rstd[:, :], k.sd[:, :]).then_inc(small, 1)
            dve.wait_ge(small, 2)
            if l2:
                nc.vector.scalar_tensor_tensor(k.ve[:, :], k.mv[:, :, 1], float(D), k.rstd[:, :], ALU.mult, ALU.mult).then_inc(small, 1)
                dve.wait_ge(small, 3)
                nc.vector.tensor_tensor(k.ve[:, :], k.ve[:, :], k.rstd[:, :], ALU.mult).then_inc(small, 1)
                dve.wait_ge(rooted, 2)
                nc.vector.tensor_scalar(k.ve[:, :], k.sd[:, :], 1e-6, None, ALU.add).then_inc(small, 1)
                dve.wait_ge(small, 5)
                nc.vector.reciprocal(k.sd[:, :], k.ve[:, :]).then_inc(small, 1)
                dve.wait_ge(small, 6)
                nc.vector.tensor_tensor(k.rstd[:, :], k.rstd[:, :], k.sd[:, :], ALU.mult).then_inc(small, 1)
                dve.wait_ge(small, 7)
            for t in range(NT):
                nc.vector.tensor_scalar(k.xn[:, t, :], k.h[:, t, :], k.mv[:, t, 0:1], k.rstd[:, t:t + 1],
                                        ALU.subtract, ALU.mult).then_inc(xn_made, 1)

        @block.scalar
        def _(act):
            act.wait_ge(small, 1)
            nc.scalar.activation(k.sd[:, :], k.ve[:, :], ACT.Sqrt).then_inc(rooted, 1)
            if l2:
                act.wait_ge(small, 4)
                nc.scalar.activation(k.sd[:, :], k.ve[:, :], ACT.Sqrt).then_inc(rooted, 1)
            for u in range(NT // 2):
                act.wait_ge(turned, u + 1)
                nc.scalar.activation(k.xnT[:, :, 2 * u * P:2 * (u + 1) * P],
                                     k.PS[0:KH, u, :].rearrange("p (k n) -> p k n", k=2), ACT.Copy)

        @block.tensor
        def _(te):
            for u in range(NT // 2):
                te.wait_ge(xn_made, 2 * u + 2)
                for i in range(2):
                    for half in range(2):
                        last = nc.tensor.transpose(k.PS[0:KH, u, half * 256 + i * P:half * 256 + (i + 1) * P],
                                                   k.xn[:, 2 * u + i, half * KH:(half + 1) * KH], k.ident)
                last.then_inc(turned, 1)


def softmax_qkv(nc, k, a, att):
    w = [k.sb(f"w0_{m}", [KH, 2, D]) for m in "qkv"]
    RING = 4
    parts = k.sb("parts", [KH, RING, 3, QW], BF16)
    rest = k.sb("rest", [KH, 2, QW])
    w_landed = k.sem("w0_landed")
    made = k.sem("qkv_made")
    part1 = k.sem("part1_made")
    rest1 = k.sem("rest1_made")
    part2 = k.sem("part2_made")
    part3 = k.sem("part3_made")
    v_kept = k.sem("v_kept")
    stored = [k.sem(f"parts_stored{i}") for i in range(RING)]
    units = [(m, mt, c) for m in range(2) for mt in range(2) for c in range(NQ)]
    NU = len(units)
    scale = (DK0 ** -0.5, 1.0)
    with nc.Block() as block:
        @block.sync
        def _(sp):
            for m, name in enumerate(("wq0", "wk0", "wv0")):
                sp.dma_start(w[m][:, :, :], a[name].rearrange("(k p) o -> p k o", p=KH)).then_inc(w_landed, 16)
            for n, (m, mt, c) in enumerate(units):
                sp.wait_ge(part3, n + 1)
                sp.dma_start(att["scratch"][m, :, mt * KH:(mt + 1) * KH, c * QW:(c + 1) * QW].rearrange("g r n -> r g n"),
                             parts[:, n % RING, :, :]).then_inc(stored[n % RING], 16)
            for i in range(RING):
                sp.wait_ge(stored[i], 16 * (NU // RING))

        @block.gpsimd
        def _(pool):
            nc.gpsimd.memset(att["v"][:, :, :, DK0:HROW], 0.0).then_inc(att["v_cleared"], 1)
            pool.wait_ge(att["v_cleared"], 1)
            nc.gpsimd.memset(att["v"][:, :, :, DK0:DK0 + 1], 1.0).then_inc(att["v_cleared"], 1)
            pool.wait_ge(att["v_cleared"], 2)
            nc.gpsimd.memset(att["ks"][STACK:STACK + 3, :, :, :], 1.0)

        @block.tensor
        def _(te):
            te.wait_ge(w_landed, 48)
            for n, (m, mt, c) in enumerate(units):
                if n >= 8:
                    te.wait_ge(rest1, n - 7)
                for half in range(2):
                    last = nc.tensor.matmul(k.PS[0:KH, n % 8, :], w[m][:, half, mt * KH:(mt + 1) * KH],
                                            k.xnT[:, half, c * QW:(c + 1) * QW], start=half == 0, stop=half == 1)
                last.then_inc(made, 1)
            for t in range(NT):
                if t < 8:
                    te.wait_ge(rest1, NU - 7 + t)
                else:
                    te.wait_ge(v_kept, t - 7)
                for half in range(2):
                    last = nc.tensor.matmul(k.PS[:, t % 8, 0:D], k.xnT[:, half, t * P:(t + 1) * P], w[2][:, half, :],
                                            start=half == 0, stop=half == 1)
                last.then_inc(made, 1)

        @block.scalar
        def _(act):
            def second(n):
                act.wait_ge(rest1, n + 1)
                nc.scalar.activation(parts[:, n % RING, 1, :], rest[:, n % 2, :], ACT.Copy).then_inc(part2, 1)

            for n, (m, mt, c) in enumerate(units):
                act.wait_ge(made, n + 1)
                if n >= RING:
                    act.wait_ge(stored[n % RING], 16 * (n // RING))
                nc.scalar.activation(parts[:, n % RING, 0, :], k.PS[0:KH, n % 8, :], ACT.Copy, scale=scale[m]).then_inc(part1, 1)
                if n >= 1:
                    second(n - 1)
            second(NU - 1)
            for t in range(NT):
                act.wait_ge(made, NU + t + 1)
                nc.scalar.activation(att["v"][:, t, :, 0:DK0], k.PS[:, t % 8, 0:D].rearrange("p (h d) -> p h d", d=DK0),
                                     ACT.Copy).then_inc(v_kept, 1)

        @block.vector
        def _(dve):
            def third(n):
                dve.wait_ge(part2, n + 1)
                nc.vector.tensor_tensor(parts[:, n % RING, 2, :], rest[:, n % 2, :], parts[:, n % RING, 1, :],
                                        ALU.subtract).then_inc(part3, 1)

            for n, (m, mt, c) in enumerate(units):
                dve.wait_ge(part1, n + 1)
                if n >= 2:
                    dve.wait_ge(part3, n - 1)
                nc.vector.scalar_tensor_tensor(rest[:, n % 2, :], k.PS[0:KH, n % 8, :], scale[m], parts[:, n % RING, 0, :],
                                               ALU.mult, ALU.subtract).then_inc(rest1, 1)
                if n >= 1:
                    third(n - 1)
            third(NU - 1)


STEPS = [(g, c) for g in range(NG) for c in range(NQ)]
SMAX, SBANK = 3, 3
B_MAX, B_SC, B_PV, B_MISC = 0, 3, 6, 7


def max_units(step):
    g, c = STEPS[step]
    return [(qt, j, kc) for qt in range(TPQ * c, TPQ * (c + 1)) for j in range(HG) for kc in range(c + 1)]


def key_tiles(step):
    return TPQ * (STEPS[step][1] + 1)


def interleave():
    order, ahead, behind, lead = [], 0, 0, 40 * QW
    pending = [("max", s, u) for s in range(len(STEPS)) for u in max_units(s)]
    last = {s: len(max_units(s)) for s in range(len(STEPS))}

    def width(u):
        qt, _, kc = u
        return min(QW, (qt + 1) * P - kc * QW)

    for s in range(len(STEPS)):
        for kt in range(key_tiles(s)):
            while pending and (pending[0][1] <= s or ahead < behind + lead):
                _, ms, u = pending.pop(0)
                order.append(("max", ms, u))
                ahead += width(u)
                last[ms] -= 1
                if not last[ms]:
                    order.append(("turn", ms, None))
            if kt == 0 and s >= 1:
                order.append(("values", s - 1, key_tiles(s - 1) - 1))
                order.append(("spread", s - 1, None))
            order.append(("scores", s, kt))
            behind += HG * (QW - max(0, kt - TPQ * STEPS[s][1]) * P)
            if kt >= 1:
                order.append(("values", s, kt - 1))
    order.append(("values", len(STEPS) - 1, key_tiles(len(STEPS) - 1) - 1))
    order.append(("spread", len(STEPS) - 1, None))
    return order


def softmax_attention(nc, k, a, att):
    qs, ks, v, o = att["qs"], att["ks"], att["v"], att["o"]
    NS = len(STEPS)
    pmax = k.sb("pmax", [P, 2, TPQ, HG, NQ])
    negm = k.sb("negm", [P, 2, HG, TPQ])
    negr = k.sb("negr", [P, 2, HG, TPQ])
    mparts = k.sb("mparts", [P, 2, HG, 3, TPQ], BF16)
    mT = k.sb("mT", [HG * 3 * TPQ, 2, P], BF16)
    probs = k.sb("probs", [P, 2, HG, QW])
    orec = k.sb("orec", [P, QW])
    loaded = [k.sem(f"stack_loaded{g}") for g in range(NG)]
    max_scored = k.sem("max_scored")
    max_taken = k.sem("max_taken")
    m_chain = k.sem("m_chain")
    m_turned = k.sem("m_turned")
    m_kept = k.sem("m_kept")
    m_placed = [k.sem(f"m_placed{s}") for s in range(NS)]
    scored = k.sem("scored")
    exped = k.sem("exped")
    summed = k.sem("summed")
    o_kept = k.sem("o_kept")
    spread = k.sem("spread")
    inverted = k.sem("inverted")
    o_done = k.sem("o_done")

    nmax = [0]
    for s in range(NS):
        nmax.append(nmax[-1] + len(max_units(s)))
    nkey = [0]
    for s in range(NS):
        nkey.append(nkey[-1] + key_tiles(s))
    M_OPS = 5

    order = interleave()

    def live(s, kt):
        return max(0, kt - TPQ * STEPS[s][1]) * P

    with nc.Block() as block:
        @block.sync
        def _(sp):
            def load(g):
                b = g % 2
                for j in range(HG):
                    r = (g * HG + j) * DK0
                    for m, stack, lot in ((0, qs, PARTS_Q), (1, ks, PARTS_K)):
                        at = 0
                        while at < 6:
                            n = 1
                            step = lot[at + 1] - lot[at] if at + 1 < 6 else 0
                            while at + n < 6 and step in (0, 1) and lot[at + n] - lot[at + n - 1] == step:
                                n += 1
                            src = att["scratch"][m, lot[at]:lot[at] + (n if step == 1 else 1), r:r + DK0, :]
                            if n > 1 and step == 0:
                                src = src.to_broadcast([n, DK0, S])
                            sp.dma_start(stack[at * DK0:(at + n) * DK0, b, j, :], src).then_inc(loaded[g], 16)
                            att["loads"][g] += 16
                            at += n

            load(0)
            load(1)
            for s, (g, c) in enumerate(STEPS):
                sp.wait_ge(m_kept, s + 1)
                for j in range(HG):
                    sp.dma_start(qs[STACK:STACK + 3, g % 2, j, c * QW:(c + 1) * QW].rearrange("r (t n) -> r t n", n=P),
                                 mT[j * 3 * TPQ:(j + 1) * 3 * TPQ, s % 2, :]).then_inc(m_placed[s], 16)
                if g == 1 and c == 0:
                    sp.wait_ge(scored, HG * nkey[NQ])
                    load(2)

        @block.tensor
        def _(te):
            u = turns = spreads = 0
            for what, s, arg in order:
                g, c = STEPS[s]
                b = g % 2
                if what == "max":
                    qt, j, kc = arg
                    if u == nmax[s] and c == 0:
                        te.wait_ge(loaded[g], att["loads"][g])
                    if u >= SMAX:
                        te.wait_ge(max_taken, u - SMAX + 1)
                    diagonal = kc == c
                    w = (qt % TPQ + 1) * P if diagonal else QW
                    bank = B_MAX + u % SMAX
                    mm = nc.tensor.matmul(k.PS[:, bank, 0:w], qs[0:STACK, b, j, qt * P:(qt + 1) * P],
                                          ks[0:STACK, b, j, kc * QW:kc * QW + w], start=True, stop=not diagonal)
                    if diagonal:
                        mm = nc.tensor.matmul(k.PS[:, bank, w - P:w], k.identb[:, :], k.mqkb[:, :], start=False, stop=True)
                    mm.then_inc(max_scored, 1)
                    u += 1
                elif what == "turn":
                    te.wait_ge(m_chain, M_OPS * (s + 1))
                    if spreads:
                        te.wait_ge(inverted, spreads)
                    turns += 1
                    if s:
                        te.wait_ge(m_kept, s)
                    nc.tensor.transpose(k.PS[:, B_MISC, :].bitcast(BF16)[0:HG * 3 * TPQ, 0:P],
                                        mparts[:, s % 2].rearrange("p j r t -> p (j r t)"), k.identb[:, :]).then_inc(m_turned, 1)
                elif what == "scores":
                    n = nkey[s] + arg
                    if arg == 0:
                        te.wait_ge(m_placed[s], 16 * HG)
                    off = live(s, arg)
                    for j in range(HG):
                        i = HG * n + j
                        if i >= SBANK:
                            te.wait_ge(exped, i - SBANK + 1)
                        diagonal = arg >= TPQ * c
                        bank = B_SC + i % SBANK
                        mm = nc.tensor.matmul(k.PS[:, bank, off:QW], ks[0:STACK + 3, b, j, arg * P:(arg + 1) * P],
                                              qs[0:STACK + 3, b, j, c * QW + off:(c + 1) * QW], start=True, stop=not diagonal)
                        if diagonal:
                            mm = nc.tensor.matmul(k.PS[:, bank, off:off + P], k.identb[:, :], k.mkqb[:, :], start=False, stop=True)
                        mm.then_inc(scored, 1)
                elif what == "values":
                    n = nkey[s] + arg
                    te.wait_ge(exped, HG * (n + 1))
                    if arg == 0 and s:
                        te.wait_ge(o_kept, s)
                    off = live(s, arg)
                    for j in range(HG):
                        mm = nc.tensor.matmul(k.PS[HROW * j:HROW * (j + 1), B_PV, off:QW], v[:, arg, g * HG + j, :],
                                              probs[:, n % 2, j, off:QW], start=arg == 0, stop=arg == key_tiles(s) - 1,
                                              tile_position=(0, HROW * j))
                    mm.then_inc(summed, 1)
                else:
                    te.wait_ge(o_kept, s + 1)
                    if s:
                        te.wait_ge(inverted, s)
                    te.wait_ge(m_kept, turns)
                    spreads += 1
                    nc.tensor.matmul(k.PS[:, B_MISC, :], k.cst[:, C_SEL:C_SEL + P], o[:, g, c * QW:(c + 1) * QW],
                                     start=True, stop=True).then_inc(spread, 1)

        @block.vector
        def _(dve):
            u = 0
            for what, s, arg in order:
                g, c = STEPS[s]
                if what == "max":
                    qt, j, kc = arg
                    dve.wait_ge(max_scored, u + 1)
                    w = (qt % TPQ + 1) * P if kc == c else QW
                    nc.vector.tensor_reduce(pmax[:, s % 2, qt % TPQ, j, kc:kc + 1], k.PS[:, B_MAX + u % SMAX, 0:w],
                                            AX.X, ALU.max).then_inc(max_taken, 1)
                    u += 1
                elif what == "turn":
                    at = M_OPS * s
                    dve.wait_ge(max_taken, nmax[s + 1])
                    nc.vector.tensor_reduce(negm[:, s % 2].rearrange("p j t -> p t j"), pmax[:, s % 2, :, :, 0:c + 1],
                                            AX.X, ALU.max, negate=True).then_inc(m_chain, 1)
                    mp = mparts[:, s % 2]
                    if s >= 2:
                        dve.wait_ge(m_turned, s - 1)
                    dve.wait_ge(m_chain, at + 1)
                    nc.vector.tensor_copy(mp[:, :, 0, :], negm[:, s % 2]).then_inc(m_chain, 1)
                    dve.wait_ge(m_chain, at + 2)
                    nc.vector.tensor_tensor(negr[:, s % 2], negm[:, s % 2], mp[:, :, 0, :], ALU.subtract).then_inc(m_chain, 1)
                    dve.wait_ge(m_chain, at + 3)
                    nc.vector.tensor_copy(mp[:, :, 1, :], negr[:, s % 2]).then_inc(m_chain, 1)
                    dve.wait_ge(m_chain, at + 4)
                    nc.vector.tensor_tensor(mp[:, :, 2, :], negr[:, s % 2], mp[:, :, 1, :], ALU.subtract).then_inc(m_chain, 1)
                elif what == "spread":
                    dve.wait_ge(spread, s + 1)
                    if s:
                        dve.wait_ge(o_done, s)
                    nc.vector.reciprocal(orec[:, :], k.PS[:, B_MISC, :]).then_inc(inverted, 1)

        @block.scalar
        def _(act):
            for what, s, arg in order:
                g, c = STEPS[s]
                if what == "turn":
                    act.wait_ge(m_turned, s + 1)
                    if s >= 2:
                        act.wait_ge(m_placed[s - 2], 16 * HG)
                    nc.scalar.activation(mT[:, s % 2, :], k.PS[:, B_MISC, :].bitcast(BF16)[0:HG * 3 * TPQ, 0:P],
                                         ACT.Copy).then_inc(m_kept, 1)
                elif what == "scores":
                    n = nkey[s] + arg
                    off = live(s, arg)
                    if n >= 2:
                        act.wait_ge(summed, n - 1)
                    for j in range(HG):
                        i = HG * n + j
                        act.wait_ge(scored, i + 1)
                        nc.scalar.activation(probs[:, n % 2, j, off:QW], k.PS[:, B_SC + i % SBANK, off:QW],
                                             ACT.Exp).then_inc(exped, 1)
                elif what == "spread":
                    act.wait_ge(summed, nkey[s + 1])
                    nc.scalar.activation(o[:, g, c * QW:(c + 1) * QW], k.PS[:, B_PV, :], ACT.Copy).then_inc(o_kept, 1)

        @block.gpsimd
        def _(pool):
            for s, (g, c) in enumerate(STEPS):
                pool.wait_ge(inverted, s + 1)
                pool.wait_ge(o_kept, s + 1)
                part = o[:, g, c * QW:(c + 1) * QW]
                nc.gpsimd.tensor_tensor(part, part, orec[:, :], ALU.mult).then_inc(o_done, 1)


def softmax_out(nc, k, a, att):
    wo = k.sb("wo0", [P, NG, D])
    cleared = k.sem("wo0_cleared")
    landed = k.sem("wo0_landed")
    made = k.sem("out0_made")
    added = k.sem("out0_added")
    with nc.Block() as block:
        @block.gpsimd
        def _(pool):
            nc.gpsimd.memset(wo[:, :, :], 0.0).then_inc(cleared, 1)

        @block.sync
        def _(sp):
            sp.wait_ge(cleared, 1)
            for j in range(HG):
                sp.dma_start(wo[HROW * j:HROW * j + DK0, :, :],
                             a["wo0"].rearrange("(g j r) o -> j r g o", j=HG, r=DK0)[j]).then_inc(landed, 16)

        @block.tensor
        def _(te):
            te.wait_ge(landed, 16 * HG)
            for t in range(NT):
                if t >= 8:
                    te.wait_ge(added, t - 7)
                for g in range(NG):
                    last = nc.tensor.matmul(k.PS[:, t % 8, 0:D], att["o"][:, g, t * P:(t + 1) * P], wo[:, g, :],
                                            start=g == 0, stop=g == NG - 1)
                last.then_inc(made, 1)

        @block.vector
        def _(dve):
            for t in range(NT):
                dve.wait_ge(made, t + 1)
                nc.vector.tensor_tensor(k.h[:, t, :], k.PS[:, t % 8, 0:D], k.h[:, t, :], ALU.add).then_inc(added, 1)


def slot_mixture(nc, k, a):
    B_LOG, B_CMX, B_CMB, B_X, B_SUM, B_XT, B_H, B_Y = range(8)
    sp_w = k.sb("slots", [KH, 2, NSLOT, PSLOT])
    sp_sq = k.sb("slots_sq", [KH, 2, NSLOT, PSLOT])
    sp_f = k.sb("slots_f", [KH, 2, PSLOT])
    sp_g = k.sb("slots_g", [KH, 2, PSLOT])
    sp_s = k.sb("slots_scale", [KH, 1])
    wd = k.sb("w_down", [KH, 2, NSLOT, HDOWN])
    wu = k.sb("w_up", [HDOWN, NSLOT, D])
    bd = k.sb("b_down", [HDOWN, NSLOT])
    bu = k.sb("b_up", [KH, 2, NSLOT])
    logit = k.sb("slot_logit", [P, NT, NP])
    cw = k.sb("c_weight", [P, NT, NP])
    dw = k.sb("d_weight", [P, NT, NP])
    row1 = k.sb("c_row1", [P, NT])
    row2 = k.sb("c_row2", [P, NT])
    cmax = k.sb("d_max", [P, NP])
    cmax1 = k.sb("d_max1", [NP, 1])
    cmaxw = k.sb("d_maxw", [NP, P])
    xt = k.sb("x_tilde", [NP, D])
    dsum = k.sb("d_sum", [NP, 1])
    xtT = k.sb("x_tildeT", [KH, 2, NP])
    hid = k.sb("hid", [HDOWN, NP])
    hact = k.sb("hact", [HDOWN, NP])
    yT = k.sb("y_tildeT", [KH, 2, NP])
    y = k.sb("y_tilde", [NP, D])
    cT = k.sb("c_T", [NP, S])
    landed = k.sem("ffn0_landed")
    dv = k.sem("ffn0_vector")
    ac = k.sem("ffn0_scalar")
    pe = k.sem("ffn0_tensor")
    c_turned = k.sem("c_turned")
    c_kept = k.sem("c_kept")
    made = k.sem("ffn0_out_made")
    added = k.sem("ffn0_out_added")
    (V_SQ, V_NORM, V_EPS, V_INV, V_FAC, V_SP, V_CMAX, V_CMAX1, V_CMAXW, V_LD, V_RMAX, V_LC, V_RSUM, V_RINV, V_C,
     V_DINV, V_XT, V_HB, V_YB) = range(1, 20)
    A_ROOT, A_LOGIT, A_DEXP, A_CEXP, A_XTT, A_GELU, A_Y = range(1, 8)
    T_LOGIT, T_CMX, T_CMB, T_X, T_XT, T_H, T_YT, T_Y = range(1, 9)
    LOADS = 8
    with nc.Block() as block:
        @block.sync
        def _(sp):
            sp.dma_start(sp_w[:, :, :, :], a["L0_ffn_slot_params"].rearrange("(k p) n s -> p k (n s)", p=KH)).then_inc(landed, 16)
            sp.dma_start(sp_s[:, :], a["L0_ffn_scale"].to_broadcast([KH, 1])).then_inc(landed, 16)
            for half in range(2):
                sp.dma_start(wd[:, half, :, :], a["L0_ffn_W_down"][:, half * KH:(half + 1) * KH, :].rearrange("n p h -> p n h")).then_inc(landed, 16)
            sp.dma_start(wu[:, :, :], a["L0_ffn_W_up"].rearrange("n h d -> h n d")).then_inc(landed, 16)
            with nc.allow_non_contiguous_dma(reason="two small biases, turned"):
                sp.dma_start(bd[:, :], a["L0_ffn_b_down"].rearrange("n h -> h n")).then_inc(landed, 16)
                for half in range(2):
                    sp.dma_start(bu[:, half, :], a["L0_ffn_b_up"][:, half * KH:(half + 1) * KH].rearrange("n p -> p n")).then_inc(landed, 16)

        @block.vector
        def _(dve):
            v = nc.vector
            slots = sp_w[:, :, :, :]
            dve.wait_ge(landed, 16 * LOADS)
            v.tensor_tensor(sp_sq[:, :, :, :], slots, slots, ALU.mult).then_inc(dv, 1)
            dve.wait_ge(dv, V_SQ)
            v.tensor_reduce(sp_f[:, :, :], sp_sq[:, :, :, :].rearrange("p k n s -> p k s n"), AX.X, ALU.add).then_inc(dv, 1)
            dve.wait_ge(ac, A_ROOT)
            v.tensor_scalar(sp_f[:, :, :], sp_g[:, :, :], 1e-6, None, ALU.add).then_inc(dv, 1)
            dve.wait_ge(dv, V_EPS)
            v.reciprocal(sp_g[:, :, :], sp_f[:, :, :]).then_inc(dv, 1)
            dve.wait_ge(dv, V_INV)
            v.tensor_scalar(sp_f[:, :, :], sp_g[:, :, :], sp_s[:, 0:1], None, ALU.mult).then_inc(dv, 1)
            dve.wait_ge(dv, V_FAC)
            for half in range(2):
                last = v.tensor_tensor(sp_sq[:, half], sp_w[:, half], sp_f[:, half:half + 1, :].to_broadcast([KH, NSLOT, PSLOT]), ALU.mult)
            last.then_inc(dv, 1)
            dve.wait_ge(ac, A_LOGIT)
            v.tensor_reduce(cmax[:, :], logit[:, :, :].rearrange("p t n -> p n t"), AX.X, ALU.max).then_inc(dv, 1)
            dve.wait_ge(pe, T_CMX)
            v.tensor_reduce(cmax1[:, :], k.PS[0:NP, B_CMX, 0:P], AX.X, ALU.max).then_inc(dv, 1)
            dve.wait_ge(dv, V_CMAX1)
            v.tensor_copy(cmaxw[:, :], cmax1[:, 0:1].to_broadcast([NP, P])).then_inc(dv, 1)
            dve.wait_ge(pe, T_CMB)
            v.tensor_tensor(dw[:, :, :], logit[:, :, :], k.PS[:, B_CMB, 0:NP].unsqueeze(1).to_broadcast([P, NT, NP]),
                            ALU.subtract).then_inc(dv, 1)
            v.tensor_reduce(row1[:, :], logit[:, :, :], AX.X, ALU.max).then_inc(dv, 1)
            dve.wait_ge(dv, V_RMAX)
            v.tensor_tensor(cw[:, :, :], logit[:, :, :], row1[:, :].unsqueeze(2).to_broadcast([P, NT, NP]), ALU.subtract).then_inc(dv, 1)
            dve.wait_ge(ac, A_CEXP)
            v.tensor_reduce(row1[:, :], cw[:, :, :], AX.X, ALU.add).then_inc(dv, 1)
            dve.wait_ge(dv, V_RSUM)
            v.reciprocal(row2[:, :], row1[:, :]).then_inc(dv, 1)
            dve.wait_ge(dv, V_RINV)
            v.tensor_tensor(cw[:, :, :], cw[:, :, :], row2[:, :].unsqueeze(2).to_broadcast([P, NT, NP]), ALU.mult).then_inc(dv, 1)
            dve.wait_ge(pe, T_X)
            v.reciprocal(dsum[:, :], k.PS[0:NP, B_SUM, 0:1]).then_inc(dv, 1)
            dve.wait_ge(dv, V_DINV)
            v.tensor_scalar(xt[:, :], k.PS[0:NP, B_X, 0:D], dsum[:, 0:1], None, ALU.mult).then_inc(dv, 1)
            dve.wait_ge(pe, T_H)
            v.tensor_tensor(hid[:, :].rearrange("p (n s) -> p n s", n=NSLOT), k.PS[0:HDOWN, B_H, 0:NP].rearrange("p (n s) -> p n s", n=NSLOT),
                            bd[:, :].unsqueeze(2).to_broadcast([HDOWN, NSLOT, PSLOT]), ALU.add).then_inc(dv, 1)
            dve.wait_ge(pe, T_YT)
            v.tensor_tensor(yT[:, :, :].rearrange("p k (n s) -> p (k n) s", n=NSLOT),
                            k.PS[0:KH, B_Y, 0:2 * NP].rearrange("p (n s) -> p n s", n=2 * NSLOT),
                            bu[:, :, :].rearrange("p k n -> p (k n)").unsqueeze(2).to_broadcast([KH, 2 * NSLOT, PSLOT]),
                            ALU.add).then_inc(dv, 1)
            for t in range(NT):
                dve.wait_ge(made, t + 1)
                v.tensor_tensor(k.h[:, t, :], k.PS[:, t % 8, 0:D], k.h[:, t, :], ALU.add).then_inc(added, 1)

        @block.scalar
        def _(act):
            act.wait_ge(dv, V_NORM)
            nc.scalar.activation(sp_g[:, :, :], sp_f[:, :, :], ACT.Sqrt).then_inc(ac, 1)
            act.wait_ge(pe, T_LOGIT)
            nc.scalar.activation(logit[:, :, :], k.PS[:, B_LOG, :].rearrange("p (t n) -> p t n", t=NT), ACT.Copy).then_inc(ac, 1)
            act.wait_ge(dv, V_LD)
            nc.scalar.activation(dw[:, :, :], dw[:, :, :], ACT.Exp).then_inc(ac, 1)
            act.wait_ge(dv, V_LC)
            nc.scalar.activation(cw[:, :, :], cw[:, :, :], ACT.Exp).then_inc(ac, 1)
            act.wait_ge(pe, T_XT)
            nc.scalar.activation(xtT[:, :, :], k.PS[0:KH, B_XT, 0:2 * NP].rearrange("p (k n) -> p k n", k=2), ACT.Copy).then_inc(ac, 1)
            act.wait_ge(dv, V_HB)
            nc.scalar.activation(hact[:, :], hid[:, :], ACT.Gelu).then_inc(ac, 1)
            for b in range(4):
                act.wait_ge(c_turned, b + 1)
                nc.scalar.activation(cT[:, b * 512:(b + 1) * 512], k.PS[0:NP, b, :], ACT.Copy).then_inc(c_kept, 1)
            act.wait_ge(pe, T_Y)
            nc.scalar.activation(y[:, :], k.PS[0:NP, B_XT, 0:D], ACT.Copy).then_inc(ac, 1)

        @block.tensor
        def _(te):
            mm = nc.tensor.matmul
            te.wait_ge(dv, V_SP)
            for t in range(NT):
                for half in range(2):
                    last = mm(k.PS[:, B_LOG, t * NP:(t + 1) * NP], k.xnT[:, half, t * P:(t + 1) * P],
                              sp_sq[:, half].rearrange("p n s -> p (n s)"), start=half == 0, stop=half == 1)
            last.then_inc(pe, 1)
            te.wait_ge(dv, V_CMAX)
            nc.tensor.transpose(k.PS[0:NP, B_CMX, 0:P], cmax[:, :], k.ident).then_inc(pe, 1)
            te.wait_ge(dv, V_CMAXW)
            mm(k.PS[:, B_CMB, 0:NP], cmaxw[:, :], k.cst[0:NP, C_ID:C_ID + NP], start=True, stop=True).then_inc(pe, 1)
            te.wait_ge(ac, A_DEXP)
            for t in range(NT):
                mm(k.PS[0:NP, B_X, 0:D], dw[:, t, :], k.xn[:, t, :], start=t == 0, stop=t == NT - 1)
                last = mm(k.PS[0:NP, B_SUM, 0:1], dw[:, t, :], k.cst[:, C_ONE:C_ONE + 1], start=t == 0, stop=t == NT - 1)
            last.then_inc(pe, 1)
            te.wait_ge(dv, V_XT)
            for half in range(2):
                last = nc.tensor.transpose(k.PS[0:KH, B_XT, half * NP:(half + 1) * NP], xt[:, half * KH:(half + 1) * KH],
                                           k.cst[0:NP, C_ID:C_ID + NP])
            last.then_inc(pe, 1)
            te.wait_ge(ac, A_XTT)
            for n in range(NSLOT):
                for half in range(2):
                    last = mm(k.PS[0:HDOWN, B_H, n * PSLOT:(n + 1) * PSLOT], wd[:, half, n, :],
                              xtT[:, half, n * PSLOT:(n + 1) * PSLOT], start=half == 0, stop=half == 1)
            last.then_inc(pe, 1)
            te.wait_ge(ac, A_GELU)
            for half in range(2):
                for n in range(NSLOT):
                    last = mm(k.PS[0:KH, B_Y, half * NP + n * PSLOT:half * NP + (n + 1) * PSLOT],
                              wu[:, n, half * KH:(half + 1) * KH], hact[:, n * PSLOT:(n + 1) * PSLOT], start=True, stop=True)
            last.then_inc(pe, 1)
            te.wait_ge(dv, V_XT)
            for b in range(4):
                for i in range(4):
                    last = nc.tensor.transpose(k.PS[0:NP, b, i * P:(i + 1) * P], cw[:, 4 * b + i, :], k.ident)
                last.then_inc(c_turned, 1)
            te.wait_ge(dv, V_YB)
            for half in range(2):
                last = nc.tensor.transpose(k.PS[0:NP, B_XT, half * KH:(half + 1) * KH], yT[:, half, :], k.cst[0:KH, C_ID:C_ID + KH])
            last.then_inc(pe, 1)
            te.wait_ge(ac, A_Y)
            te.wait_ge(c_kept, 4)
            for t in range(NT):
                if t >= 8:
                    te.wait_ge(added, t - 7)
                mm(k.PS[:, t % 8, 0:D], cT[:, t * P:(t + 1) * P], y[:, :], start=True, stop=True).then_inc(made, 1)


def linear_project(nc, k, a, lin):
    w = {m: k.sb(f"w1_{m}", [KH, 2, DIM1 if m != "g" else D]) for m in "qkvg"}
    low = k.sb("low", [P, 2, QW])
    elo = k.sb("elo", [P, 2, QW])
    landed = k.sem("w1_landed")
    made = k.sem("lin_made")
    lowered = k.sem("lowered")
    exped = k.sem("lin_exped")
    mapped = k.sem("mapped")
    kept = k.sem("lin_kept")
    v_ones = k.sem("v_ones")
    units = [(m, pair, c) for m in "kq" for pair in range(NPAIR) for c in range(NQ)]
    NU = len(units)
    rest = [(what, t) for what in ("turn", "v", "gate") for t in range(NT)]
    with nc.Block() as block:
        @block.sync
        def _(sp):
            for m, name in (("k", "L1_attn_Wk"), ("q", "L1_attn_Wq"), ("v", "L1_attn_Wv"), ("g", "L1_attn_Wg")):
                sp.dma_start(w[m][:, :, :], a[name].rearrange("(k p) o -> p k o", p=KH)).then_inc(landed, 16)

        @block.gpsimd
        def _(pool):
            nc.gpsimd.memset(lin["v"][:, :, :, D1:D1 + 1], 1.0)
            nc.gpsimd.memset(lin["state"][:, :, :], 0.0)

        @block.tensor
        def _(te):
            te.wait_ge(landed, 64)
            for n, (m, pair, c) in enumerate(units):
                if n >= 8:
                    te.wait_ge(mapped, n - 7)
                for half in range(2):
                    last = nc.tensor.matmul(k.PS[:, n % 8, :], w[m][:, half, pair * P:(pair + 1) * P],
                                            k.xnT[:, half, c * QW:(c + 1) * QW], start=half == 0, stop=half == 1)
                last.then_inc(made, 1)
            for i, (what, t) in enumerate(rest):
                if i < 8:
                    te.wait_ge(mapped, NU - 7 + i)
                else:
                    te.wait_ge(kept, i - 7)
                bank = i % 8
                if what == "turn":
                    for pair in range(NPAIR):
                        last = nc.tensor.transpose(k.PS[:, bank, pair * P:(pair + 1) * P],
                                                   lin["kT"][:, pair, t * P:(t + 1) * P], k.ident)
                else:
                    n, m = (DIM1, "v") if what == "v" else (D, "g")
                    for half in range(2):
                        last = nc.tensor.matmul(k.PS[:, bank, 0:n], k.xnT[:, half, t * P:(t + 1) * P], w[m][:, half, :],
                                                start=half == 0, stop=half == 1)
                last.then_inc(made, 1)

        @block.vector
        def _(dve):
            def finish(n):
                m, pair, c = units[n]
                dve.wait_ge(exped, n + 1)
                nc.vector.scalar_tensor_tensor(lin[m + "T"][:, pair, c * QW:(c + 1) * QW], k.PS[:, n % 8, :], 0.0,
                                               elo[:, n % 2, :], ALU.max, ALU.add).then_inc(mapped, 1)

            for n in range(NU):
                dve.wait_ge(made, n + 1)
                if n >= 2:
                    dve.wait_ge(exped, n - 1)
                nc.vector.tensor_scalar(low[:, n % 2, :], k.PS[:, n % 8, :], 0.0, None, ALU.min).then_inc(lowered, 1)
                if n >= 1:
                    finish(n - 1)
            finish(NU - 1)

        @block.scalar
        def _(act):
            for n in range(NU):
                act.wait_ge(lowered, n + 1)
                if n >= 2:
                    act.wait_ge(mapped, n - 1)
                nc.scalar.activation(elo[:, n % 2, :], low[:, n % 2, :], ACT.Exp).then_inc(exped, 1)
            for i, (what, t) in enumerate(rest):
                act.wait_ge(made, NU + i + 1)
                ps = k.PS[:, i % 8, :]
                if what == "turn":
                    last = nc.scalar.activation(lin["k"][:, t, :], ps[:, 0:DIM1], ACT.Copy)
                elif what == "v":
                    last = nc.scalar.activation(lin["v"][:, t, :, 0:D1], ps[:, 0:DIM1].rearrange("p (h d) -> p h d", d=D1), ACT.Copy)
                else:
                    last = nc.scalar.activation(lin["gate"][:, t, :], ps[:, 0:D], ACT.Sigmoid)
                last.then_inc(kept, 1)


def linear_attention(nc, k, a, lin):
    B_A, B_N, B_S, B_T, B_Y = 0, 2, 4, 5, 6
    wo = k.sb("wo1", [P, NPAIR, D])
    at = k.sb("lin_scores", [P, 2, 2, NPAIR, P])
    den = k.sb("lin_den", [P, 2, NPAIR])
    inv = k.sb("lin_inv", [P, 2, NPAIR])
    on = k.sb("lin_out", [P, 2, NPAIR, 2, D1])
    oT = k.sb("lin_outT", [P, 2, NPAIR, P])
    gated = k.sb("gated", [P, 2, D])
    landed = k.sem("wo1_landed")
    scored = k.sem("lin_scored")
    masked = k.sem("lin_masked")
    numed = k.sem("lin_numed")
    stated = k.sem("lin_stated")
    summed = k.sem("lin_summed")
    dened = k.sem("lin_dened")
    inved = k.sem("lin_inved")
    normed = k.sem("lin_normed")
    turned = k.sem("lin_turned")
    kept = k.sem("lin_outT_kept")
    made = k.sem("lin_y_made")
    gates = k.sem("lin_gated")
    added = k.sem("lin_added")
    with nc.Block() as block:
        @block.sync
        def _(sp):
            sp.dma_start(wo[:, :, :], a["L1_attn_Wo"].rearrange("(k p) o -> p k o", p=P)).then_inc(landed, 16)

        @block.tensor
        def _(te):
            mm = nc.tensor.matmul

            def scores(c):
                if c >= 1:
                    te.wait_ge(masked, c)
                for odd in range(2):
                    rows = slice(odd * D1, (odd + 1) * D1)
                    for pair in range(NPAIR):
                        last = mm(k.PS[:, B_A + odd, pair * P:(pair + 1) * P], lin["kT"][rows, pair, c * P:(c + 1) * P],
                                  lin["qT"][rows, pair, c * P:(c + 1) * P], start=True, stop=True)
                last.then_inc(scored, 1)

            def project(c):
                te.wait_ge(normed, c + 1)
                if c >= 1:
                    te.wait_ge(kept, c)
                for pair in range(NPAIR):
                    last = nc.tensor.transpose(k.PS[:, B_T, pair * P:(pair + 1) * P],
                                               on[:, c % 2, pair].rearrange("p o d -> p (o d)"), k.ident)
                last.then_inc(turned, 1)
                te.wait_ge(kept, c + 1)
                if c >= 1:
                    te.wait_ge(gates, c)
                for pair in range(NPAIR):
                    last = mm(k.PS[:, B_Y, 0:D], oT[:, c % 2, pair, :], wo[:, pair, :], start=pair == 0, stop=pair == NPAIR - 1)
                last.then_inc(made, 1)

            te.wait_ge(landed, 16)
            scores(0)
            for c in range(NT):
                if c >= 1:
                    te.wait_ge(summed, c)
                for h in range(H1):
                    last = mm(k.PS[(h % 2) * D1:(h % 2 + 1) * D1, B_S, (h // 2) * (D1 + 1):(h // 2 + 1) * (D1 + 1)],
                              lin["k"][:, c, h * D1:(h + 1) * D1], lin["v"][:, c, h, :], start=True, stop=True)
                last.then_inc(stated, 1)
                if c + 1 < NT:
                    scores(c + 1)
                te.wait_ge(masked, c + 1)
                if c >= 1:
                    te.wait_ge(normed, c)
                for odd in range(2):
                    rows = slice(odd * D1, (odd + 1) * D1)
                    for pair in range(NPAIR):
                        out = k.PS[:, B_N + odd, pair * (D1 + 1):(pair + 1) * (D1 + 1)]
                        last = mm(out, at[:, c % 2, odd, pair, :], lin["v"][:, c, 2 * pair + odd, :], start=True, stop=c == 0)
                        if c:
                            last = mm(out, lin["qT"][rows, pair, c * P:(c + 1) * P], lin["states"][rows, c % 2, pair, :],
                                      start=False, stop=True)
                last.then_inc(numed, 1)
                if c >= 1:
                    project(c - 1)
            project(NT - 1)

        @block.vector
        def _(dve):
            v = nc.vector

            def norm(c):
                num = k.PS[:, B_N:B_N + 2, 0:2 * (D1 + 1)].rearrange("p o (q d) -> p o q d", q=NPAIR)
                dve.wait_ge(numed, c + 1)
                v.tensor_scalar(den[:, :, :], num[:, :, :, D1], 1e-6, None, ALU.max).then_inc(dened, 1)
                dve.wait_ge(dened, c + 1)
                v.reciprocal(inv[:, :, :], den[:, :, :]).then_inc(inved, 1)
                dve.wait_ge(inved, c + 1)
                if c >= 2:
                    dve.wait_ge(turned, c - 1)
                for odd in range(2):
                    last = v.tensor_tensor(on[:, c % 2, :, odd, :], num[:, odd, :, 0:D1],
                                           inv[:, odd, :].unsqueeze(2).to_broadcast([P, NPAIR, D1]), ALU.mult)
                last.then_inc(normed, 1)

            def add(c):
                dve.wait_ge(made, c + 1)
                v.tensor_tensor(gated[:, c % 2, :], k.PS[:, B_Y, 0:D], lin["gate"][:, c, :], ALU.mult).then_inc(gates, 1)
                dve.wait_ge(gates, c + 1)
                v.tensor_tensor(k.h[:, c, :], k.h[:, c, :], gated[:, c % 2, :], ALU.add).then_inc(added, 1)

            def mask(c):
                dve.wait_ge(scored, c + 1)
                if c >= 2:
                    dve.wait_ge(numed, c - 1)
                for odd in range(2):
                    last = v.tensor_tensor(at[:, c % 2, odd], k.PS[:, B_A + odd, 0:NPAIR * P].rearrange("p (q n) -> p q n", q=NPAIR),
                                           k.tri.unsqueeze(1).to_broadcast([P, NPAIR, P]), ALU.mult)
                last.then_inc(masked, 1)

            mask(0)
            for c in range(NT):
                dve.wait_ge(stated, c + 1)
                if c >= 1:
                    dve.wait_ge(summed, c)
                    dve.wait_ge(numed, c)
                v.tensor_tensor(lin["states"][:, (c + 1) % 2], k.PS[:, B_S, 0:NPAIR * (D1 + 1)].rearrange("p (q d) -> p q d", q=NPAIR),
                                lin["states"][:, c % 2] if c else lin["state"][:, :, :], ALU.add).then_inc(summed, 1)
                if c + 1 < NT:
                    mask(c + 1)
                norm(c)
                if c >= 1:
                    add(c - 1)
            add(NT - 1)

        @block.scalar
        def _(act):
            for c in range(NT):
                act.wait_ge(turned, c + 1)
                if c >= 2:
                    act.wait_ge(made, c - 1)
                nc.scalar.activation(oT[:, c % 2], k.PS[:, B_T, 0:NPAIR * P].rearrange("p (q n) -> p q n", q=NPAIR),
                                     ACT.Copy).then_inc(kept, 1)


def route(nc, k, a, moe):
    wr = k.sb("w_router", [KH, 2, E])
    t1 = k.sb("route1", [P, NT, E])
    t2 = k.sb("route2", [P, NT, E])
    prob = k.sb("prob", [P, NT, E])
    row = k.sb("route_row", [P, 2, NT])
    mask = k.sb("mask", [P, NT, 2, E])
    maskb = k.sb("maskb", [P, NT, 2, E], BF16)
    place = k.sb("place", [P, NT, 2, E])
    total = k.sb("total", [P, NT, 2, E])
    both = k.sb("both", [P, GRP, E])
    landed = k.sem("wr_landed")
    made = k.sem("router_made")
    dv = k.sem("route_vector")
    ac = k.sem("route_scalar")
    with nc.Block() as block:
        @block.sync
        def _(sp):
            sp.dma_start(wr[:, :, :], a["L1_ffn_w_router"].rearrange("(k p) e -> p k e", p=KH)).then_inc(landed, 16)

        @block.tensor
        def _(te):
            te.wait_ge(landed, 16)
            for t in range(NT):
                for half in range(2):
                    last = nc.tensor.matmul(k.PS[:, 0, t * E:(t + 1) * E], k.xnT[:, half, t * P:(t + 1) * P], wr[:, half, :],
                                            start=half == 0, stop=half == 1)
            last.then_inc(made, 1)
            te.wait_ge(dv, MASKED_AT)
            rhs = maskb[:, :, :, :].rearrange("p t c e -> p (t c e)")
            nc.tensor.matmul(k.PS[:, 1, 0:2 * NT * E], k.trib[:, :], rhs, start=True, stop=True)
            nc.tensor.matmul(k.PS[:, 2, 0:2 * NT * E], k.oneb[:, :], rhs, start=True, stop=True).then_inc(made, 1)

        @block.scalar
        def _(act):
            act.wait_ge(dv, 2)
            nc.scalar.activation(t2[:, :, :], t1[:, :, :], ACT.Exp).then_inc(ac, 1)

        @block.vector
        def _(dve):
            v = nc.vector
            steps = [0]

            def wide(x):
                return x.unsqueeze(2).to_broadcast([P, NT, E])

            def then(ins):
                steps[0] += 1
                ins.then_inc(dv, 1)
                dve.wait_ge(dv, steps[0])

            logits = k.PS[:, 0, 0:NT * E].rearrange("p (t e) -> p t e", t=NT)
            dve.wait_ge(made, 1)
            then(v.tensor_reduce(row[:, 0, :], logits, AX.X, ALU.max))
            then(v.tensor_tensor(t1[:, :, :], logits, wide(row[:, 0, :]), ALU.subtract))
            dve.wait_ge(ac, 1)
            then(v.tensor_reduce(row[:, 0, :], t2[:, :, :], AX.X, ALU.add))
            then(v.reciprocal(row[:, 1, :], row[:, 0, :]))
            then(v.tensor_tensor(prob[:, :, :], t2[:, :, :], wide(row[:, 1, :]), ALU.mult))
            rank = k.cst[:, C_RANK:C_RANK + E].unsqueeze(1).to_broadcast([P, NT, E])
            for c in range(2):
                src = prob if c == 0 else t2
                then(v.tensor_reduce(row[:, 0, :], src[:, :, :], AX.X, ALU.max))
                then(v.tensor_tensor(t1[:, :, :], src[:, :, :], wide(row[:, 0, :]), ALU.is_equal))
                then(v.tensor_tensor(t1[:, :, :], t1[:, :, :], rank, ALU.mult))
                then(v.tensor_reduce(row[:, 1, :], t1[:, :, :], AX.X, ALU.max))
                then(v.tensor_tensor(mask[:, :, c, :], t1[:, :, :], wide(row[:, 1, :]), ALU.is_equal))
                if c == 0:
                    then(v.scalar_tensor_tensor(t2[:, :, :], mask[:, :, 0, :], -2.0, prob[:, :, :], ALU.mult, ALU.add))
            then(v.tensor_copy(maskb[:, :, :, :], mask[:, :, :, :]))
            assert steps[0] == MASKED_AT
            then(v.tensor_tensor(t1[:, :, :], mask[:, :, 0, :], mask[:, :, 1, :], ALU.add))
            then(v.tensor_tensor(moe["gate"][:, :, :], t1[:, :, :], prob[:, :, :], ALU.mult))
            dve.wait_ge(made, 2)
            shape = "p (t c e) -> p t c e"
            then(v.tensor_copy(place[:, :, :, :].rearrange("p t c e -> p (t c e)"), k.PS[:, 1, 0:2 * NT * E]))
            then(v.tensor_copy(total[:, :, :, :].rearrange("p t c e -> p (t c e)"), k.PS[:, 2, 0:2 * NT * E]))
            pg = place[:, :, :, :].rearrange("p (g i) c e -> p g i (c e)", i=TPG)
            tg = total[:, :, :, :].rearrange("p (g i) c e -> p g i (c e)", i=TPG)
            then(v.tensor_tensor(pg[:, :, 1, :], pg[:, :, 1, :], tg[:, :, 0, :], ALU.add))
            then(v.tensor_tensor(both[:, :, :], tg[:, :, 0, 0:E], tg[:, :, 1, 0:E], ALU.add))
            for i in range(TPG):
                then(v.tensor_tensor(pg[:, :, i, E:2 * E], pg[:, :, i, E:2 * E], both[:, :, :], ALU.add))
            then(v.tensor_tensor(place[:, :, :, :], place[:, :, :, :], mask[:, :, :, :], ALU.mult))
            then(v.tensor_tensor(t1[:, :, :], place[:, :, 0, :], place[:, :, 1, :], ALU.add))
            then(v.tensor_scalar(moe["place"][:, :, :], t1[:, :, :], -1.0, None, ALU.add))


MASKED_AT = 17


def dispatch(nc, k, a, moe):
    disp = k.sb("disp", [P, 2, TPG, E, CAP])
    listed = k.sem("disp_listed")
    made = k.sem("disp_made")
    kept = k.sem("disp_kept")
    with nc.Block() as block:
        @block.vector
        def _(dve):
            for g in range(GRP):
                if g >= 2:
                    dve.wait_ge(made, 4 * (g - 1))
                for i in range(TPG):
                    t = g * TPG + i
                    for e in range(E):
                        last = nc.vector.tensor_scalar(disp[:, g % 2, i, e, :], k.cst[:, C_IOTA:C_IOTA + CAP],
                                                       moe["place"][:, t, e:e + 1], None, ALU.is_equal)
                last.then_inc(listed, 1)

        @block.tensor
        def _(te):
            n = 0
            for g in range(GRP):
                te.wait_ge(listed, g + 1)
                for half in range(2):
                    for eh in range(2):
                        if n >= 8:
                            te.wait_ge(kept, n - 7)
                        for i in range(TPG):
                            last = nc.tensor.matmul(k.PS[0:KH, n % 8, 0:EHALF], k.xn[:, g * TPG + i, half * KH:(half + 1) * KH],
                                                    disp[:, g % 2, i, eh * 4:(eh + 1) * 4, :].rearrange("p e c -> p (e c)"),
                                                    start=i == 0, stop=i == TPG - 1)
                        last.then_inc(made, 1)
                        n += 1

        @block.scalar
        def _(act):
            n = 0
            for g in range(GRP):
                for half in range(2):
                    for eh in range(2):
                        act.wait_ge(made, n + 1)
                        nc.scalar.activation(moe["xin"][:, half, eh * 4:(eh + 1) * 4, g, :],
                                             k.PS[0:KH, n % 8, 0:EHALF].rearrange("p (e c) -> p e c", c=CAP), ACT.Copy).then_inc(kept, 1)
                        n += 1


def experts(nc, k, a, moe):
    NS2 = 2
    SH = SLOTS // NS2
    wi = k.sb("wi", [KH, 2, 2, F])
    wo = k.sb("wo2", [P, 2, NF, D])
    hid = k.sb("moe_hid", [P, NF, SLOTS])
    loaded = [k.sem(f"expert_loaded{i}") for i in range(2)]
    made = k.sem("expert_made")
    relued = k.sem("relued")
    outed = k.sem("expert_outed")
    kept = k.sem("expert_kept")
    UN = NF * NS2
    B_H, B_O = 4, 4
    with nc.Block() as block:
        @block.sync
        def _(sp):
            for e in range(E):
                if e >= 2:
                    sp.wait_ge(outed, GRP * (e - 1))
                sp.dma_start(wi[:, e % 2], a["L1_ffn_wi"][e].rearrange("(k p) f -> p k f", p=KH)).then_inc(loaded[e % 2], 16)
                sp.dma_start(wo[:, e % 2], a["L1_ffn_wo"][e].rearrange("(f p) d -> p f d", p=P)).then_inc(loaded[e % 2], 16)

        @block.tensor
        def _(te):
            for e in range(E):
                te.wait_ge(loaded[e % 2], 32 * (e // 2 + 1))
                for f in range(NF):
                    for s in range(NS2):
                        n = UN * e + f * NS2 + s
                        if n >= B_H:
                            te.wait_ge(relued, n - B_H + 1)
                        for half in range(2):
                            last = nc.tensor.matmul(k.PS[:, n % B_H, 0:SH], wi[:, e % 2, half, f * P:(f + 1) * P],
                                                    moe["xin"][:, half, e, s * (GRP // NS2):(s + 1) * (GRP // NS2), :].rearrange("p g c -> p (g c)"),
                                                    start=half == 0, stop=half == 1)
                        last.then_inc(made, 1)
                te.wait_ge(relued, UN * (e + 1))
                for g in range(GRP):
                    n = GRP * e + g
                    if n >= B_O:
                        te.wait_ge(kept, n - B_O + 1)
                    for f in range(NF):
                        last = nc.tensor.matmul(k.PS[0:CAP, B_H + n % B_O, 0:D], hid[:, f, g * CAP:(g + 1) * CAP], wo[:, e % 2, f, :],
                                                start=f == 0, stop=f == NF - 1)
                    last.then_inc(outed, 1)

        @block.vector
        def _(dve):
            for e in range(E):
                for f in range(NF):
                    for s in range(NS2):
                        n = UN * e + f * NS2 + s
                        dve.wait_ge(made, n + 1)
                        if e and f == 0 and s == 0:
                            dve.wait_ge(outed, GRP * e)
                        nc.vector.tensor_scalar(hid[:, f, s * SH:(s + 1) * SH], k.PS[:, n % B_H, 0:SH], 0.0, None, ALU.max).then_inc(relued, 1)

        @block.scalar
        def _(act):
            for n in range(E * GRP):
                act.wait_ge(outed, n + 1)
                nc.scalar.activation(moe["eo"][:, n // GRP, n % GRP, :], k.PS[0:CAP, B_H + n % B_O, 0:D], ACT.Copy).then_inc(kept, 1)


def combine(nc, k, a, moe, out):
    comb = k.sb("comb", [P, 2, E, CAP])
    combT = k.sb("combT", [CAP, 2, E, P])
    listed = k.sem("comb_listed")
    turned = k.sem("comb_turned")
    kept = k.sem("comb_kept")
    made = k.sem("comb_made")
    added = k.sem("comb_added")
    stored = k.sem("stored")
    with nc.Block() as block:
        @block.vector
        def _(dve):
            def add(t):
                dve.wait_ge(made, t + 1)
                nc.vector.tensor_tensor(k.h[:, t, :], k.PS[:, 4 + t % 2, 0:D], k.h[:, t, :], ALU.add).then_inc(added, 1)

            for t in range(NT):
                if t >= 2:
                    dve.wait_ge(turned, 2 * (t - 1))
                for e in range(E):
                    last = nc.vector.tensor_scalar(comb[:, t % 2, e, :], k.cst[:, C_IOTA:C_IOTA + CAP], moe["place"][:, t, e:e + 1],
                                                   moe["gate"][:, t, e:e + 1], ALU.is_equal, ALU.mult)
                last.then_inc(listed, 1)
                if t >= 1:
                    add(t - 1)
            add(NT - 1)

        @block.tensor
        def _(te):
            def turn(t):
                te.wait_ge(listed, t + 1)
                for b in range(2):
                    n = 2 * t + b
                    if n >= 4:
                        te.wait_ge(kept, n - 3)
                    for i in range(4):
                        last = nc.tensor.transpose(k.PS[0:CAP, n % 4, i * P:(i + 1) * P], comb[:, t % 2, 4 * b + i, :], k.ident)
                    last.then_inc(turned, 1)

            turn(0)
            for t in range(NT):
                if t + 1 < NT:
                    turn(t + 1)
                te.wait_ge(kept, 2 * t + 2)
                if t >= 2:
                    te.wait_ge(added, t - 1)
                for e in range(E):
                    last = nc.tensor.matmul(k.PS[:, 4 + t % 2, 0:D], combT[:, t % 2, e, :], moe["eo"][:, e, t // TPG, :],
                                            start=e == 0, stop=e == E - 1)
                last.then_inc(made, 1)

        @block.scalar
        def _(act):
            for n in range(2 * NT):
                t, b = n // 2, n % 2
                act.wait_ge(turned, n + 1)
                if t >= 2:
                    act.wait_ge(made, t - 1)
                nc.scalar.activation(combT[:, t % 2, 4 * b:4 * b + 4, :], k.PS[0:CAP, n % 4, :].rearrange("p (e n) -> p e n", e=4),
                                     ACT.Copy).then_inc(kept, 1)

        @block.sync
        def _(sp):
            view = out.rearrange("(q t p) d -> q p t d", p=P, t=4)
            for q in range(NT // 4):
                sp.wait_ge(added, 4 * q + 4)
                sp.dma_start(view[q], k.h[:, 4 * q:4 * q + 4, :]).then_inc(stored, 16)
            sp.wait_ge(stored, 16 * (NT // 4))


def store(nc, k, out):
    stored = k.sem("stored")
    with nc.Block() as block:
        @block.sync
        def _(sp):
            sp.dma_start(out.rearrange("(t p) d -> p t d", p=P), k.h[:, :, :]).then_inc(stored, 16)
            sp.wait_ge(stored, 16)


def program(nc, a, out, upto=99):
    with ExitStack() as ctx:
        k = Core(nc, ctx)
        with k.room():
            embed(nc, k, a)
        if upto >= 1:
            layernorm(nc, k, "ln1")
            with k.room():
                att = {
                    "scratch": nc.dram_tensor("qk_parts", [2, 3, D, S], BF16, kind="Internal").ap(),
                    "o": k.sb("o0", [P, NG, S]),
                    "v": k.sb("v0", [P, NT, H0, HROW]),
                    "v_cleared": k.sem("v_cleared"),
                    "loads": [0] * NG,
                }
                with k.room():
                    att["qs"] = k.sb("qs", [P, 2, HG, S], BF16)
                    att["ks"] = k.sb("ks", [P, 2, HG, S], BF16)
                    with k.room():
                        softmax_qkv(nc, k, a, att)
                    if upto >= 2:
                        with k.room():
                            softmax_attention(nc, k, a, att)
                if upto >= 2:
                    softmax_out(nc, k, a, att)
        if upto >= 3:
            layernorm(nc, k, "ln2", l2=True)
            with k.room():
                slot_mixture(nc, k, a)
        if upto >= 4:
            layernorm(nc, k, "ln3")
            with k.room():
                lin = {
                    "qT": k.sb("lin_qT", [P, NPAIR, S]),
                    "kT": k.sb("lin_kT", [P, NPAIR, S]),
                    "k": k.sb("lin_k", [P, NT, DIM1]),
                    "v": k.sb("lin_v", [P, NT, H1, D1 + 1]),
                    "gate": k.sb("lin_gate", [P, NT, D]),
                    "state": k.sb("lin_state0", [P, NPAIR, D1 + 1]),
                    "states": k.sb("lin_states", [P, 2, NPAIR, D1 + 1]),
                }
                with k.room():
                    linear_project(nc, k, a, lin)
                with k.room():
                    linear_attention(nc, k, a, lin)
        if upto >= 5:
            layernorm(nc, k, "ln4")
            with k.room():
                moe = {
                    "gate": k.sb("moe_gate", [P, NT, E]),
                    "place": k.sb("moe_place", [P, NT, E]),
                    "xin": k.sb("moe_xin", [KH, 2, E, GRP, CAP]),
                    "eo": k.sb("moe_eo", [CAP, E, GRP, D]),
                }
                with k.room():
                    route(nc, k, a, moe)
                with k.room():
                    dispatch(nc, k, a, moe)
                with k.room():
                    experts(nc, k, a, moe)
                with k.room():
                    combine(nc, k, a, moe, out)
            return
        store(nc, k, out)


_HOST = {
    "L0_attn_Wq": "wq0", "L0_attn_Wk": "wk0", "L0_attn_Wv": "wv0", "L0_attn_Wo": "wo0",
}


def laid_out(inputs):
    arrays = {}
    for name, x in inputs.items():
        x = np.asarray(x)
        arrays[_HOST.get(name, name)] = np.ascontiguousarray(x.T) if name in _HOST else np.ascontiguousarray(x)
    arrays["L0_ffn_scale"] = arrays["L0_ffn_scale"].reshape(1, 1)
    arrays["consts"], arrays["pe"] = constants()
    return arrays


def kernel(**inputs):
    import concourse.bacc as _bacc
    from concourse.bass_utils import run_bass_kernel_spmd as _run

    nc = _bacc.Bacc("TRN2", target_bir_lowering=False, num_devices=1)
    arrays, a = {}, {}
    for name, x in laid_out(inputs).items():
        arrays[f"in_{name}"] = x
        a[name] = nc.dram_tensor(f"in_{name}", x.shape, mybir.dt.from_np(x.dtype), kind="ExternalInput").ap()
    out = nc.dram_tensor("out_0", (S, D), F32, kind="ExternalOutput").ap()
    program(nc, a, out)
    r = _run(nc, [arrays], core_ids=[0])
    return r.results[0]["out_0"].reshape(1, S, D)
```

```python
import math
from contextlib import ExitStack, contextmanager

import numpy as np
import concourse.bass as bass
from concourse import mybir

F32 = mybir.dt.float32
BF16 = mybir.dt.bfloat16
F32R = mybir.dt.float32r
I32 = mybir.dt.int32
ALU = mybir.AluOpType
ACT = mybir.ActivationFunctionType
AX = mybir.AxisListType

P = 128
S = 2048
D = 192
NT = S // P
KH = D // 2
QW = 512
NQ = S // QW
TPQ = QW // P
VOCAB = 70

H0 = 12
DK0 = D // H0
HG = 4
NG = H0 // HG
HROW = P // HG
STACK = 6 * DK0
PARTS_Q = (0, 0, 0, 1, 1, 2)
PARTS_K = (0, 1, 2, 0, 1, 0)

NSLOT, PSLOT, HDOWN = 8, 4, 24
NP = NSLOT * PSLOT

H1, D1 = 4, 64
DIM1 = H1 * D1
NPAIR = H1 // 2

E = 8
F = 768
NF = F // P
GRP = 8
SG = S // GRP
CAP = 80
TPG = SG // P
SLOTS = GRP * CAP
EHALF = E * CAP // 2

MASKED = -1.0e30
C_ID, C_TRI, C_MQK, C_MKQ, C_SEL, C_ONE, C_IOTA, C_PIDX, C_RANK, C_SEL4 = 0, 128, 256, 384, 512, 640, 768, 848, 849, 857
C_ALL = 861


def constants():
    p, f = np.arange(P)[:, None], np.arange(P)[None, :]
    c = np.zeros((P, C_ALL), np.float32)
    c[:, C_ID:C_ID + P] = p == f
    c[:, C_TRI:C_TRI + P] = p <= f
    c[:, C_MQK:C_MQK + P] = np.where(f > p, MASKED, 0)
    c[:, C_MKQ:C_MKQ + P] = np.where(p > f, MASKED, 0)
    c[:, C_SEL:C_SEL + P] = p == HROW * (f // HROW) + DK0
    c[:, C_ONE:C_ONE + P] = 1
    c[:, C_IOTA:C_IOTA + CAP] = np.arange(CAP)
    c[:, C_PIDX] = np.arange(P)
    c[:, C_SEL4:C_SEL4 + HG] = p == HROW * np.arange(HG)[None, :] + DK0
    c[:, C_RANK:C_RANK + E] = np.arange(E, 0, -1)
    pos = np.arange(S, dtype=np.float32)[:, None]
    even = np.arange(0, D, 2, dtype=np.float32)
    exponent = -(even / np.float32(D)) * np.float32(math.log(10000.0))
    angle = pos * np.exp(exponent.astype(np.float64)).astype(np.float32)
    pe = np.stack([np.sin(angle), np.cos(angle)], axis=-1).reshape(S, D).astype(np.float32)
    return c, pe


class Core:

    def __init__(self, nc, ctx):
        self.nc = nc
        self.ctx = ctx
        self.sems = ctx
        self.h = self.sb("h", [P, NT, D])
        self.cst = self.sb("cst", [P, C_ALL])
        self.identb = self.sb("identb", [P, P], BF16)
        self.mqkb = self.sb("mqkb", [P, P], BF16)
        self.mkqb = self.sb("mkqb", [P, P], BF16)
        self.trib = self.sb("trib", [P, P], BF16)
        self.oneb = self.sb("oneb", [P, P], BF16)
        self.stats = self.sb("stats", [P, NT, 6])
        self.mv = self.sb("mv", [P, NT, 2])
        self.ve = self.sb("ve", [P, NT])
        self.sd = self.sb("sd", [P, NT])
        self.rstd = self.sb("rstd", [P, NT])
        self.PS = ctx.enter_context(nc.psum_tensor("PS", [P, 8, 512], F32))
        self.ident = self.cst[:, C_ID:C_ID + P]
        self.tri = self.cst[:, C_TRI:C_TRI + P]

    def sb(self, name, shape, dt=F32):
        return self.ctx.enter_context(self.nc.sbuf_tensor(name, shape, dt))

    def sem(self, name):
        return self.sems.enter_context(self.nc.semaphore(name))

    def rows(self, layer):
        self.xn = self.sb(f"xn{layer}", [P, NT, D])
        self.xnT = self.sb(f"xnT{layer}", [KH, 2, S])

    @contextmanager
    def room(self):
        outer = self.ctx
        with ExitStack() as self.ctx:
            yield
        self.ctx = outer


def embed(nc, k, a):
    tok = k.sb("tok", [VOCAB, S], I32)
    onehot = k.xnT[0:VOCAB, 0, :]
    table = k.sb("table", [VOCAB, D])
    pe = k.xn
    landed = k.sem("emb_landed")
    pe_landed = k.sem("pe_landed")
    onehot_made = k.sem("onehot_made")
    rows_made = k.sem("rows_made")
    h_made = k.sem("h_made")
    base = D // 3
    with nc.Block() as block:
        @block.sync
        def _(sp):
            sp.dma_start(k.cst[:, :], a["consts"]).then_inc(landed, 16)
            sp.dma_start(tok[:, :], a["x"].to_broadcast([VOCAB, S])).then_inc(landed, 16)
            sp.dma_start(table[0:64, 0:base], a["L0_tok_color_W"].unsqueeze(1).to_broadcast([4, 16, base])).then_inc(landed, 16)
            for c in range(4):
                sp.dma_start(table[16 * c:16 * c + 16, base:2 * base],
                             a["L0_tok_shape_W"].unsqueeze(1).to_broadcast([4, 4, base])).then_inc(landed, 16)
            sp.dma_start(table[0:64, 2 * base:D], a["L0_tok_quantity_W"].unsqueeze(0).to_broadcast([16, 4, base])).then_inc(landed, 16)
            sp.dma_start(table[64:VOCAB, :], a["L0_tok_special_W"]).then_inc(landed, 16)
            sp.dma_start(pe[:, :, :], a["pe"].rearrange("(t p) d -> p t d", p=P)).then_inc(pe_landed, 16)

        @block.vector
        def _(dve):
            dve.wait_ge(landed, 16 * 9)
            nc.vector.tensor_scalar(onehot, tok[:, :], float(VOCAB - 1), k.cst[0:VOCAB, C_PIDX:C_PIDX + 1],
                                    ALU.min, ALU.is_equal).then_inc(onehot_made, 1)
            for dst, c in ((k.identb, C_ID), (k.mqkb, C_MQK), (k.mkqb, C_MKQ), (k.trib, C_TRI), (k.oneb, C_ONE)):
                nc.vector.tensor_copy(dst[:, :], k.cst[:, c:c + P])
            dve.wait_ge(pe_landed, 16)
            for t in range(NT):
                dve.wait_ge(rows_made, t + 1)
                nc.vector.scalar_tensor_tensor(k.h[:, t, :], k.PS[:, t % 8, 0:D], math.sqrt(D),
                                               pe[:, t, :], ALU.mult, ALU.add).then_inc(h_made, 1)

        @block.tensor
        def _(te):
            te.wait_ge(onehot_made, 1)
            for t in range(NT):
                if t >= 8:
                    te.wait_ge(h_made, t - 7)
                nc.tensor.matmul(k.PS[:, t % 8, 0:D], onehot[:, t * P:(t + 1) * P], table[:, :],
                                 start=True, stop=True).then_inc(rows_made, 1)


def layernorm(nc, k, name, l2=False):
    stats_made = k.sem(name + "_stats_made")
    mv_made = k.sem(name + "_mv_made")
    small = k.sem(name + "_small")
    rooted = k.sem(name + "_rooted")
    xn_made = k.sem(name + "_xn_made")
    turned = k.sem(name + "_turned")
    with nc.Block() as block:
        @block.vector
        def _(dve):
            for t in range(NT):
                nc.vector.bn_stats(k.stats[:, t, :], k.h[:, t, :]).then_inc(stats_made, 1)
            for t in range(NT):
                dve.wait_ge(stats_made, t + 1)
                nc.vector.bn_aggr(k.mv[:, t, :], k.stats[:, t, :]).then_inc(mv_made, 1)
            dve.wait_ge(mv_made, NT)
            nc.vector.tensor_scalar(k.ve[:, :], k.mv[:, :, 1], 1e-5, None, ALU.add).then_inc(small, 1)
            dve.wait_ge(rooted, 1)
            nc.vector.reciprocal(k.rstd[:, :], k.sd[:, :]).then_inc(small, 1)
            dve.wait_ge(small, 2)
            if l2:
                nc.vector.scalar_tensor_tensor(k.ve[:, :], k.mv[:, :, 1], float(D), k.rstd[:, :], ALU.mult, ALU.mult).then_inc(small, 1)
                dve.wait_ge(small, 3)
                nc.vector.tensor_tensor(k.ve[:, :], k.ve[:, :], k.rstd[:, :], ALU.mult).then_inc(small, 1)
                dve.wait_ge(rooted, 2)
                nc.vector.tensor_scalar(k.ve[:, :], k.sd[:, :], 1e-6, None, ALU.add).then_inc(small, 1)
                dve.wait_ge(small, 5)
                nc.vector.reciprocal(k.sd[:, :], k.ve[:, :]).then_inc(small, 1)
                dve.wait_ge(small, 6)
                nc.vector.tensor_tensor(k.rstd[:, :], k.rstd[:, :], k.sd[:, :], ALU.mult).then_inc(small, 1)
                dve.wait_ge(small, 7)
            for t in range(NT):
                nc.vector.tensor_scalar(k.xn[:, t, :], k.h[:, t, :], k.mv[:, t, 0:1], k.rstd[:, t:t + 1],
                                        ALU.subtract, ALU.mult).then_inc(xn_made, 1)

        @block.scalar
        def _(act):
            act.wait_ge(small, 1)
            nc.scalar.activation(k.sd[:, :], k.ve[:, :], ACT.Sqrt).then_inc(rooted, 1)
            if l2:
                act.wait_ge(small, 4)
                nc.scalar.activation(k.sd[:, :], k.ve[:, :], ACT.Sqrt).then_inc(rooted, 1)
            for u in range(NT // 2):
                act.wait_ge(turned, u + 1)
                nc.scalar.activation(k.xnT[:, :, 2 * u * P:2 * (u + 1) * P],
                                     k.PS[0:KH, u, :].rearrange("p (k n) -> p k n", k=2), ACT.Copy)

        @block.tensor
        def _(te):
            for u in range(NT // 2):
                te.wait_ge(xn_made, 2 * u + 2)
                for i in range(2):
                    for half in range(2):
                        last = nc.tensor.transpose(k.PS[0:KH, u, half * 256 + i * P:half * 256 + (i + 1) * P],
                                                   k.xn[:, 2 * u + i, half * KH:(half + 1) * KH], k.ident)
                last.then_inc(turned, 1)


def softmax_qkv(nc, k, a, att):
    w = [k.sb(f"w0_{m}", [KH, 2, D]) for m in "qkv"]
    RING = 4
    parts = k.sb("parts", [KH, RING, 3, QW], BF16)
    rest = k.sb("rest", [KH, 2, QW])
    w_landed = k.sem("w0_landed")
    made = k.sem("qkv_made")
    part1 = k.sem("part1_made")
    rest1 = k.sem("rest1_made")
    part2 = k.sem("part2_made")
    part3 = k.sem("part3_made")
    v_kept = k.sem("v_kept")
    stored = [k.sem(f"parts_stored{i}") for i in range(RING)]
    units = [(m, mt, c) for m in range(2) for mt in range(2) for c in range(NQ)]
    NU = len(units)
    scale = (DK0 ** -0.5, 1.0)
    with nc.Block() as block:
        @block.sync
        def _(sp):
            for m, name in enumerate(("wq0", "wk0", "wv0")):
                sp.dma_start(w[m][:, :, :], a[name].rearrange("(k p) o -> p k o", p=KH)).then_inc(w_landed, 16)
            for n, (m, mt, c) in enumerate(units):
                sp.wait_ge(part3, n + 1)
                sp.dma_start(att["scratch"][m, :, mt * KH:(mt + 1) * KH, c * QW:(c + 1) * QW].rearrange("g r n -> r g n"),
                             parts[:, n % RING, :, :]).then_inc(stored[n % RING], 16)
            for i in range(RING):
                sp.wait_ge(stored[i], 16 * (NU // RING))

        @block.gpsimd
        def _(pool):
            nc.gpsimd.memset(att["v"][:, :, :, DK0:HROW], 0.0).then_inc(att["v_cleared"], 1)
            pool.wait_ge(att["v_cleared"], 1)
            nc.gpsimd.memset(att["v"][:, :, :, DK0:DK0 + 1], 1.0).then_inc(att["v_cleared"], 1)
            pool.wait_ge(att["v_cleared"], 2)
            nc.gpsimd.memset(att["ks"][STACK:STACK + 3, :, :, :], 1.0)

        @block.tensor
        def _(te):
            te.wait_ge(w_landed, 48)
            for n, (m, mt, c) in enumerate(units):
                if n >= 8:
                    te.wait_ge(rest1, n - 7)
                for half in range(2):
                    last = nc.tensor.matmul(k.PS[0:KH, n % 8, :], w[m][:, half, mt * KH:(mt + 1) * KH],
                                            k.xnT[:, half, c * QW:(c + 1) * QW], start=half == 0, stop=half == 1)
                last.then_inc(made, 1)
            for t in range(NT):
                if t < 8:
                    te.wait_ge(rest1, NU - 7 + t)
                else:
                    te.wait_ge(v_kept, t - 7)
                for half in range(2):
                    last = nc.tensor.matmul(k.PS[:, t % 8, 0:D], k.xnT[:, half, t * P:(t + 1) * P], w[2][:, half, :],
                                            start=half == 0, stop=half == 1)
                last.then_inc(made, 1)

        @block.scalar
        def _(act):
            def second(n):
                act.wait_ge(rest1, n + 1)
                nc.scalar.activation(parts[:, n % RING, 1, :], rest[:, n % 2, :], ACT.Copy).then_inc(part2, 1)

            for n, (m, mt, c) in enumerate(units):
                act.wait_ge(made, n + 1)
                if n >= RING:
                    act.wait_ge(stored[n % RING], 16 * (n // RING))
                nc.scalar.activation(parts[:, n % RING, 0, :], k.PS[0:KH, n % 8, :], ACT.Copy, scale=scale[m]).then_inc(part1, 1)
                if n >= 1:
                    second(n - 1)
            second(NU - 1)
            for t in range(NT):
                act.wait_ge(made, NU + t + 1)
                nc.scalar.activation(att["v"][:, t, :, 0:DK0], k.PS[:, t % 8, 0:D].rearrange("p (h d) -> p h d", d=DK0),
                                     ACT.Copy).then_inc(v_kept, 1)

        @block.vector
        def _(dve):
            def third(n):
                dve.wait_ge(part2, n + 1)
                nc.vector.tensor_tensor(parts[:, n % RING, 2, :], rest[:, n % 2, :], parts[:, n % RING, 1, :],
                                        ALU.subtract).then_inc(part3, 1)

            for n, (m, mt, c) in enumerate(units):
                dve.wait_ge(part1, n + 1)
                if n >= 2:
                    dve.wait_ge(part3, n - 1)
                nc.vector.scalar_tensor_tensor(rest[:, n % 2, :], k.PS[0:KH, n % 8, :], scale[m], parts[:, n % RING, 0, :],
                                               ALU.mult, ALU.subtract).then_inc(rest1, 1)
                if n >= 1:
                    third(n - 1)
            third(NU - 1)


STEPS = [(0, c) for c in range(NQ)] + [(1, c) for c in range(NQ)] + [(2, c) for c in reversed(range(NQ))]
MAX_SLOTS, S_BANKS = 2, 3
B_MAX, B_SC, B_PV = 0, 4, 7
MSTACK = 4 * DK0
MPARTS_Q, MPARTS_K = (0, 0, 1, 1), (0, 1, 0, 1)


def max_units(step):
    g, c = STEPS[step]
    return [(qt, pair, kc) for qt in range(TPQ * c, TPQ * (c + 1)) for pair in range(HG // 2) for kc in range(c + 1)]


def max_width(step, unit):
    qt, _, kc = unit
    return (qt % TPQ + 1) * P if kc == STEPS[step][1] else QW


def key_tiles(step):
    return TPQ * (STEPS[step][1] + 1)


def live(step, kt):
    return max(0, kt - TPQ * STEPS[step][1]) * P


def attention_order():
    NS = len(STEPS)
    hop = 120
    maxq = [("max", s, u) for s in range(NS) for u in max_units(s)]
    scoreq = [("score", s, (kt, j)) for s in range(NS) for kt in range(key_tiles(s)) for j in range(HG)]
    left = [len(max_units(s)) for s in range(NS)]
    pe = dve = act = 0.0
    slot_free, bank_free = [0.0] * MAX_SLOTS, [0.0] * S_BANKS
    placed = [None] * NS
    finished = [None] * NS
    small, values = [], []
    order = []
    slots = scores = 0
    pv_free = 0.0
    while maxq or scoreq or small or values:
        options = []
        if values:
            options.append((max(values[0][0], pv_free if values[0][1][2] == 0 else 0), 0, "values"))
        if small:
            options.append((max(small[0][0], slot_free[slots % MAX_SLOTS]), 1, "small"))
        if scoreq and placed[scoreq[0][1]] is not None and len(values) < 2:
            options.append((max(placed[scoreq[0][1]], bank_free[scores % S_BANKS]), 2, "score"))
        if maxq:
            s = maxq[0][1]
            ready = slot_free[slots % MAX_SLOTS]
            g = STEPS[s][0]
            if g >= 2:
                done = finished[NQ * (g - 1) - 1]
                ready = None if done is None else max(ready, done + 12000)
            if ready is not None and (s < 2 or finished[s - 2] is not None or s - 2 == (scoreq[0][1] if scoreq else NS)
                                      or placed[s - 2] is not None):
                options.append((ready, 3, "max"))
        when, _, kind = min((max(pe, o[0]), o[1], o[2]) for o in options)
        pe = when
        if kind == "values":
            item = values.pop(0)[1]
            _, s, kt = item
            pe += 1.75 * (QW - live(s, kt))
            if kt == key_tiles(s) - 1:
                act = max(act, pe + hop) + 480
                pv_free = act + hop
                finished[s] = act
                small.append((act + hop, ("den", s, None)))
        elif kind == "small":
            item = small.pop(0)[1]
            pe += {"turn": 60, "den": 430, "inv": 860}[item[0]]
            dve = max(dve, pe + hop) + {"turn": 250, "den": 150, "inv": 620}[item[0]]
            slot_free[slots % MAX_SLOTS] = dve + hop
            slots += 1
            if item[0] == "turn":
                placed[item[1]] = dve + 3500
            if item[0] == "den":
                small.append((dve + hop, ("inv", item[1], None)))
        elif kind == "score":
            item = scoreq.pop(0)
            _, s, (kt, j) = item
            w = QW - live(s, kt)
            pe += w / 2.4 + 60 * (kt >= TPQ * STEPS[s][1])
            act = max(act, pe + hop) + 50 + w / 1.2
            bank_free[scores % S_BANKS] = act + hop
            scores += 1
            if j == HG - 1:
                values.append((act + hop, ("values", s, kt)))
        else:
            item = maxq.pop(0)
            _, s, u = item
            w = max_width(s, u)
            pe += w / 2.4 + 20 + 120 * (u[2] == STEPS[s][1])
            dve = max(dve, pe + hop) + 65 + 2 * w / 0.96
            slot_free[slots % MAX_SLOTS] = dve + hop
            slots += 1
            left[s] -= 1
            if not left[s]:
                dve += 900
                small.append((dve + hop, ("turn", s, None)))
        order.append(item)
    return order


def softmax_attention(nc, k, a, att):
    qs, ks, qm, km, v, o = (att[x] for x in ("qs", "ks", "qm", "km", "v", "o"))
    NS = len(STEPS)
    pmax = k.sb("pmax", [P, 2, TPQ, HG, NQ])
    negm = k.sb("negm", [P, 2, HG, TPQ])
    negr = k.sb("negr", [P, 2, HG, TPQ])
    mparts = k.sb("mparts", [P, 2, HG, 3, TPQ], BF16)
    mT = k.sb("mT", [HG * 3 * TPQ, 2, P], BF16)
    probs = k.sb("probs", [P, 2, HG, QW])
    inv = k.sb("inv", [P, TPQ, HG])
    invw = k.sb("invw", [P, TPQ, HG, HROW])
    m_loaded = [[k.sem(f"mstack_loaded_{m}{g}") for g in range(NG)] for m in "qk"]
    s_loaded = [[k.sem(f"stack_loaded_{m}{g}") for g in range(NG)] for m in "qk"]
    slot_made = k.sem("slot_made")
    slot_read = k.sem("slot_read")
    m_chain = k.sem("m_chain")
    m_placed = [k.sem(f"m_placed{s}") for s in range(NS)]
    scored = k.sem("scored")
    exped = k.sem("exped")
    summed = k.sem("summed")
    o_kept = k.sem("o_kept")
    inv_wide = k.sem("inv_wide")
    order = attention_order()
    slot_order = [x for x in order if x[0] in ("max", "turn", "den", "inv")]
    slots_to_max = [0] * NS
    slots_to_turn = [0] * NS
    for i, (what, s, _) in enumerate(slot_order):
        if what == "max":
            slots_to_max[s] = i + 1
        if what == "turn":
            slots_to_turn[s] = i + 1
    nkey = [0]
    for s in range(NS):
        nkey.append(nkey[-1] + key_tiles(s))
    CHAIN = 5
    SLOADS, MLOADS = 16 * HG * 3, 16 * HG * 2

    def load_max(eng, m, g):
        stack, lot = (qm, MPARTS_Q) if m == 0 else (km, MPARTS_K)
        for j in range(HG):
            r = (g * HG + j) * DK0
            for at in (0, 2):
                src = att["scratch"][m, lot[at]:lot[at + 1] + 1, r:r + DK0, :]
                if m == 0:
                    src = src.to_broadcast([2, DK0, S])
                row = (j % 2) * MSTACK + at * DK0
                eng.dma_start(stack[row:row + 2 * DK0, g % 2, j // 2, :], src).then_inc(m_loaded[m][g], 16)

    def load_scores(eng, m, g):
        stack, lot = (qs, PARTS_Q) if m == 0 else (ks, PARTS_K)
        for j in range(HG):
            r = (g * HG + j) * DK0
            for at, n in ((0, 3), (3, 2), (5, 1)):
                src = att["scratch"][m, lot[at]:lot[at + n - 1] + 1, r:r + DK0, :]
                if m == 0 and n > 1:
                    src = src.to_broadcast([n, DK0, S])
                eng.dma_start(stack[at * DK0:(at + n) * DK0, g % 2, j, :], src).then_inc(s_loaded[m][g], 16)

    with nc.Block() as block:
        @block.sync
        def _(sp):
            load_max(sp, 0, 0)
            load_scores(sp, 0, 0)
            load_max(sp, 0, 1)
            load_scores(sp, 0, 1)
            for s, (g, c) in enumerate(STEPS):
                sp.wait_ge(slot_read, slots_to_turn[s])
                for j in range(HG):
                    sp.dma_start(qs[STACK:STACK + 3, g % 2, j, c * QW:(c + 1) * QW].rearrange("r (t n) -> r t n", n=P),
                                 mT[j * 3 * TPQ:(j + 1) * 3 * TPQ, s % 2, :]).then_inc(m_placed[s], 16)
                if s == NQ - 1:
                    load_max(sp, 0, 2)

        @block.gpsimd
        def _(pool):
            load_max(pool, 1, 0)
            load_scores(pool, 1, 0)
            load_max(pool, 1, 1)
            load_scores(pool, 1, 1)
            pool.wait_ge(slot_read, slots_to_max[NQ - 1])
            load_max(pool, 1, 2)
            pool.wait_ge(scored, HG * nkey[NQ])
            load_scores(pool, 1, 2)
            load_scores(pool, 0, 2)

        @block.tensor
        def _(te):
            slot = score = 0
            for what, s, arg in order:
                g, c = STEPS[s]
                b = g % 2
                if what in ("max", "turn", "den", "inv"):
                    bank = B_MAX + 2 * (slot % MAX_SLOTS)
                    if slot >= MAX_SLOTS:
                        te.wait_ge(slot_read, slot - MAX_SLOTS + 1)
                    slot += 1
                if what == "max":
                    qt, pair, kc = arg
                    if arg == max_units(s)[0] and s % NQ == 0:
                        for m in range(2):
                            te.wait_ge(m_loaded[m][g], MLOADS)
                    w = max_width(s, arg)
                    diagonal = kc == c
                    for i in range(2):
                        rows = slice(MSTACK * i, MSTACK * (i + 1))
                        mm = nc.tensor.matmul(k.PS[:, bank + i, 0:w], qm[rows, b, pair, qt * P:(qt + 1) * P],
                                              km[rows, b, pair, kc * QW:kc * QW + w], start=True, stop=not diagonal)
                    if diagonal:
                        for i in range(2):
                            mm = nc.tensor.matmul(k.PS[:, bank + i, w - P:w], k.identb[:, :], k.mqkb[:, :], start=False, stop=True)
                    mm.then_inc(slot_made, 1)
                elif what == "turn":
                    te.wait_ge(m_chain, CHAIN * (s + 1))
                    nc.tensor.transpose(k.PS[:, bank, :].bitcast(BF16)[0:HG * 3 * TPQ, 0:P],
                                        mparts[:, s % 2].rearrange("p j r t -> p (j r t)"), k.identb[:, :]).then_inc(slot_made, 1)
                elif what == "score":
                    kt, j = arg
                    if arg == (0, 0):
                        if s % NQ == 0:
                            for m in range(2):
                                te.wait_ge(s_loaded[m][g], SLOADS)
                        te.wait_ge(m_placed[s], 16 * HG)
                    if score >= S_BANKS:
                        te.wait_ge(exped, score - S_BANKS + 1)
                    off = live(s, kt)
                    diagonal = kt >= TPQ * c
                    bank = B_SC + score % S_BANKS
                    score += 1
                    mm = nc.tensor.matmul(k.PS[:, bank, off:QW], ks[0:STACK + 3, b, j, kt * P:(kt + 1) * P],
                                          qs[0:STACK + 3, b, j, c * QW + off:(c + 1) * QW], start=True, stop=not diagonal)
                    if diagonal:
                        mm = nc.tensor.matmul(k.PS[:, bank, off:off + P], k.identb[:, :], k.mkqb[:, :], start=False, stop=True)
                    mm.then_inc(scored, 1)
                elif what == "values":
                    n = nkey[s] + arg
                    te.wait_ge(exped, HG * (n + 1))
                    if arg == 0 and s:
                        te.wait_ge(o_kept, s)
                    off = live(s, arg)
                    for j in range(HG):
                        mm = nc.tensor.matmul(k.PS[HROW * j:HROW * (j + 1), B_PV, off:QW], v[:, arg, g * HG + j, :],
                                              probs[:, n % 2, j, off:QW], start=arg == 0, stop=arg == key_tiles(s) - 1,
                                              tile_position=(0, HROW * j))
                    mm.then_inc(summed, 1)
                elif what == "den":
                    te.wait_ge(o_kept, s + 1)
                    for i in range(TPQ):
                        mm = nc.tensor.matmul(k.PS[:, bank, i * HG:(i + 1) * HG], o[:, g, c * QW + i * P:c * QW + (i + 1) * P],
                                              k.cst[:, C_SEL4:C_SEL4 + HG], start=True, stop=True)
                    mm.then_inc(slot_made, 1)
                else:
                    te.wait_ge(inv_wide, s + 1)
                    for i in range(TPQ):
                        mm = nc.tensor.matmul(k.PS[:, bank, i * P:(i + 1) * P], invw[:, i].rearrange("p j r -> p (j r)"),
                                              k.ident, start=True, stop=True)
                    mm.then_inc(slot_made, 1)

        @block.vector
        def _(dve):
            for slot, (what, s, arg) in enumerate(slot_order):
                g, c = STEPS[s]
                bank = B_MAX + 2 * (slot % MAX_SLOTS)
                dve.wait_ge(slot_made, slot + 1)
                if what == "max":
                    qt, pair, kc = arg
                    w = max_width(s, arg)
                    nc.vector.tensor_reduce(pmax[:, s % 2, qt % TPQ, 2 * pair:2 * pair + 2, kc], k.PS[:, bank:bank + 2, 0:w],
                                            AX.X, ALU.max).then_inc(slot_read, 1)
                    if slot + 1 == slots_to_max[s]:
                        at = CHAIN * s
                        mp = mparts[:, s % 2]
                        dve.wait_ge(slot_read, slot + 1)
                        nc.vector.tensor_reduce(negm[:, s % 2].rearrange("p j t -> p t j"), pmax[:, s % 2, :, :, 0:c + 1],
                                                AX.X, ALU.max, negate=True).then_inc(m_chain, 1)
                        dve.wait_ge(m_chain, at + 1)
                        nc.vector.tensor_copy(mp[:, :, 0, :], negm[:, s % 2]).then_inc(m_chain, 1)
                        dve.wait_ge(m_chain, at + 2)
                        nc.vector.tensor_tensor(negr[:, s % 2], negm[:, s % 2], mp[:, :, 0, :], ALU.subtract).then_inc(m_chain, 1)
                        dve.wait_ge(m_chain, at + 3)
                        nc.vector.tensor_copy(mp[:, :, 1, :], negr[:, s % 2]).then_inc(m_chain, 1)
                        dve.wait_ge(m_chain, at + 4)
                        nc.vector.tensor_tensor(mp[:, :, 2, :], negr[:, s % 2], mp[:, :, 1, :], ALU.subtract).then_inc(m_chain, 1)
                elif what == "turn":
                    if s >= 2:
                        dve.wait_ge(m_placed[s - 2], 16 * HG)
                    nc.vector.tensor_copy(mT[:, s % 2, :], k.PS[:, bank, :].bitcast(BF16)[0:HG * 3 * TPQ, 0:P]).then_inc(slot_read, 1)
                elif what == "den":
                    nc.vector.reciprocal(inv[:, :, :].rearrange("p i j -> p (i j)"), k.PS[:, bank, 0:TPQ * HG]).then_inc(slot_read, 1)
                    dve.wait_ge(slot_read, slot + 1)
                    nc.vector.tensor_copy(invw[:, :, :, :].rearrange("p i j r -> p (i j) r"),
                                          inv[:, :, :].rearrange("p i j -> p (i j)").unsqueeze(2).to_broadcast([P, TPQ * HG, HROW])).then_inc(inv_wide, 1)
                else:
                    part = o[:, g, c * QW:(c + 1) * QW]
                    nc.vector.tensor_tensor(part, part, k.PS[:, bank, :], ALU.mult).then_inc(slot_read, 1)

        @block.scalar
        def _(act):
            i = 0
            for what, s, arg in order:
                g, c = STEPS[s]
                if what == "score":
                    kt, j = arg
                    n = nkey[s] + kt
                    off = live(s, kt)
                    if j == 0 and n >= 2:
                        act.wait_ge(summed, n - 1)
                    act.wait_ge(scored, i + 1)
                    nc.scalar.activation(probs[:, n % 2, j, off:QW], k.PS[:, B_SC + i % S_BANKS, off:QW],
                                         ACT.Exp).then_inc(exped, 1)
                    i += 1
                elif what == "values" and arg == key_tiles(s) - 1:
                    act.wait_ge(summed, nkey[s + 1])
                    nc.scalar.activation(o[:, g, c * QW:(c + 1) * QW], k.PS[:, B_PV, :], ACT.Copy).then_inc(o_kept, 1)


def softmax_out(nc, k, a, att):
    wo = k.sb("wo0", [P, NG, D])
    cleared = k.sem("wo0_cleared")
    landed = k.sem("wo0_landed")
    made = k.sem("out0_made")
    added = k.sem("out0_added")
    with nc.Block() as block:
        @block.gpsimd
        def _(pool):
            nc.gpsimd.memset(wo[:, :, :], 0.0).then_inc(cleared, 1)

        @block.sync
        def _(sp):
            sp.wait_ge(cleared, 1)
            for j in range(HG):
                sp.dma_start(wo[HROW * j:HROW * j + DK0, :, :],
                             a["wo0"].rearrange("(g j r) o -> j r g o", j=HG, r=DK0)[j]).then_inc(landed, 16)

        @block.tensor
        def _(te):
            te.wait_ge(landed, 16 * HG)
            for t in range(NT):
                if t >= 8:
                    te.wait_ge(added, t - 7)
                for g in range(NG):
                    last = nc.tensor.matmul(k.PS[:, t % 8, 0:D], att["o"][:, g, t * P:(t + 1) * P], wo[:, g, :],
                                            start=g == 0, stop=g == NG - 1)
                last.then_inc(made, 1)

        @block.vector
        def _(dve):
            for t in range(NT):
                dve.wait_ge(made, t + 1)
                nc.vector.tensor_tensor(k.h[:, t, :], k.PS[:, t % 8, 0:D], k.h[:, t, :], ALU.add).then_inc(added, 1)


def slot_mixture(nc, k, a):
    B_LOG, B_CMX, B_CMB, B_X, B_SUM, B_XT, B_H, B_Y = range(8)
    sp_w = k.sb("slots", [KH, 2, NSLOT, PSLOT])
    sp_sq = k.sb("slots_sq", [KH, 2, NSLOT, PSLOT])
    sp_f = k.sb("slots_f", [KH, 2, PSLOT])
    sp_g = k.sb("slots_g", [KH, 2, PSLOT])
    sp_s = k.sb("slots_scale", [KH, 1])
    wd = k.sb("w_down", [KH, 2, NSLOT, HDOWN])
    wu = k.sb("w_up", [HDOWN, NSLOT, D])
    bd = k.sb("b_down", [HDOWN, NSLOT])
    bu = k.sb("b_up", [KH, 2, NSLOT])
    logit = k.sb("slot_logit", [P, NT, NP])
    cw = k.sb("c_weight", [P, NT, NP])
    dw = k.sb("d_weight", [P, NT, NP])
    row1 = k.sb("c_row1", [P, NT])
    row2 = k.sb("c_row2", [P, NT])
    cmax = k.sb("d_max", [P, NP])
    cmax1 = k.sb("d_max1", [NP, 1])
    cmaxw = k.sb("d_maxw", [NP, P])
    xt = k.sb("x_tilde", [NP, D])
    dsum = k.sb("d_sum", [NP, 1])
    xtT = k.sb("x_tildeT", [KH, 2, NP])
    hid = k.sb("hid", [HDOWN, NP])
    hact = k.sb("hact", [HDOWN, NP])
    yT = k.sb("y_tildeT", [KH, 2, NP])
    y = k.sb("y_tilde", [NP, D])
    cT = k.sb("c_T", [NP, S])
    landed = k.sem("ffn0_landed")
    dv = k.sem("ffn0_vector")
    ac = k.sem("ffn0_scalar")
    pe = k.sem("ffn0_tensor")
    c_turned = k.sem("c_turned")
    c_kept = k.sem("c_kept")
    made = k.sem("ffn0_out_made")
    added = k.sem("ffn0_out_added")
    (V_SQ, V_NORM, V_EPS, V_INV, V_FAC, V_SP, V_CMAX, V_CMAX1, V_CMAXW, V_LD, V_RMAX, V_LC, V_RSUM, V_RINV, V_C,
     V_DINV, V_XT, V_HB, V_YB) = range(1, 20)
    A_ROOT, A_LOGIT, A_DEXP, A_CEXP, A_XTT, A_GELU, A_Y = range(1, 8)
    T_LOGIT, T_CMX, T_CMB, T_X, T_XT, T_H, T_YT, T_Y = range(1, 9)
    LOADS = 8
    with nc.Block() as block:
        @block.sync
        def _(sp):
            sp.dma_start(sp_w[:, :, :, :], a["L0_ffn_slot_params"].rearrange("(k p) n s -> p k (n s)", p=KH)).then_inc(landed, 16)
            sp.dma_start(sp_s[:, :], a["L0_ffn_scale"].to_broadcast([KH, 1])).then_inc(landed, 16)
            for half in range(2):
                sp.dma_start(wd[:, half, :, :], a["L0_ffn_W_down"][:, half * KH:(half + 1) * KH, :].rearrange("n p h -> p n h")).then_inc(landed, 16)
            sp.dma_start(wu[:, :, :], a["L0_ffn_W_up"].rearrange("n h d -> h n d")).then_inc(landed, 16)
            with nc.allow_non_contiguous_dma(reason="two small biases, turned"):
                sp.dma_start(bd[:, :], a["L0_ffn_b_down"].rearrange("n h -> h n")).then_inc(landed, 16)
                for half in range(2):
                    sp.dma_start(bu[:, half, :], a["L0_ffn_b_up"][:, half * KH:(half + 1) * KH].rearrange("n p -> p n")).then_inc(landed, 16)

        @block.vector
        def _(dve):
            v = nc.vector
            slots = sp_w[:, :, :, :]
            dve.wait_ge(landed, 16 * LOADS)
            v.tensor_tensor(sp_sq[:, :, :, :], slots, slots, ALU.mult).then_inc(dv, 1)
            dve.wait_ge(dv, V_SQ)
            v.tensor_reduce(sp_f[:, :, :], sp_sq[:, :, :, :].rearrange("p k n s -> p k s n"), AX.X, ALU.add).then_inc(dv, 1)
            dve.wait_ge(ac, A_ROOT)
            v.tensor_scalar(sp_f[:, :, :], sp_g[:, :, :], 1e-6, None, ALU.add).then_inc(dv, 1)
            dve.wait_ge(dv, V_EPS)
            v.reciprocal(sp_g[:, :, :], sp_f[:, :, :]).then_inc(dv, 1)
            dve.wait_ge(dv, V_INV)
            v.tensor_scalar(sp_f[:, :, :], sp_g[:, :, :], sp_s[:, 0:1], None, ALU.mult).then_inc(dv, 1)
            dve.wait_ge(dv, V_FAC)
            for half in range(2):
                last = v.tensor_tensor(sp_sq[:, half], sp_w[:, half], sp_f[:, half:half + 1, :].to_broadcast([KH, NSLOT, PSLOT]), ALU.mult)
            last.then_inc(dv, 1)
            dve.wait_ge(ac, A_LOGIT)
            v.tensor_reduce(cmax[:, :], logit[:, :, :].rearrange("p t n -> p n t"), AX.X, ALU.max).then_inc(dv, 1)
            dve.wait_ge(pe, T_CMX)
            v.tensor_reduce(cmax1[:, :], k.PS[0:NP, B_CMX, 0:P], AX.X, ALU.max).then_inc(dv, 1)
            dve.wait_ge(dv, V_CMAX1)
            v.tensor_copy(cmaxw[:, :], cmax1[:, 0:1].to_broadcast([NP, P])).then_inc(dv, 1)
            dve.wait_ge(pe, T_CMB)
            v.tensor_tensor(dw[:, :, :], logit[:, :, :], k.PS[:, B_CMB, 0:NP].unsqueeze(1).to_broadcast([P, NT, NP]),
                            ALU.subtract).then_inc(dv, 1)
            v.tensor_reduce(row1[:, :], logit[:, :, :], AX.X, ALU.max).then_inc(dv, 1)
            dve.wait_ge(dv, V_RMAX)
            v.tensor_tensor(cw[:, :, :], logit[:, :, :], row1[:, :].unsqueeze(2).to_broadcast([P, NT, NP]), ALU.subtract).then_inc(dv, 1)
            dve.wait_ge(ac, A_CEXP)
            v.tensor_reduce(row1[:, :], cw[:, :, :], AX.X, ALU.add).then_inc(dv, 1)
            dve.wait_ge(dv, V_RSUM)
            v.reciprocal(row2[:, :], row1[:, :]).then_inc(dv, 1)
            dve.wait_ge(dv, V_RINV)
            v.tensor_tensor(cw[:, :, :], cw[:, :, :], row2[:, :].unsqueeze(2).to_broadcast([P, NT, NP]), ALU.mult).then_inc(dv, 1)
            dve.wait_ge(pe, T_X)
            v.reciprocal(dsum[:, :], k.PS[0:NP, B_SUM, 0:1]).then_inc(dv, 1)
            dve.wait_ge(dv, V_DINV)
            v.tensor_scalar(xt[:, :], k.PS[0:NP, B_X, 0:D], dsum[:, 0:1], None, ALU.mult).then_inc(dv, 1)
            dve.wait_ge(pe, T_H)
            v.tensor_tensor(hid[:, :].rearrange("p (n s) -> p n s", n=NSLOT), k.PS[0:HDOWN, B_H, 0:NP].rearrange("p (n s) -> p n s", n=NSLOT),
                            bd[:, :].unsqueeze(2).to_broadcast([HDOWN, NSLOT, PSLOT]), ALU.add).then_inc(dv, 1)
            dve.wait_ge(pe, T_YT)
            v.tensor_tensor(yT[:, :, :].rearrange("p k (n s) -> p (k n) s", n=NSLOT),
                            k.PS[0:KH, B_Y, 0:2 * NP].rearrange("p (n s) -> p n s", n=2 * NSLOT),
                            bu[:, :, :].rearrange("p k n -> p (k n)").unsqueeze(2).to_broadcast([KH, 2 * NSLOT, PSLOT]),
                            ALU.add).then_inc(dv, 1)
            for t in range(NT):
                dve.wait_ge(made, t + 1)
                v.tensor_tensor(k.h[:, t, :], k.PS[:, t % 8, 0:D], k.h[:, t, :], ALU.add).then_inc(added, 1)

        @block.scalar
        def _(act):
            act.wait_ge(dv, V_NORM)
            nc.scalar.activation(sp_g[:, :, :], sp_f[:, :, :], ACT.Sqrt).then_inc(ac, 1)
            act.wait_ge(pe, T_LOGIT)
            nc.scalar.activation(logit[:, :, :], k.PS[:, B_LOG, :].rearrange("p (t n) -> p t n", t=NT), ACT.Copy).then_inc(ac, 1)
            act.wait_ge(dv, V_LD)
            nc.scalar.activation(dw[:, :, :], dw[:, :, :], ACT.Exp).then_inc(ac, 1)
            act.wait_ge(dv, V_LC)
            nc.scalar.activation(cw[:, :, :], cw[:, :, :], ACT.Exp).then_inc(ac, 1)
            act.wait_ge(pe, T_XT)
            nc.scalar.activation(xtT[:, :, :], k.PS[0:KH, B_XT, 0:2 * NP].rearrange("p (k n) -> p k n", k=2), ACT.Copy).then_inc(ac, 1)
            act.wait_ge(dv, V_HB)
            nc.scalar.activation(hact[:, :], hid[:, :], ACT.Gelu).then_inc(ac, 1)
            for b in range(4):
                act.wait_ge(c_turned, b + 1)
                nc.scalar.activation(cT[:, b * 512:(b + 1) * 512], k.PS[0:NP, b, :], ACT.Copy).then_inc(c_kept, 1)
            act.wait_ge(pe, T_Y)
            nc.scalar.activation(y[:, :], k.PS[0:NP, B_XT, 0:D], ACT.Copy).then_inc(ac, 1)

        @block.tensor
        def _(te):
            mm = nc.tensor.matmul
            te.wait_ge(dv, V_SP)
            for t in range(NT):
                for half in range(2):
                    last = mm(k.PS[:, B_LOG, t * NP:(t + 1) * NP], k.xnT[:, half, t * P:(t + 1) * P],
                              sp_sq[:, half].rearrange("p n s -> p (n s)"), start=half == 0, stop=half == 1)
            last.then_inc(pe, 1)
            te.wait_ge(dv, V_CMAX)
            nc.tensor.transpose(k.PS[0:NP, B_CMX, 0:P], cmax[:, :], k.ident).then_inc(pe, 1)
            te.wait_ge(dv, V_CMAXW)
            mm(k.PS[:, B_CMB, 0:NP], cmaxw[:, :], k.cst[0:NP, C_ID:C_ID + NP], start=True, stop=True).then_inc(pe, 1)
            te.wait_ge(ac, A_DEXP)
            for t in range(NT):
                mm(k.PS[0:NP, B_X, 0:D], dw[:, t, :], k.xn[:, t, :], start=t == 0, stop=t == NT - 1)
                last = mm(k.PS[0:NP, B_SUM, 0:1], dw[:, t, :], k.cst[:, C_ONE:C_ONE + 1], start=t == 0, stop=t == NT - 1)
            last.then_inc(pe, 1)
            te.wait_ge(dv, V_XT)
            for half in range(2):
                last = nc.tensor.transpose(k.PS[0:KH, B_XT, half * NP:(half + 1) * NP], xt[:, half * KH:(half + 1) * KH],
                                           k.cst[0:NP, C_ID:C_ID + NP])
            last.then_inc(pe, 1)
            te.wait_ge(ac, A_XTT)
            for n in range(NSLOT):
                for half in range(2):
                    last = mm(k.PS[0:HDOWN, B_H, n * PSLOT:(n + 1) * PSLOT], wd[:, half, n, :],
                              xtT[:, half, n * PSLOT:(n + 1) * PSLOT], start=half == 0, stop=half == 1)
            last.then_inc(pe, 1)
            te.wait_ge(ac, A_GELU)
            for half in range(2):
                for n in range(NSLOT):
                    last = mm(k.PS[0:KH, B_Y, half * NP + n * PSLOT:half * NP + (n + 1) * PSLOT],
                              wu[:, n, half * KH:(half + 1) * KH], hact[:, n * PSLOT:(n + 1) * PSLOT], start=True, stop=True)
            last.then_inc(pe, 1)
            te.wait_ge(dv, V_XT)
            for b in range(4):
                for i in range(4):
                    last = nc.tensor.transpose(k.PS[0:NP, b, i * P:(i + 1) * P], cw[:, 4 * b + i, :], k.ident)
                last.then_inc(c_turned, 1)
            te.wait_ge(dv, V_YB)
            for half in range(2):
                last = nc.tensor.transpose(k.PS[0:NP, B_XT, half * KH:(half + 1) * KH], yT[:, half, :], k.cst[0:KH, C_ID:C_ID + KH])
            last.then_inc(pe, 1)
            te.wait_ge(ac, A_Y)
            te.wait_ge(c_kept, 4)
            for t in range(NT):
                if t >= 8:
                    te.wait_ge(added, t - 7)
                mm(k.PS[:, t % 8, 0:D], cT[:, t * P:(t + 1) * P], y[:, :], start=True, stop=True).then_inc(made, 1)


def linear_project(nc, k, a, lin):
    w = {m: k.sb(f"w1_{m}", [KH, 2, DIM1 if m != "g" else D]) for m in "qkvg"}
    low = k.sb("low", [P, 2, QW])
    elo = k.sb("elo", [P, 2, QW])
    landed = k.sem("w1_landed")
    made = k.sem("lin_made")
    lowered = k.sem("lowered")
    exped = k.sem("lin_exped")
    mapped = k.sem("mapped")
    kept = k.sem("lin_kept")
    v_ones = k.sem("v_ones")
    units = [(m, pair, c) for m in "kq" for pair in range(NPAIR) for c in range(NQ)]
    NU = len(units)
    rest = [(what, t) for what in ("turn", "v", "gate") for t in range(NT)]
    with nc.Block() as block:
        @block.sync
        def _(sp):
            for m, name in (("k", "L1_attn_Wk"), ("q", "L1_attn_Wq"), ("v", "L1_attn_Wv"), ("g", "L1_attn_Wg")):
                sp.dma_start(w[m][:, :, :], a[name].rearrange("(k p) o -> p k o", p=KH)).then_inc(landed, 16)

        @block.gpsimd
        def _(pool):
            nc.gpsimd.memset(lin["v"][:, :, :, D1:D1 + 1], 1.0)
            nc.gpsimd.memset(lin["state"][:, :, :], 0.0)

        @block.tensor
        def _(te):
            te.wait_ge(landed, 64)
            for n, (m, pair, c) in enumerate(units):
                if n >= 8:
                    te.wait_ge(mapped, n - 7)
                for half in range(2):
                    last = nc.tensor.matmul(k.PS[:, n % 8, :], w[m][:, half, pair * P:(pair + 1) * P],
                                            k.xnT[:, half, c * QW:(c + 1) * QW], start=half == 0, stop=half == 1)
                last.then_inc(made, 1)
            for i, (what, t) in enumerate(rest):
                if i < 8:
                    te.wait_ge(mapped, NU - 7 + i)
                else:
                    te.wait_ge(kept, i - 7)
                bank = i % 8
                if what == "turn":
                    for pair in range(NPAIR):
                        last = nc.tensor.transpose(k.PS[:, bank, pair * P:(pair + 1) * P],
                                                   lin["kT"][:, pair, t * P:(t + 1) * P], k.ident)
                else:
                    n, m = (DIM1, "v") if what == "v" else (D, "g")
                    for half in range(2):
                        last = nc.tensor.matmul(k.PS[:, bank, 0:n], k.xnT[:, half, t * P:(t + 1) * P], w[m][:, half, :],
                                                start=half == 0, stop=half == 1)
                last.then_inc(made, 1)

        @block.vector
        def _(dve):
            def finish(n):
                m, pair, c = units[n]
                dve.wait_ge(exped, n + 1)
                nc.vector.scalar_tensor_tensor(lin[m + "T"][:, pair, c * QW:(c + 1) * QW], k.PS[:, n % 8, :], 0.0,
                                               elo[:, n % 2, :], ALU.max, ALU.add).then_inc(mapped, 1)

            for n in range(NU):
                dve.wait_ge(made, n + 1)
                if n >= 2:
                    dve.wait_ge(exped, n - 1)
                nc.vector.tensor_scalar(low[:, n % 2, :], k.PS[:, n % 8, :], 0.0, None, ALU.min).then_inc(lowered, 1)
                if n >= 1:
                    finish(n - 1)
            finish(NU - 1)

        @block.scalar
        def _(act):
            for n in range(NU):
                act.wait_ge(lowered, n + 1)
                if n >= 2:
                    act.wait_ge(mapped, n - 1)
                nc.scalar.activation(elo[:, n % 2, :], low[:, n % 2, :], ACT.Exp).then_inc(exped, 1)
            for i, (what, t) in enumerate(rest):
                act.wait_ge(made, NU + i + 1)
                ps = k.PS[:, i % 8, :]
                if what == "turn":
                    last = nc.scalar.activation(lin["k"][:, t, :], ps[:, 0:DIM1], ACT.Copy)
                elif what == "v":
                    last = nc.scalar.activation(lin["v"][:, t, :, 0:D1], ps[:, 0:DIM1].rearrange("p (h d) -> p h d", d=D1), ACT.Copy)
                else:
                    last = nc.scalar.activation(lin["gate"][:, t, :], ps[:, 0:D], ACT.Sigmoid)
                last.then_inc(kept, 1)


def linear_attention(nc, k, a, lin):
    B_A, B_N, B_S, B_T, B_Y = 0, 2, 4, 5, 6
    wo = k.sb("wo1", [P, NPAIR, D])
    at = k.sb("lin_scores", [P, 2, 2, NPAIR, P])
    den = k.sb("lin_den", [P, 2, NPAIR])
    inv = k.sb("lin_inv", [P, 2, NPAIR])
    on = k.sb("lin_out", [P, 2, NPAIR, 2, D1])
    oT = k.sb("lin_outT", [P, 2, NPAIR, P])
    gated = k.sb("gated", [P, 2, D])
    landed = k.sem("wo1_landed")
    scored = k.sem("lin_scored")
    masked = k.sem("lin_masked")
    numed = k.sem("lin_numed")
    stated = k.sem("lin_stated")
    summed = k.sem("lin_summed")
    dened = k.sem("lin_dened")
    inved = k.sem("lin_inved")
    normed = k.sem("lin_normed")
    turned = k.sem("lin_turned")
    kept = k.sem("lin_outT_kept")
    made = k.sem("lin_y_made")
    gates = k.sem("lin_gated")
    added = k.sem("lin_added")
    with nc.Block() as block:
        @block.sync
        def _(sp):
            sp.dma_start(wo[:, :, :], a["L1_attn_Wo"].rearrange("(k p) o -> p k o", p=P)).then_inc(landed, 16)

        @block.tensor
        def _(te):
            mm = nc.tensor.matmul

            def scores(c):
                if c >= 1:
                    te.wait_ge(masked, c)
                for odd in range(2):
                    rows = slice(odd * D1, (odd + 1) * D1)
                    for pair in range(NPAIR):
                        last = mm(k.PS[:, B_A + odd, pair * P:(pair + 1) * P], lin["kT"][rows, pair, c * P:(c + 1) * P],
                                  lin["qT"][rows, pair, c * P:(c + 1) * P], start=True, stop=True)
                last.then_inc(scored, 1)

            def project(c):
                te.wait_ge(normed, c + 1)
                if c >= 1:
                    te.wait_ge(kept, c)
                for pair in range(NPAIR):
                    last = nc.tensor.transpose(k.PS[:, B_T, pair * P:(pair + 1) * P],
                                               on[:, c % 2, pair].rearrange("p o d -> p (o d)"), k.ident)
                last.then_inc(turned, 1)
                te.wait_ge(kept, c + 1)
                if c >= 1:
                    te.wait_ge(gates, c)
                for pair in range(NPAIR):
                    last = mm(k.PS[:, B_Y, 0:D], oT[:, c % 2, pair, :], wo[:, pair, :], start=pair == 0, stop=pair == NPAIR - 1)
                last.then_inc(made, 1)

            te.wait_ge(landed, 16)
            scores(0)
            for c in range(NT):
                if c >= 1:
                    te.wait_ge(summed, c)
                for h in range(H1):
                    last = mm(k.PS[(h % 2) * D1:(h % 2 + 1) * D1, B_S, (h // 2) * (D1 + 1):(h // 2 + 1) * (D1 + 1)],
                              lin["k"][:, c, h * D1:(h + 1) * D1], lin["v"][:, c, h, :], start=True, stop=True)
                last.then_inc(stated, 1)
                if c + 1 < NT:
                    scores(c + 1)
                te.wait_ge(masked, c + 1)
                if c >= 1:
                    te.wait_ge(normed, c)
                for odd in range(2):
                    rows = slice(odd * D1, (odd + 1) * D1)
                    for pair in range(NPAIR):
                        out = k.PS[:, B_N + odd, pair * (D1 + 1):(pair + 1) * (D1 + 1)]
                        last = mm(out, at[:, c % 2, odd, pair, :], lin["v"][:, c, 2 * pair + odd, :], start=True, stop=c == 0)
                        if c:
                            last = mm(out, lin["qT"][rows, pair, c * P:(c + 1) * P], lin["states"][rows, c % 2, pair, :],
                                      start=False, stop=True)
                last.then_inc(numed, 1)
                if c >= 1:
                    project(c - 1)
            project(NT - 1)

        @block.vector
        def _(dve):
            v = nc.vector

            def norm(c):
                num = k.PS[:, B_N:B_N + 2, 0:2 * (D1 + 1)].rearrange("p o (q d) -> p o q d", q=NPAIR)
                dve.wait_ge(numed, c + 1)
                v.tensor_scalar(den[:, :, :], num[:, :, :, D1], 1e-6, None, ALU.max).then_inc(dened, 1)
                dve.wait_ge(dened, c + 1)
                v.reciprocal(inv[:, :, :], den[:, :, :]).then_inc(inved, 1)
                dve.wait_ge(inved, c + 1)
                if c >= 2:
                    dve.wait_ge(turned, c - 1)
                for odd in range(2):
                    last = v.tensor_tensor(on[:, c % 2, :, odd, :], num[:, odd, :, 0:D1],
                                           inv[:, odd, :].unsqueeze(2).to_broadcast([P, NPAIR, D1]), ALU.mult)
                last.then_inc(normed, 1)

            def add(c):
                dve.wait_ge(made, c + 1)
                v.tensor_tensor(gated[:, c % 2, :], k.PS[:, B_Y, 0:D], lin["gate"][:, c, :], ALU.mult).then_inc(gates, 1)
                dve.wait_ge(gates, c + 1)
                v.tensor_tensor(k.h[:, c, :], k.h[:, c, :], gated[:, c % 2, :], ALU.add).then_inc(added, 1)

            def mask(c):
                dve.wait_ge(scored, c + 1)
                if c >= 2:
                    dve.wait_ge(numed, c - 1)
                for odd in range(2):
                    last = v.tensor_tensor(at[:, c % 2, odd], k.PS[:, B_A + odd, 0:NPAIR * P].rearrange("p (q n) -> p q n", q=NPAIR),
                                           k.tri.unsqueeze(1).to_broadcast([P, NPAIR, P]), ALU.mult)
                last.then_inc(masked, 1)

            mask(0)
            for c in range(NT):
                dve.wait_ge(stated, c + 1)
                if c >= 1:
                    dve.wait_ge(summed, c)
                    dve.wait_ge(numed, c)
                v.tensor_tensor(lin["states"][:, (c + 1) % 2], k.PS[:, B_S, 0:NPAIR * (D1 + 1)].rearrange("p (q d) -> p q d", q=NPAIR),
                                lin["states"][:, c % 2] if c else lin["state"][:, :, :], ALU.add).then_inc(summed, 1)
                if c + 1 < NT:
                    mask(c + 1)
                norm(c)
                if c >= 1:
                    add(c - 1)
            add(NT - 1)

        @block.scalar
        def _(act):
            for c in range(NT):
                act.wait_ge(turned, c + 1)
                if c >= 2:
                    act.wait_ge(made, c - 1)
                nc.scalar.activation(oT[:, c % 2], k.PS[:, B_T, 0:NPAIR * P].rearrange("p (q n) -> p q n", q=NPAIR),
                                     ACT.Copy).then_inc(kept, 1)


def route(nc, k, a, moe):
    wr = k.sb("w_router", [KH, 2, E])
    t1 = k.sb("route1", [P, NT, E])
    t2 = k.sb("route2", [P, NT, E])
    prob = k.sb("prob", [P, NT, E])
    row = k.sb("route_row", [P, 2, NT])
    mask = k.sb("mask", [P, NT, 2, E])
    maskb = k.sb("maskb", [P, NT, 2, E], BF16)
    place = k.sb("place", [P, NT, 2, E])
    total = k.sb("total", [P, NT, 2, E])
    both = k.sb("both", [P, GRP, E])
    landed = k.sem("wr_landed")
    made = k.sem("router_made")
    dv = k.sem("route_vector")
    ac = k.sem("route_scalar")
    with nc.Block() as block:
        @block.sync
        def _(sp):
            sp.dma_start(wr[:, :, :], a["L1_ffn_w_router"].rearrange("(k p) e -> p k e", p=KH)).then_inc(landed, 16)

        @block.tensor
        def _(te):
            te.wait_ge(landed, 16)
            for t in range(NT):
                for half in range(2):
                    last = nc.tensor.matmul(k.PS[:, 0, t * E:(t + 1) * E], k.xnT[:, half, t * P:(t + 1) * P], wr[:, half, :],
                                            start=half == 0, stop=half == 1)
            last.then_inc(made, 1)
            te.wait_ge(dv, MASKED_AT)
            rhs = maskb[:, :, :, :].rearrange("p t c e -> p (t c e)")
            nc.tensor.matmul(k.PS[:, 1, 0:2 * NT * E], k.trib[:, :], rhs, start=True, stop=True)
            nc.tensor.matmul(k.PS[:, 2, 0:2 * NT * E], k.oneb[:, :], rhs, start=True, stop=True).then_inc(made, 1)

        @block.scalar
        def _(act):
            act.wait_ge(dv, 2)
            nc.scalar.activation(t2[:, :, :], t1[:, :, :], ACT.Exp).then_inc(ac, 1)

        @block.vector
        def _(dve):
            v = nc.vector
            steps = [0]

            def wide(x):
                return x.unsqueeze(2).to_broadcast([P, NT, E])

            def then(ins):
                steps[0] += 1
                ins.then_inc(dv, 1)
                dve.wait_ge(dv, steps[0])

            logits = k.PS[:, 0, 0:NT * E].rearrange("p (t e) -> p t e", t=NT)
            dve.wait_ge(made, 1)
            then(v.tensor_reduce(row[:, 0, :], logits, AX.X, ALU.max))
            then(v.tensor_tensor(t1[:, :, :], logits, wide(row[:, 0, :]), ALU.subtract))
            dve.wait_ge(ac, 1)
            then(v.tensor_reduce(row[:, 0, :], t2[:, :, :], AX.X, ALU.add))
            then(v.reciprocal(row[:, 1, :], row[:, 0, :]))
            then(v.tensor_tensor(prob[:, :, :], t2[:, :, :], wide(row[:, 1, :]), ALU.mult))
            rank = k.cst[:, C_RANK:C_RANK + E].unsqueeze(1).to_broadcast([P, NT, E])
            for c in range(2):
                src = prob if c == 0 else t2
                then(v.tensor_reduce(row[:, 0, :], src[:, :, :], AX.X, ALU.max))
                then(v.tensor_tensor(t1[:, :, :], src[:, :, :], wide(row[:, 0, :]), ALU.is_equal))
                then(v.tensor_tensor(t1[:, :, :], t1[:, :, :], rank, ALU.mult))
                then(v.tensor_reduce(row[:, 1, :], t1[:, :, :], AX.X, ALU.max))
                then(v.tensor_tensor(mask[:, :, c, :], t1[:, :, :], wide(row[:, 1, :]), ALU.is_equal))
                if c == 0:
                    then(v.scalar_tensor_tensor(t2[:, :, :], mask[:, :, 0, :], -2.0, prob[:, :, :], ALU.mult, ALU.add))
            then(v.tensor_copy(maskb[:, :, :, :], mask[:, :, :, :]))
            assert steps[0] == MASKED_AT
            then(v.tensor_tensor(t1[:, :, :], mask[:, :, 0, :], mask[:, :, 1, :], ALU.add))
            then(v.tensor_tensor(moe["gate"][:, :, :], t1[:, :, :], prob[:, :, :], ALU.mult))
            dve.wait_ge(made, 2)
            shape = "p (t c e) -> p t c e"
            then(v.tensor_copy(place[:, :, :, :].rearrange("p t c e -> p (t c e)"), k.PS[:, 1, 0:2 * NT * E]))
            then(v.tensor_copy(total[:, :, :, :].rearrange("p t c e -> p (t c e)"), k.PS[:, 2, 0:2 * NT * E]))
            pg = place[:, :, :, :].rearrange("p (g i) c e -> p g i (c e)", i=TPG)
            tg = total[:, :, :, :].rearrange("p (g i) c e -> p g i (c e)", i=TPG)
            then(v.tensor_tensor(pg[:, :, 1, :], pg[:, :, 1, :], tg[:, :, 0, :], ALU.add))
            then(v.tensor_tensor(both[:, :, :], tg[:, :, 0, 0:E], tg[:, :, 1, 0:E], ALU.add))
            for i in range(TPG):
                then(v.tensor_tensor(pg[:, :, i, E:2 * E], pg[:, :, i, E:2 * E], both[:, :, :], ALU.add))
            then(v.tensor_tensor(place[:, :, :, :], place[:, :, :, :], mask[:, :, :, :], ALU.mult))
            then(v.tensor_tensor(t1[:, :, :], place[:, :, 0, :], place[:, :, 1, :], ALU.add))
            then(v.tensor_scalar(moe["place"][:, :, :], t1[:, :, :], -1.0, None, ALU.add))


MASKED_AT = 17


def dispatch(nc, k, a, moe):
    disp = k.sb("disp", [P, 2, TPG, E, CAP])
    listed = k.sem("disp_listed")
    made = k.sem("disp_made")
    kept = k.sem("disp_kept")
    with nc.Block() as block:
        @block.vector
        def _(dve):
            for g in range(GRP):
                if g >= 2:
                    dve.wait_ge(made, 4 * (g - 1))
                for i in range(TPG):
                    t = g * TPG + i
                    last = nc.vector.tensor_tensor(disp[:, g % 2, i], k.cst[:, C_IOTA:C_IOTA + CAP].unsqueeze(1).to_broadcast([P, E, CAP]),
                                                   moe["place"][:, t, :].unsqueeze(2).to_broadcast([P, E, CAP]), ALU.is_equal)
                last.then_inc(listed, 1)

        @block.tensor
        def _(te):
            n = 0
            for g in range(GRP):
                te.wait_ge(listed, g + 1)
                for half in range(2):
                    for eh in range(2):
                        if n >= 8:
                            te.wait_ge(kept, n - 7)
                        for i in range(TPG):
                            last = nc.tensor.matmul(k.PS[0:KH, n % 8, 0:EHALF], k.xn[:, g * TPG + i, half * KH:(half + 1) * KH],
                                                    disp[:, g % 2, i, eh * 4:(eh + 1) * 4, :].rearrange("p e c -> p (e c)"),
                                                    start=i == 0, stop=i == TPG - 1)
                        last.then_inc(made, 1)
                        n += 1

        @block.scalar
        def _(act):
            n = 0
            for g in range(GRP):
                for half in range(2):
                    for eh in range(2):
                        act.wait_ge(made, n + 1)
                        nc.scalar.activation(moe["xin"][:, half, eh * 4:(eh + 1) * 4, g, :],
                                             k.PS[0:KH, n % 8, 0:EHALF].rearrange("p (e c) -> p e c", c=CAP), ACT.Copy).then_inc(kept, 1)
                        n += 1


def experts(nc, k, a, moe):
    HALVES = 2
    SH = SLOTS // HALVES
    GH = GRP // HALVES
    wi = k.sb("wi", [KH, 2, F])
    wo = k.sb("wo2", [P, NF, D])
    wih, wil = (k.sb(f"wi_{x}", [KH, 2, F], F32R) for x in ("high", "low"))
    woh, wol = (k.sb(f"wo_{x}", [P, NF, D], F32R) for x in ("high", "low"))
    xh, xl = (k.sb(f"xin_{x}", [KH, 2, SLOTS], F32R) for x in ("high", "low"))
    hh, hl = (k.sb(f"hid_{x}", [P, HALVES, NF, SH], F32R) for x in ("high", "low"))
    wi_landed = k.sem("wi_landed")
    wo_landed = k.sem("wo_landed")
    in_high = k.sem("in_high")
    in_low = k.sem("in_low")
    wo_high = k.sem("wo_high_made")
    wo_low = k.sem("wo_low_made")
    made = k.sem("expert_made")
    hid_high = k.sem("hid_high_made")
    hid_low = k.sem("hid_low_made")
    outed = k.sem("expert_outed")
    kept = k.sem("expert_kept")
    UN = NF * HALVES
    RING = 4
    SPLIT_WO = 4

    def f(x):
        return x.bitcast(F32)

    with nc.Block() as block:
        @block.sync
        def _(sp):
            for e in range(E):
                if e >= 1:
                    sp.wait_ge(in_low, 2 * e)
                sp.dma_start(wi[:, :, :], a["L1_ffn_wi"][e].rearrange("(k p) f -> p k f", p=KH)).then_inc(wi_landed, 16)
                if e >= 1:
                    sp.wait_ge(wo_low, e)
                sp.dma_start(wo[:, :, :], a["L1_ffn_wo"][e].rearrange("(f p) d -> p f d", p=P)).then_inc(wo_landed, 16)

        @block.tensor
        def _(te):
            mm = nc.tensor.matmul
            n = m = 0
            for e in range(E):
                te.wait_ge(in_low, 2 * (e + 1))
                for s in range(HALVES):
                    for t in range(NF):
                        if n >= RING:
                            te.wait_ge(hid_low, n - RING + 1)
                        out = k.PS[:, n % RING, 0:SH]
                        for half in range(2):
                            cols, rows = slice(t * P, (t + 1) * P), slice(s * SH, (s + 1) * SH)
                            mm(out, wih[:, half, cols], xh[:, half, rows], start=half == 0, stop=False)
                            mm(out, wih[:, half, cols], xl[:, half, rows], start=False, stop=False)
                            last = mm(out, wil[:, half, cols], xh[:, half, rows], start=False, stop=half == 1)
                        last.then_inc(made, 1)
                        n += 1
                te.wait_ge(wo_low, e + 1)
                for s in range(HALVES):
                    te.wait_ge(hid_low, UN * e + NF * (s + 1))
                    for g in range(GH):
                        if m >= RING:
                            te.wait_ge(kept, m - RING + 1)
                        out = k.PS[0:CAP, RING + m % RING, 0:D]
                        rows = slice(g * CAP, (g + 1) * CAP)
                        for t in range(NF):
                            mm(out, hh[:, s, t, rows], woh[:, t, :], start=t == 0, stop=False)
                            mm(out, hh[:, s, t, rows], wol[:, t, :], start=False, stop=False)
                            last = mm(out, hl[:, s, t, rows], woh[:, t, :], start=False, stop=t == NF - 1)
                        last.then_inc(outed, 1)
                        m += 1

        @block.vector
        def _(dve):
            def low_in(e):
                dve.wait_ge(in_high, 2 * e + 1)
                nc.vector.tensor_tensor(xl[:, :, :], moe["xin"][:, :, e].rearrange("p k g c -> p k (g c)"), f(xh[:, :, :]),
                                        ALU.subtract).then_inc(in_low, 1)
                dve.wait_ge(in_high, 2 * e + 2)
                nc.vector.tensor_tensor(wil[:, :, :], wi[:, :, :], f(wih[:, :, :]), ALU.subtract).then_inc(in_low, 1)

            low_in(0)
            for e in range(E):
                for u in range(UN):
                    s, t = u // NF, u % NF
                    n = UN * e + u
                    if u == SPLIT_WO:
                        dve.wait_ge(wo_high, e + 1)
                        nc.vector.tensor_tensor(wol[:, :, :], wo[:, :, :], f(woh[:, :, :]), ALU.subtract).then_inc(wo_low, 1)
                    dve.wait_ge(hid_high, n + 1)
                    nc.vector.scalar_tensor_tensor(hl[:, s, t, :], k.PS[:, n % RING, 0:SH], 0.0, f(hh[:, s, t, :]),
                                                   ALU.max, ALU.subtract).then_inc(hid_low, 1)
                if e + 1 < E:
                    low_in(e + 1)

        @block.scalar
        def _(act):
            def high_in(e):
                if e:
                    act.wait_ge(made, UN * e)
                nc.scalar.activation(xh[:, :, :], moe["xin"][:, :, e].rearrange("p k g c -> p k (g c)"), ACT.Copy).then_inc(in_high, 1)
                act.wait_ge(wi_landed, 16 * (e + 1))
                nc.scalar.activation(wih[:, :, :], wi[:, :, :], ACT.Copy).then_inc(in_high, 1)

            def keep(e, g):
                n = GRP * e + g
                act.wait_ge(outed, n + 1)
                nc.scalar.activation(moe["eo"][:, e, g, :], k.PS[0:CAP, RING + n % RING, 0:D], ACT.Copy).then_inc(kept, 1)

            high_in(0)
            for e in range(E):
                for u in range(UN):
                    s, t = u // NF, u % NF
                    n = UN * e + u
                    if u == SPLIT_WO:
                        if e:
                            act.wait_ge(outed, GRP * e)
                        act.wait_ge(wo_landed, 16 * (e + 1))
                        nc.scalar.activation(woh[:, :, :], wo[:, :, :], ACT.Copy).then_inc(wo_high, 1)
                    act.wait_ge(made, n + 1)
                    if e and t == 0:
                        act.wait_ge(outed, GRP * (e - 1) + GH * (s + 1))
                    nc.scalar.activation(hh[:, s, t, :], k.PS[:, n % RING, 0:SH], ACT.Relu).then_inc(hid_high, 1)
                for g in range(GRP):
                    if g == 2 and e + 1 < E:
                        high_in(e + 1)
                    keep(e, g)


def combine(nc, k, a, moe, out):
    LISTS, TURNS = 4, 3
    comb = k.sb("comb", [P, LISTS, E, CAP])
    combT = k.sb("combT", [CAP, TURNS, E, P])
    listed = k.sem("comb_listed")
    turned = k.sem("comb_turned")
    kept = k.sem("comb_kept")
    made = k.sem("comb_made")
    added = k.sem("comb_added")
    stored = k.sem("stored")
    with nc.Block() as block:
        @block.vector
        def _(dve):
            def place(t):
                if t >= LISTS:
                    dve.wait_ge(turned, 2 * (t - LISTS + 1))
                for e in range(E):
                    last = nc.vector.tensor_scalar(comb[:, t % LISTS, e, :], k.cst[:, C_IOTA:C_IOTA + CAP], moe["place"][:, t, e:e + 1],
                                                   moe["gate"][:, t, e:e + 1], ALU.is_equal, ALU.mult)
                last.then_inc(listed, 1)

            for t in range(LISTS):
                place(t)
            for t in range(NT):
                dve.wait_ge(made, t + 1)
                nc.vector.tensor_tensor(k.h[:, t, :], k.PS[:, 4 + t % 4, 0:D], k.h[:, t, :], ALU.add).then_inc(added, 1)
                if t + LISTS < NT:
                    place(t + LISTS)

        @block.tensor
        def _(te):
            def turn(t):
                te.wait_ge(listed, t + 1)
                for b in range(2):
                    n = 2 * t + b
                    if n >= 4:
                        te.wait_ge(kept, n - 3)
                    for i in range(4):
                        last = nc.tensor.transpose(k.PS[0:CAP, n % 4, i * P:(i + 1) * P], comb[:, t % LISTS, 4 * b + i, :], k.ident)
                    last.then_inc(turned, 1)

            turn(0)
            turn(1)
            for t in range(NT):
                if t + 2 < NT:
                    turn(t + 2)
                te.wait_ge(kept, 2 * t + 2)
                if t >= 4:
                    te.wait_ge(added, t - 3)
                for e in range(E):
                    last = nc.tensor.matmul(k.PS[:, 4 + t % 4, 0:D], combT[:, t % TURNS, e, :], moe["eo"][:, e, t // TPG, :],
                                            start=e == 0, stop=e == E - 1)
                last.then_inc(made, 1)

        @block.scalar
        def _(act):
            for n in range(2 * NT):
                t, b = n // 2, n % 2
                act.wait_ge(turned, n + 1)
                if t >= TURNS:
                    act.wait_ge(made, t - TURNS + 1)
                nc.scalar.activation(combT[:, t % TURNS, 4 * b:4 * b + 4, :], k.PS[0:CAP, n % 4, :].rearrange("p (e n) -> p e n", e=4),
                                     ACT.Copy).then_inc(kept, 1)

        @block.sync
        def _(sp):
            view = out.rearrange("(q t p) d -> q p t d", p=P, t=4)
            for q in range(NT // 4):
                sp.wait_ge(added, 4 * q + 4)
                sp.dma_start(view[q], k.h[:, 4 * q:4 * q + 4, :]).then_inc(stored, 16)
            sp.wait_ge(stored, 16 * (NT // 4))


def store(nc, k, out):
    stored = k.sem("stored")
    with nc.Block() as block:
        @block.sync
        def _(sp):
            sp.dma_start(out.rearrange("(t p) d -> p t d", p=P), k.h[:, :, :]).then_inc(stored, 16)
            sp.wait_ge(stored, 16)


def program(nc, a, out, upto=99):
    with ExitStack() as ctx:
        k = Core(nc, ctx)
        with k.room():
            att = {
                "scratch": nc.dram_tensor("qk_parts", [2, 3, D, S], BF16, kind="Internal").ap(),
                "o": k.sb("o0", [P, NG, S]),
                "v": k.sb("v0", [P, NT, H0, HROW]),
                "ks": k.sb("ks", [P, 2, HG, S], BF16),
                "v_cleared": k.sem("v_cleared"),
            }
            with k.room():
                k.rows(0)
                with k.room():
                    embed(nc, k, a)
                if upto >= 1:
                    layernorm(nc, k, "ln1")
                    with k.room():
                        softmax_qkv(nc, k, a, att)
            if upto >= 2:
                with k.room():
                    att["qs"] = k.sb("qs", [P, 2, HG, S], BF16)
                    att["qm"] = k.sb("qm", [P, 2, HG // 2, S], BF16)
                    att["km"] = k.sb("km", [P, 2, HG // 2, S], BF16)
                    softmax_attention(nc, k, a, att)
                with k.room():
                    softmax_out(nc, k, a, att)
        moe = {
            "gate": k.sb("moe_gate", [P, NT, E]),
            "place": k.sb("moe_place", [P, NT, E]),
            "xin": k.sb("moe_xin", [KH, 2, E, GRP, CAP]),
        }
        with k.room():
            k.rows(1)
            if upto >= 3:
                layernorm(nc, k, "ln2", l2=True)
                with k.room():
                    slot_mixture(nc, k, a)
            if upto >= 4:
                layernorm(nc, k, "ln3")
                with k.room():
                    lin = {
                        "qT": k.sb("lin_qT", [P, NPAIR, S]),
                        "kT": k.sb("lin_kT", [P, NPAIR, S]),
                        "k": k.sb("lin_k", [P, NT, DIM1]),
                        "v": k.sb("lin_v", [P, NT, H1, D1 + 1]),
                        "gate": k.sb("lin_gate", [P, NT, D]),
                        "state": k.sb("lin_state0", [P, NPAIR, D1 + 1]),
                        "states": k.sb("lin_states", [P, 2, NPAIR, D1 + 1]),
                    }
                    with k.room():
                        linear_project(nc, k, a, lin)
                    with k.room():
                        linear_attention(nc, k, a, lin)
            if upto >= 5:
                layernorm(nc, k, "ln4")
                with k.room():
                    route(nc, k, a, moe)
                with k.room():
                    dispatch(nc, k, a, moe)
        if upto >= 5:
            with k.room():
                moe["eo"] = k.sb("moe_eo", [CAP, E, GRP, D])
                with k.room():
                    experts(nc, k, a, moe)
                with k.room():
                    combine(nc, k, a, moe, out)
            return
        store(nc, k, out)


_HOST = {
    "L0_attn_Wq": "wq0", "L0_attn_Wk": "wk0", "L0_attn_Wv": "wv0", "L0_attn_Wo": "wo0",
}


def laid_out(inputs):
    arrays = {}
    for name, x in inputs.items():
        x = np.asarray(x)
        arrays[_HOST.get(name, name)] = np.ascontiguousarray(x.T) if name in _HOST else np.ascontiguousarray(x)
    arrays["L0_ffn_scale"] = arrays["L0_ffn_scale"].reshape(1, 1)
    arrays["consts"], arrays["pe"] = constants()
    return arrays


def kernel(**inputs):
    import concourse.bacc as _bacc
    from concourse.bass_utils import run_bass_kernel_spmd as _run

    nc = _bacc.Bacc("TRN2", target_bir_lowering=False, num_devices=1)
    arrays, a = {}, {}
    for name, x in laid_out(inputs).items():
        arrays[f"in_{name}"] = x
        a[name] = nc.dram_tensor(f"in_{name}", x.shape, mybir.dt.from_np(x.dtype), kind="ExternalInput").ap()
    out = nc.dram_tensor("out_0", (S, D), F32, kind="ExternalOutput").ap()
    program(nc, a, out)
    r = _run(nc, [arrays], core_ids=[0])
    return r.results[0]["out_0"].reshape(1, S, D)
```

```python
import math
from contextlib import ExitStack, contextmanager

import numpy as np
import concourse.bass as bass
from concourse import mybir

F32 = mybir.dt.float32
BF16 = mybir.dt.bfloat16
F32R = mybir.dt.float32r
I32 = mybir.dt.int32
ALU = mybir.AluOpType
ACT = mybir.ActivationFunctionType
AX = mybir.AxisListType

P = 128
S = 2048
D = 192
NT = S // P
KH = D // 2
DB = D - P
QW = 512
NQ = S // QW
TPQ = QW // P
VOCAB = 70

H0 = 12
DK0 = D // H0
HG = 4
NG = H0 // HG
HROW = P // HG
STACK = 6 * DK0
PARTS_Q = (0, 0, 0, 1, 1, 2)
PARTS_K = (0, 1, 2, 0, 1, 0)

NSLOT, PSLOT, HDOWN = 8, 4, 24
NP = NSLOT * PSLOT

H1, D1 = 4, 64
DIM1 = H1 * D1
NPAIR = H1 // 2

E = 8
F = 768
NF = F // P
GRP = 8
SG = S // GRP
CAP = 80
TPG = SG // P
SLOTS = GRP * CAP
EHALF = E * CAP // 2
ST = SLOTS // P
CT = P // GRP

MASKED = -1.0e30
C_ID, C_TRI, C_MQK, C_MKQ, C_ONE = range(0, 5 * P, P)
C_IOTA = C_ONE + P
C_PIDX = C_IOTA + CAP
C_RANK = C_PIDX + 1
C_SEL4 = C_RANK + E
C_CROW = C_SEL4 + HG
C_ALL = C_CROW + ST


def constants():
    p, f = np.arange(P)[:, None], np.arange(P)[None, :]
    c = np.zeros((P, C_ALL), np.float32)
    c[:, C_ID:C_ID + P] = p == f
    c[:, C_TRI:C_TRI + P] = p <= f
    c[:, C_MQK:C_MQK + P] = np.where(f > p, MASKED, 0)
    c[:, C_MKQ:C_MKQ + P] = np.where(p > f, MASKED, 0)
    c[:, C_ONE:C_ONE + P] = 1
    c[:, C_IOTA:C_IOTA + CAP] = np.arange(CAP)
    c[:, C_PIDX] = np.arange(P)
    c[:, C_SEL4:C_SEL4 + HG] = p == HROW * np.arange(HG)[None, :] + DK0
    c[:, C_RANK:C_RANK + E] = np.arange(E, 0, -1)
    slot = np.arange(E * CAP)
    c[:, C_CROW:C_CROW + ST] = (slot % CAP).reshape(ST, P).T
    row = np.arange(4 * E)[:, None]
    mine = row % E == slot[None, :] // CAP
    sel = np.stack([mine & (row < E), mine & (row >= E)], axis=1).astype(np.float32)
    pos = np.arange(S, dtype=np.float32)[:, None]
    even = np.arange(0, D, 2, dtype=np.float32)
    exponent = -(even / np.float32(D)) * np.float32(math.log(10000.0))
    angle = pos * np.exp(exponent.astype(np.float64)).astype(np.float32)
    pe = np.stack([np.sin(angle), np.cos(angle)], axis=-1).reshape(S, D).astype(np.float32)
    return c, pe, sel


class Core:

    def __init__(self, nc, ctx):
        self.nc = nc
        self.ctx = ctx
        self.sems = ctx
        self.h = self.sb("h", [P, NT, D])
        self.cst = self.sb("cst", [P, C_ALL])
        self.identb = self.sb("identb", [P, P], BF16)
        self.mqkb = self.sb("mqkb", [P, P], BF16)
        self.mkqb = self.sb("mkqb", [P, P], BF16)
        self.trib = self.sb("trib", [P, P], BF16)
        self.oneb = self.sb("oneb", [P, P], BF16)
        self.stats = self.sb("stats", [P, NT, 6])
        self.mv = self.sb("mv", [P, NT, 2])
        self.ve = self.sb("ve", [P, NT])
        self.sd = self.sb("sd", [P, NT])
        self.rstd = self.sb("rstd", [P, NT])
        self.spare = self.sb("spare", [P, 1])
        self.stat_made = self.sem("stat_made")
        self.mv_made = self.sem("mv_made")
        self.stat_count = 0
        self.norm_sems = {x: self.sem("norm_" + x) for x in NORM_SEMS}
        self.counted = {x: 0 for x in NORM_SEMS}
        self.PS = ctx.enter_context(nc.psum_tensor("PS", [P, 8, 512], F32))
        self.ident = self.cst[:, C_ID:C_ID + P]
        self.tri = self.cst[:, C_TRI:C_TRI + P]

    def sb(self, name, shape, dt=F32):
        return self.ctx.enter_context(self.nc.sbuf_tensor(name, shape, dt))

    def sem(self, name):
        return self.sems.enter_context(self.nc.semaphore(name))

    def stat(self, dve, t, made, n):
        dve.wait_ge(made, n)
        self.nc.vector.bn_stats(self.stats[:, t, :], self.h[:, t, :]).then_inc(self.stat_made, 1)
        if t:
            self.aggregate(dve, t - 1)

    def aggregate(self, dve, t):
        self.stat_count += 1
        dve.wait_ge(self.stat_made, self.stat_count)
        self.nc.vector.bn_aggr(self.mv[:, t, :], self.stats[:, t, :]).then_inc(self.mv_made, 1)

    def rows(self, layer):
        self.xn = self.sb(f"xn{layer}", [P, NT, D])
        self.xT = self.sb(f"xT{layer}", [P, 2, S], F32R)
        self.xl = self.sb(f"xl{layer}", [P, S], F32R)

    @contextmanager
    def room(self):
        outer = self.ctx
        with ExitStack() as self.ctx:
            yield
        self.ctx = outer


class Loads:

    def __init__(self, nc, landed, pairs):
        self.nc, self.landed, self.pairs = nc, landed, pairs
        self.all = 16 * len(pairs)

    def load(self, eng):
        with self.nc.allow_non_contiguous_dma(reason="small weights, turned"):
            for dst, src in self.pairs:
                eng.dma_start(dst, src).then_inc(self.landed, 16)

    def wait(self, eng):
        eng.wait_ge(self.landed, self.all)


class Weights:

    def __init__(self, nc, k, name, src):
        n = src.shape[1]
        self.nc, self.src = nc, src
        self.raw = k.sb(name, [P, 2, n])
        self.high = k.sb(name + "_high", [P, 2, n], F32R)
        self.low = k.sb(name + "_low", [P, 2, n], F32R)
        self.landed = k.sem(name + "_landed")
        self.parts = k.sem(name + "_parts")

    def load(self, eng):
        for rows, at, where in ((slice(0, P), 0, slice(0, P)), (slice(P, D), 1, slice(0, DB)), (slice(P, D), 1, slice(DB, P))):
            eng.dma_start(self.raw[where, at, :], self.src[rows, :]).then_inc(self.landed, 16)

    def split(self, pool):
        pool.wait_ge(self.landed, 48)
        self.nc.gpsimd.tensor_copy(self.high[:, :, :], self.raw[:, :, :]).then_inc(self.parts, 1)
        pool.wait_ge(self.parts, 1)
        self.nc.gpsimd.tensor_tensor(self.low[:, :, :], self.raw[:, :, :], self.high[:, :, :].bitcast(F32),
                                     ALU.subtract).then_inc(self.parts, 1)


def part_pairs(high, low, cols, xT, xl, rows):
    return [(high[:, 0, cols], xT[:, 0, rows]), (high[:, 0, cols], xl[:, rows]), (low[:, 0, cols], xT[:, 0, rows]),
            (high[:, 1, cols], xT[:, 1, rows]), (low[0:DB, 1, cols], xT[0:DB, 1, rows])]


def product_wx(nc, out, high, low, cols, xT, xl, rows):
    pairs = part_pairs(high, low, cols, xT, xl, rows)
    for i, (w, x) in enumerate(pairs):
        last = nc.tensor.matmul(out, w, x, start=i == 0, stop=i == len(pairs) - 1)
    return last


def product_xw(nc, out, high, low, cols, xT, xl, rows):
    pairs = part_pairs(high, low, cols, xT, xl, rows)
    for i, (w, x) in enumerate(pairs):
        last = nc.tensor.matmul(out, x, w, start=i == 0, stop=i == len(pairs) - 1)
    return last


def embed(nc, k, a, att, loads):
    tok = k.sb("tok", [VOCAB, S], I32)
    onehot = k.sb("onehot", [VOCAB, S])
    table = k.sb("table", [VOCAB, D])
    pe = k.xn
    landed = k.sem("emb_landed")
    table_landed = k.sem("table_landed")
    pe_landed = [k.sem(f"pe_landed{c}") for c in range(NQ)]
    onehot_made = k.sem("onehot_made")
    rows_made = k.sem("rows_made")
    h_made = k.sem("h_made")
    base = D // 3
    with nc.Block() as block:
        @block.sync
        def _(sp):
            sp.dma_start(tok[:, :], a["x"].to_broadcast([VOCAB, S])).then_inc(landed, 16)
            sp.dma_start(k.cst[:, :], a["consts"]).then_inc(landed, 16)
            sp.wait_ge(landed, 16 * 2)
            for x in loads:
                x.load(sp)

        @block.gpsimd
        def _(pool):
            nc.gpsimd.memset(att["ks"][STACK:STACK + 3, :, :, :], 1.0)

        @block.scalar
        def _(act):
            act.dma_start(table[0:64, 0:base], a["L0_tok_color_W"].unsqueeze(1).to_broadcast([4, 16, base])).then_inc(table_landed, 16)
            for c in range(4):
                act.dma_start(table[16 * c:16 * c + 16, base:2 * base],
                              a["L0_tok_shape_W"].unsqueeze(1).to_broadcast([4, 4, base])).then_inc(table_landed, 16)
            act.dma_start(table[0:64, 2 * base:D], a["L0_tok_quantity_W"].unsqueeze(0).to_broadcast([16, 4, base])).then_inc(table_landed, 16)
            act.dma_start(table[64:VOCAB, :], a["L0_tok_special_W"]).then_inc(table_landed, 16)
            for c in range(NQ):
                tiles = slice(c * TPQ, (c + 1) * TPQ)
                act.dma_start(pe[:, tiles, :], a["pe"].rearrange("(t p) d -> p t d", p=P)[:, tiles, :]).then_inc(pe_landed[c], 16)

        @block.vector
        def _(dve):
            dve.wait_ge(landed, 16 * 2)
            for c in range(NQ):
                cols = slice(c * QW, (c + 1) * QW)
                nc.vector.tensor_scalar(onehot[:, cols], tok[:, cols], float(VOCAB - 1), k.cst[0:VOCAB, C_PIDX:C_PIDX + 1],
                                        ALU.min, ALU.is_equal).then_inc(onehot_made, 1)
            for dst, c in ((k.identb, C_ID), (k.mqkb, C_MQK), (k.mkqb, C_MKQ), (k.trib, C_TRI), (k.oneb, C_ONE)):
                nc.vector.tensor_copy(dst[:, :], k.cst[:, c:c + P])
            for t in range(NT):
                if t % TPQ == 0:
                    dve.wait_ge(pe_landed[t // TPQ], 16)
                dve.wait_ge(rows_made, t + 1)
                nc.vector.scalar_tensor_tensor(k.h[:, t, :], k.PS[:, t % 8, 0:D], math.sqrt(D),
                                               pe[:, t, :], ALU.mult, ALU.add).then_inc(h_made, 1)
                if t >= 1:
                    k.stat(dve, t - 1, h_made, t)
            k.stat(dve, NT - 1, h_made, NT)

        @block.tensor
        def _(te):
            te.wait_ge(table_landed, 16 * 7)
            for t in range(NT):
                te.wait_ge(onehot_made, t // TPQ + 1)
                if t >= 8:
                    te.wait_ge(h_made, t - 7)
                nc.tensor.matmul(k.PS[:, t % 8, 0:D], onehot[:, t * P:(t + 1) * P], table[:, :],
                                 start=True, stop=True).then_inc(rows_made, 1)


NORM_SEMS = ("small", "rooted", "xn_made", "late_made", "turned", "high_made")
LATE = 2


def layernorm(nc, k, loads=(), splits=(), slots=None, l2=False):
    small, rooted, xn_made, late_made, turned, high_made = (k.norm_sems[x] for x in NORM_SEMS)
    SMALL, ROOTED = 7 if l2 else 2, 2 if l2 else 1

    def at(sem, n):
        return k.counted[sem] + n

    with nc.Block() as block:
        @block.sync
        def _(sp):
            for x in loads:
                x.load(sp)

        @block.gpsimd
        def _(pool):
            pool.wait_ge(small, at("small", SMALL))
            for t in range(NT - LATE, NT):
                nc.gpsimd.tensor_scalar(k.xn[:, t, :], k.h[:, t, :], k.mv[:, t, 0:1], k.rstd[:, t:t + 1],
                                        ALU.subtract, ALU.mult).then_inc(late_made, 1)
            for x in splits:
                x.split(pool)

        @block.vector
        def _(dve):
            if slots:
                slots.square(dve)
            k.aggregate(dve, NT - 1)
            dve.wait_ge(k.mv_made, k.stat_count)
            nc.vector.tensor_scalar(k.ve[:, :], k.mv[:, :, 1], 1e-5, None, ALU.add).then_inc(small, 1)
            dve.wait_ge(rooted, at("rooted", 1))
            nc.vector.reciprocal(k.rstd[:, :], k.sd[:, :]).then_inc(small, 1)
            dve.wait_ge(small, at("small", 2))
            if l2:
                nc.vector.scalar_tensor_tensor(k.ve[:, :], k.mv[:, :, 1], float(D), k.rstd[:, :], ALU.mult, ALU.mult).then_inc(small, 1)
                dve.wait_ge(small, at("small", 3))
                nc.vector.tensor_tensor(k.ve[:, :], k.ve[:, :], k.rstd[:, :], ALU.mult).then_inc(small, 1)
                if slots:
                    slots.divide(dve)
                dve.wait_ge(rooted, at("rooted", 2))
                nc.vector.tensor_scalar(k.ve[:, :], k.sd[:, :], 1e-6, None, ALU.add).then_inc(small, 1)
                dve.wait_ge(small, at("small", 5))
                nc.vector.reciprocal(k.sd[:, :], k.ve[:, :]).then_inc(small, 1)
                dve.wait_ge(small, at("small", 6))
                nc.vector.tensor_tensor(k.rstd[:, :], k.rstd[:, :], k.sd[:, :], ALU.mult).then_inc(small, 1)
                dve.wait_ge(small, at("small", 7))
            for t in range(NT - LATE):
                nc.vector.tensor_scalar(k.xn[:, t, :], k.h[:, t, :], k.mv[:, t, 0:1], k.rstd[:, t:t + 1],
                                        ALU.subtract, ALU.mult).then_inc(xn_made, 1)
            for u in range(NT // 2):
                cols = slice(2 * u * P, 2 * (u + 1) * P)
                dve.wait_ge(high_made, at("high_made", u + 1))
                nc.vector.tensor_tensor(k.xl[:, cols], k.PS[:, u, 0:2 * P], k.xT[:, 0, cols].bitcast(F32), ALU.subtract)
                nc.vector.tensor_tensor(k.xT[DB:P, 1, cols], k.PS[DB:P, u, 2 * P:4 * P], k.xT[DB:P, 1, cols].bitcast(F32), ALU.subtract)

        @block.scalar
        def _(act):
            nc.scalar.activation(k.spare[:, :], k.cst[:, C_ONE:C_ONE + 1], ACT.Sqrt)
            act.wait_ge(small, at("small", 1))
            nc.scalar.activation(k.sd[:, :], k.ve[:, :], ACT.Sqrt).then_inc(rooted, 1)
            if slots:
                slots.root(act)
            if l2:
                act.wait_ge(small, at("small", 4))
                nc.scalar.activation(k.sd[:, :], k.ve[:, :], ACT.Sqrt).then_inc(rooted, 1)
            for u in range(NT // 2):
                act.wait_ge(turned, at("turned", u + 1))
                nc.scalar.activation(k.xT[:, :, 2 * u * P:2 * (u + 1) * P],
                                     k.PS[:, u, :].rearrange("p (k n) -> p k n", k=2), ACT.Copy).then_inc(high_made, 1)

        @block.tensor
        def _(te):
            for u in range(NT // 2):
                if 2 * u < NT - LATE:
                    te.wait_ge(xn_made, at("xn_made", 2 * u + 2))
                else:
                    te.wait_ge(late_made, at("late_made", 2 * u + 2 - (NT - LATE)))
                for i in range(2):
                    nc.tensor.transpose(k.PS[:, u, i * P:(i + 1) * P], k.xn[:, 2 * u + i, 0:P], k.ident)
                    for copy in range(2):
                        last = nc.tensor.matmul(k.PS[copy * DB:(copy + 1) * DB, u, (2 + i) * P:(3 + i) * P],
                                                k.xn[:, 2 * u + i, P:D], k.ident, start=True, stop=True,
                                                tile_position=(0, copy * DB))
                last.then_inc(turned, 1)
    for sem, n in zip(NORM_SEMS, (SMALL, ROOTED, NT - LATE, LATE, NT // 2, NT // 2)):
        k.counted[sem] += n


UNITS = 2 * 2 * NQ


def softmax_qkv(nc, k, w, att):
    RING = len(att["stored"])
    parts = k.sb("parts", [KH, RING, 3, QW], BF16)
    rest = k.sb("rest", [KH, 2, QW])
    made = k.sem("qkv_made")
    part1 = k.sem("part1_made")
    rest1 = k.sem("rest1_made")
    part2 = k.sem("part2_made")
    part3 = k.sem("part3_made")
    v_made = k.sem("v_made")
    v_kept = k.sem("v_kept")
    cleared = k.sem("cleared")
    stored = att["stored"]
    units = [(m, mt, c) for mt in range(2) for m in range(2) for c in range(NQ)]
    NU = len(units)
    assert NU == UNITS
    QK_BANKS, V_BANKS = 5, 3
    LOAD_FROM = NU // 2 + 2
    assert NU == NT
    scale = (DK0 ** -0.5, 1.0)
    with nc.Block() as block:
        @block.sync
        def _(sp):
            for n, (m, mt, c) in enumerate(units):
                sp.wait_ge(part3, n + 1)
                sp.dma_start(att["scratch"][m, :, mt * KH:(mt + 1) * KH, c * QW:(c + 1) * QW].rearrange("g r n -> r g n"),
                             parts[:, n % RING, :, :]).then_inc(stored[n % RING], 16)
                if n >= LOAD_FROM and n - LOAD_FROM < HG:
                    if n == LOAD_FROM:
                        for i in range(RING):
                            sp.wait_ge(stored[i], 16 * (NU // 2 // RING))
                    load_max(sp, att, 0, 0, [n - LOAD_FROM])

        @block.gpsimd
        def _(pool):
            nc.gpsimd.memset(att["v"][:, :, :, DK0:HROW], 0.0).then_inc(cleared, 1)
            pool.wait_ge(cleared, 1)
            nc.gpsimd.memset(att["v"][:, :, :, DK0:DK0 + 1], 1.0).then_inc(cleared, 1)
            pool.wait_ge(cleared, 2)
            nc.gpsimd.memset(att["wo"][:, :, :], 0.0)
            for i in range(RING):
                pool.wait_ge(stored[i], 16 * (NU // 2 // RING))
            load_max(pool, att, 1, 0)

        @block.tensor
        def _(te):
            for m in range(3):
                te.wait_ge(w[m].parts, 2)
            for n, (m, mt, c) in enumerate(units):
                if n >= QK_BANKS:
                    te.wait_ge(rest1, n - QK_BANKS + 1)
                product_wx(nc, k.PS[0:KH, n % QK_BANKS, :], w[m].high, w[m].low, slice(mt * KH, (mt + 1) * KH),
                           k.xT, k.xl, slice(c * QW, (c + 1) * QW)).then_inc(made, 1)
                t = n
                if t >= V_BANKS:
                    te.wait_ge(v_kept, t - V_BANKS + 1)
                product_xw(nc, k.PS[:, QK_BANKS + t % V_BANKS, 0:D], w[2].high, w[2].low, slice(0, D),
                           k.xT, k.xl, slice(t * P, (t + 1) * P)).then_inc(v_made, 1)

        @block.scalar
        def _(act):
            def second(n):
                act.wait_ge(rest1, n + 1)
                nc.scalar.activation(parts[:, n % RING, 1, :], rest[:, n % 2, :], ACT.Copy).then_inc(part2, 1)

            for n, (m, mt, c) in enumerate(units):
                act.wait_ge(made, n + 1)
                if n >= RING:
                    act.wait_ge(stored[n % RING], 16 * (n // RING))
                nc.scalar.activation(parts[:, n % RING, 0, :], k.PS[0:KH, n % QK_BANKS, :], ACT.Copy, scale=scale[m]).then_inc(part1, 1)
                if n >= 1:
                    second(n - 1)
                t = n
                act.wait_ge(v_made, t + 1)
                nc.scalar.activation(att["v"][:, t, :, 0:DK0], k.PS[:, QK_BANKS + t % V_BANKS, 0:D].rearrange("p (h d) -> p h d", d=DK0),
                                     ACT.Copy).then_inc(v_kept, 1)
            second(NU - 1)

        @block.vector
        def _(dve):
            def third(n):
                dve.wait_ge(part2, n + 1)
                nc.vector.tensor_tensor(parts[:, n % RING, 2, :], rest[:, n % 2, :], parts[:, n % RING, 1, :],
                                        ALU.subtract).then_inc(part3, 1)

            for n, (m, mt, c) in enumerate(units):
                dve.wait_ge(part1, n + 1)
                if n >= 2:
                    dve.wait_ge(part3, n - 1)
                nc.vector.scalar_tensor_tensor(rest[:, n % 2, :], k.PS[0:KH, n % QK_BANKS, :], scale[m], parts[:, n % RING, 0, :],
                                               ALU.mult, ALU.subtract).then_inc(rest1, 1)
                if n >= 1:
                    third(n - 1)
            third(NU - 1)


def load_max(eng, att, m, g, heads=range(HG)):
    stack, lot = (att["qm"], MPARTS_Q) if m == 0 else (att["km"], MPARTS_K)
    for j in heads:
        r = (g * HG + j) * DK0
        for at in (0, 2):
            src = att["scratch"][m, lot[at]:lot[at + 1] + 1, r:r + DK0, :]
            if m == 0:
                src = src.to_broadcast([2, DK0, S])
            row = (j % 2) * MSTACK + at * DK0
            eng.dma_start(stack[row:row + 2 * DK0, g % 2, j // 2, :], src).then_inc(att["m_loaded"][m][g], 16)


def load_scores(eng, att, m, g):
    stack, lot = (att["qs"], PARTS_Q) if m == 0 else (att["ks"], PARTS_K)
    for at, part in enumerate(lot):
        src = att["scratch"][m, part, g * HG * DK0:(g + 1) * HG * DK0, :]
        eng.dma_start(stack[at * DK0:(at + 1) * DK0, g % 2, :, :], src.rearrange("(j d) n -> d j n", d=DK0)).then_inc(att["s_loaded"][m][g], 16)


SLOADS, MLOADS = 16 * 6, 16 * 2 * HG


STEPS = [(0, c) for c in range(NQ)] + [(1, c) for c in range(NQ)] + [(2, c) for c in reversed(range(NQ))]
MAX_RANK, VALUES_RANK = 1.5, 2.5
STACKS_IN = 27000
MAXIMA_IN = 20000
PROBS = 2
HOP = 120
MAX_SLOTS, S_BANKS = 2, 3
B_MAX, B_SC, B_PV = 0, 4, 7
MSTACK = 4 * DK0
MPARTS_Q, MPARTS_K = (0, 0, 1, 1), (0, 1, 0, 1)


def max_units(step):
    g, c = STEPS[step]
    return [(qt, pair, kc) for qt in range(TPQ * c, TPQ * (c + 1)) for pair in range(HG // 2) for kc in range(c + 1)]


def max_width(step, unit):
    qt, _, kc = unit
    return (qt % TPQ + 1) * P if kc == STEPS[step][1] else QW


def key_tiles(step):
    return TPQ * (STEPS[step][1] + 1)


def live(step, kt):
    return max(0, kt - TPQ * STEPS[step][1]) * P


def attention_order():
    NS = len(STEPS)
    maxq = [("max", s, u) for s in range(NS) for u in max_units(s)]
    scoreq = [("score", s, (kt, j)) for s in range(NS) for kt in range(key_tiles(s)) for j in range(HG)]
    left = [len(max_units(s)) for s in range(NS)]
    pe = dve = act = 0.0
    slot_free, bank_free = [0.0] * MAX_SLOTS, [0.0] * S_BANKS
    placed = [None] * NS
    maxed, finished = [None] * NS, [None] * NS
    small, values = [], []
    order = []
    slots = scores = 0
    pv_free = 0.0

    def may_turn(s):
        g = STEPS[s][0]
        return g < 2 or finished[NQ * (g - 1) - 1] is not None

    while maxq or scoreq or small or values:
        options = []
        if values:
            options.append((max(values[0][0], pv_free if values[0][1][2] == 0 else 0), VALUES_RANK, "values"))
        turnable = [x for x in small if x[1][0] != "turn" or may_turn(x[1][1])]
        if turnable:
            options.append((max(turnable[0][0], slot_free[slots % MAX_SLOTS]), 1, "small"))
        if scoreq and placed[scoreq[0][1]] is not None and len(values) < PROBS:
            options.append((max(placed[scoreq[0][1]], STACKS_IN, bank_free[scores % S_BANKS]), 2, "score"))
        if maxq:
            s = maxq[0][1]
            ready = slot_free[slots % MAX_SLOTS]
            g = STEPS[s][0]
            if g == 1:
                ready = max(ready, MAXIMA_IN)
            if g >= 2:
                done = maxed[NQ * (g - 1) - 1]
                ready = None if done is None else max(ready, done + 12000)
            if ready is not None and (s < 2 or placed[s - 2] is not None):
                options.append((ready, MAX_RANK, "max"))
        when, _, kind = min((max(pe, o[0]), o[1], o[2]) for o in options)
        pe = when
        if kind == "values":
            item = values.pop(0)[1]
            _, s, kt = item
            pe += 1.75 * (QW - live(s, kt))
            if kt == key_tiles(s) - 1:
                act = max(act, pe + HOP) + 480
                pv_free = act + HOP
                finished[s] = act
                small.append((act + HOP, ("den", s, None)))
        elif kind == "small":
            small.remove(turnable[0])
            item = turnable[0][1]
            pe += {"turn": 60, "den": 430, "inv": 860}[item[0]]
            dve = max(dve, pe + HOP) + {"turn": 250, "den": 150, "inv": 620}[item[0]]
            slot_free[slots % MAX_SLOTS] = dve + HOP
            slots += 1
            if item[0] == "turn":
                placed[item[1]] = dve + 3500
            if item[0] == "den":
                small.append((dve + HOP, ("inv", item[1], None)))
        elif kind == "score":
            item = scoreq.pop(0)
            _, s, (kt, j) = item
            w = QW - live(s, kt)
            pe += w / 2.4 + 60 * (kt >= TPQ * STEPS[s][1])
            act = max(act, pe + HOP) + 50 + w / 1.2
            bank_free[scores % S_BANKS] = act + HOP
            scores += 1
            if j == HG - 1:
                values.append((act + HOP, ("values", s, kt)))
        else:
            item = maxq.pop(0)
            _, s, u = item
            w = max_width(s, u)
            pe += 2 * w / 2.4 + 110 * (u[2] == STEPS[s][1])
            dve = max(dve, pe + HOP) + 65 + 2 * w / 0.96
            slot_free[slots % MAX_SLOTS] = dve + HOP
            slots += 1
            left[s] -= 1
            if not left[s]:
                dve += 900
                maxed[s] = dve
                small.append((dve + HOP, ("turn", s, None)))
        order.append(item)
    return order


def softmax_attention(nc, k, a, att):
    qs, ks, qm, km, v, o = (att[x] for x in ("qs", "ks", "qm", "km", "v", "o"))
    NS = len(STEPS)
    pmax = k.sb("pmax", [P, 2, TPQ, HG, NQ])
    negm = k.sb("negm", [P, 2, HG, TPQ])
    negr = k.sb("negr", [P, 2, HG, TPQ])
    mparts = k.sb("mparts", [P, 2, HG, 3, TPQ], BF16)
    mT = k.sb("mT", [HG * 3 * TPQ, 2, P], BF16)
    probs = k.sb("probs", [P, PROBS, HG, QW])
    inv = k.sb("inv", [P, TPQ, HG])
    invw = k.sb("invw", [P, TPQ, HG, HROW])
    m_loaded, s_loaded = att["m_loaded"], att["s_loaded"]
    slot_made = k.sem("slot_made")
    slot_read = k.sem("slot_read")
    m_chain = k.sem("m_chain")
    m_placed = [k.sem(f"m_placed{i}") for i in range(2)]
    scored = k.sem("scored")
    exped = k.sem("exped")
    summed = k.sem("summed")
    o_kept = k.sem("o_kept")
    inv_wide = k.sem("inv_wide")
    order = attention_order()
    slot_order = [x for x in order if x[0] in ("max", "turn", "den", "inv")]
    slots_to_max = [0] * NS
    slots_to_turn = [0] * NS
    for i, (what, s, _) in enumerate(slot_order):
        if what == "max":
            slots_to_max[s] = i + 1
        if what == "turn":
            slots_to_turn[s] = i + 1
    nkey = [0]
    for s in range(NS):
        nkey.append(nkey[-1] + key_tiles(s))
    CHAIN = 5

    with nc.Block() as block:
        @block.sync
        def _(sp):
            load_scores(sp, att, 0, 0)
            att["wo_loads"].load(sp)
            for s, (g, c) in enumerate(STEPS):
                sp.wait_ge(slot_read, slots_to_turn[s])
                if g >= 2 and c == STEPS[NQ * g][1]:
                    sp.wait_ge(scored, HG * nkey[NQ * (g - 1)])
                for j in range(HG):
                    sp.dma_start(qs[STACK:STACK + 3, g % 2, j, c * QW:(c + 1) * QW].rearrange("r (t n) -> r t n", n=P),
                                 mT[j * 3 * TPQ:(j + 1) * 3 * TPQ, s % 2, :]).then_inc(m_placed[s % 2], 16)

        @block.gpsimd
        def _(pool):
            for stored in att["stored"]:
                pool.wait_ge(stored, 16 * UNITS // len(att["stored"]))
            for m in range(2):
                load_max(pool, att, m, 1)
            for m in range(2):
                load_scores(pool, att, m, 1)
            pool.wait_ge(slot_read, slots_to_max[NQ - 1])
            for m in range(2):
                load_max(pool, att, m, 2)
            pool.wait_ge(scored, HG * nkey[NQ])
            for m in range(2):
                load_scores(pool, att, m, 2)

        @block.tensor
        def _(te):
            slot = score = 0
            for what, s, arg in order:
                g, c = STEPS[s]
                b = g % 2
                if what in ("max", "turn", "den", "inv"):
                    bank = B_MAX + 2 * (slot % MAX_SLOTS)
                    if slot >= MAX_SLOTS:
                        te.wait_ge(slot_read, slot - MAX_SLOTS + 1)
                    slot += 1
                if what == "max":
                    qt, pair, kc = arg
                    if arg == max_units(s)[0] and s % NQ == 0:
                        for m in range(2):
                            te.wait_ge(m_loaded[m][g], MLOADS)
                    w = max_width(s, arg)
                    diagonal = kc == c
                    for i in range(2):
                        rows = slice(MSTACK * i, MSTACK * (i + 1))
                        mm = nc.tensor.matmul(k.PS[:, bank + i, 0:w], qm[rows, b, pair, qt * P:(qt + 1) * P],
                                              km[rows, b, pair, kc * QW:kc * QW + w], start=True, stop=not diagonal)
                    if diagonal:
                        for i in range(2):
                            mm = nc.tensor.matmul(k.PS[:, bank + i, w - P:w], k.identb[:, :], k.mqkb[:, :], start=False, stop=True)
                    mm.then_inc(slot_made, 1)
                elif what == "turn":
                    te.wait_ge(m_chain, CHAIN * (s + 1))
                    nc.tensor.transpose(k.PS[:, bank, :].bitcast(BF16)[0:HG * 3 * TPQ, 0:P],
                                        mparts[:, s % 2].rearrange("p j r t -> p (j r t)"), k.identb[:, :]).then_inc(slot_made, 1)
                elif what == "score":
                    kt, j = arg
                    if arg == (0, 0):
                        if s % NQ == 0:
                            for m in range(2):
                                te.wait_ge(s_loaded[m][g], SLOADS)
                        te.wait_ge(m_placed[s % 2], 16 * HG * (s // 2 + 1))
                    if score >= S_BANKS:
                        te.wait_ge(exped, score - S_BANKS + 1)
                    off = live(s, kt)
                    diagonal = kt >= TPQ * c
                    bank = B_SC + score % S_BANKS
                    score += 1
                    mm = nc.tensor.matmul(k.PS[:, bank, off:QW], ks[0:STACK + 3, b, j, kt * P:(kt + 1) * P],
                                          qs[0:STACK + 3, b, j, c * QW + off:(c + 1) * QW], start=True, stop=not diagonal)
                    if diagonal:
                        mm = nc.tensor.matmul(k.PS[:, bank, off:off + P], k.identb[:, :], k.mkqb[:, :], start=False, stop=True)
                    mm.then_inc(scored, 1)
                elif what == "values":
                    n = nkey[s] + arg
                    te.wait_ge(exped, HG * (n + 1))
                    if arg == 0 and s:
                        te.wait_ge(o_kept, s)
                    off = live(s, arg)
                    for j in range(HG):
                        mm = nc.tensor.matmul(k.PS[HROW * j:HROW * (j + 1), B_PV, off:QW], v[:, arg, g * HG + j, :],
                                              probs[:, n % PROBS, j, off:QW], start=arg == 0, stop=arg == key_tiles(s) - 1,
                                              tile_position=(0, HROW * j))
                    mm.then_inc(summed, 1)
                elif what == "den":
                    te.wait_ge(o_kept, s + 1)
                    for i in range(TPQ):
                        mm = nc.tensor.matmul(k.PS[:, bank, i * HG:(i + 1) * HG], o[:, g, c * QW + i * P:c * QW + (i + 1) * P],
                                              k.cst[:, C_SEL4:C_SEL4 + HG], start=True, stop=True)
                    mm.then_inc(slot_made, 1)
                else:
                    te.wait_ge(inv_wide, s + 1)
                    for i in range(TPQ):
                        mm = nc.tensor.matmul(k.PS[:, bank, i * P:(i + 1) * P], invw[:, i].rearrange("p j r -> p (j r)"),
                                              k.ident, start=True, stop=True)
                    mm.then_inc(slot_made, 1)

        @block.vector
        def _(dve):
            for slot, (what, s, arg) in enumerate(slot_order):
                g, c = STEPS[s]
                bank = B_MAX + 2 * (slot % MAX_SLOTS)
                dve.wait_ge(slot_made, slot + 1)
                if what == "max":
                    qt, pair, kc = arg
                    w = max_width(s, arg)
                    nc.vector.tensor_reduce(pmax[:, s % 2, qt % TPQ, 2 * pair:2 * pair + 2, kc], k.PS[:, bank:bank + 2, 0:w],
                                            AX.X, ALU.max).then_inc(slot_read, 1)
                    if slot + 1 == slots_to_max[s]:
                        at = CHAIN * s
                        mp = mparts[:, s % 2]
                        dve.wait_ge(slot_read, slot + 1)
                        nc.vector.tensor_reduce(negm[:, s % 2].rearrange("p j t -> p t j"), pmax[:, s % 2, :, :, 0:c + 1],
                                                AX.X, ALU.max, negate=True).then_inc(m_chain, 1)
                        dve.wait_ge(m_chain, at + 1)
                        nc.vector.tensor_copy(mp[:, :, 0, :], negm[:, s % 2]).then_inc(m_chain, 1)
                        dve.wait_ge(m_chain, at + 2)
                        nc.vector.tensor_tensor(negr[:, s % 2], negm[:, s % 2], mp[:, :, 0, :], ALU.subtract).then_inc(m_chain, 1)
                        dve.wait_ge(m_chain, at + 3)
                        nc.vector.tensor_copy(mp[:, :, 1, :], negr[:, s % 2]).then_inc(m_chain, 1)
                        dve.wait_ge(m_chain, at + 4)
                        nc.vector.tensor_tensor(mp[:, :, 2, :], negr[:, s % 2], mp[:, :, 1, :], ALU.subtract).then_inc(m_chain, 1)
                elif what == "turn":
                    if s >= 2:
                        dve.wait_ge(m_placed[s % 2], 16 * HG * (s // 2))
                    nc.vector.tensor_copy(mT[:, s % 2, :], k.PS[:, bank, :].bitcast(BF16)[0:HG * 3 * TPQ, 0:P]).then_inc(slot_read, 1)
                elif what == "den":
                    nc.vector.reciprocal(inv[:, :, :].rearrange("p i j -> p (i j)"), k.PS[:, bank, 0:TPQ * HG]).then_inc(slot_read, 1)
                    dve.wait_ge(slot_read, slot + 1)
                    nc.vector.tensor_copy(invw[:, :, :, :].rearrange("p i j r -> p (i j) r"),
                                          inv[:, :, :].rearrange("p i j -> p (i j)").unsqueeze(2).to_broadcast([P, TPQ * HG, HROW])).then_inc(inv_wide, 1)
                else:
                    part = o[:, g, c * QW:(c + 1) * QW]
                    nc.vector.tensor_tensor(part, part, k.PS[:, bank, :], ALU.mult).then_inc(slot_read, 1)

        @block.scalar
        def _(act):
            load_scores(act, att, 1, 0)
            i = 0
            for what, s, arg in order:
                g, c = STEPS[s]
                if what == "score":
                    kt, j = arg
                    n = nkey[s] + kt
                    off = live(s, kt)
                    if j == 0 and n >= PROBS:
                        act.wait_ge(summed, n - PROBS + 1)
                    act.wait_ge(scored, i + 1)
                    nc.scalar.activation(probs[:, n % PROBS, j, off:QW], k.PS[:, B_SC + i % S_BANKS, off:QW],
                                         ACT.Exp).then_inc(exped, 1)
                    i += 1
                elif what == "values" and arg == key_tiles(s) - 1:
                    act.wait_ge(summed, nkey[s + 1])
                    nc.scalar.activation(o[:, g, c * QW:(c + 1) * QW], k.PS[:, B_PV, :], ACT.Copy).then_inc(o_kept, 1)


def softmax_out(nc, k, att, loads):
    made = k.sem("out0_made")
    added = k.sem("out0_added")
    with nc.Block() as block:
        @block.sync
        def _(sp):
            for x in loads:
                x.load(sp)

        @block.tensor
        def _(te):
            att["wo_loads"].wait(te)
            for t in range(NT):
                if t >= 8:
                    te.wait_ge(added, t - 7)
                for g in range(NG):
                    last = nc.tensor.matmul(k.PS[:, t % 8, 0:D], att["o"][:, g, t * P:(t + 1) * P], att["wo"][:, g, :],
                                            start=g == 0, stop=g == NG - 1)
                last.then_inc(made, 1)

        @block.vector
        def _(dve):
            for t in range(NT):
                dve.wait_ge(made, t + 1)
                nc.vector.tensor_tensor(k.h[:, t, :], k.PS[:, t % 8, 0:D], k.h[:, t, :], ALU.add).then_inc(added, 1)
                if t >= 1:
                    k.stat(dve, t - 1, added, t)
            k.stat(dve, NT - 1, added, NT)


def mlp_weights(k, a):
    wd = k.sb("w_down", [KH, 2, NSLOT, HDOWN])
    wu = k.sb("w_up", [HDOWN, NSLOT, D])
    bd = k.sb("b_down", [HDOWN, NSLOT])
    bu = k.sb("b_up", [KH, 2, NSLOT])
    pairs = [(wd[:, half, :, :], a["L0_ffn_W_down"][:, half * KH:(half + 1) * KH, :].rearrange("n p h -> p n h")) for half in range(2)]
    pairs.append((wu[:, :, :], a["L0_ffn_W_up"].rearrange("n h d -> h n d")))
    pairs.append((bd[:, :], a["L0_ffn_b_down"].rearrange("n h -> h n")))
    pairs += [(bu[:, half, :], a["L0_ffn_b_up"][:, half * KH:(half + 1) * KH].rearrange("n p -> p n")) for half in range(2)]
    return {"wd": wd, "wu": wu, "bd": bd, "bu": bu, "loads": Loads(k.nc, k.sem("ffn0_landed"), pairs)}


class Slots:

    def __init__(self, nc, k, a):
        self.nc, self.a = nc, a
        self.w = k.sb("slots", [P, 2, NSLOT, PSLOT])
        self.sq = k.sb("slots_sq", [P, 2, NSLOT, PSLOT])
        self.high, self.low = (k.sb(f"slots_{x}", [P, 2, NP], F32R) for x in ("high", "low"))
        self.f = k.sb("slots_f", [P, 2, PSLOT])
        self.g = k.sb("slots_g", [P, 2, PSLOT])
        self.scale = k.sb("slots_scale", [P, 1])
        self.landed = k.sem("slots_landed")
        self.steps = k.sem("slots_steps")
        self.rooted = k.sem("slots_rooted")

    def load(self, eng):
        for rows, at, where in ((slice(0, P), 0, slice(0, P)), (slice(P, D), 1, slice(0, DB)), (slice(P, D), 1, slice(DB, P))):
            eng.dma_start(self.w[where, at], self.a["L0_ffn_slot_params"][rows]).then_inc(self.landed, 16)
        eng.dma_start(self.scale[:, :], self.a["L0_ffn_scale"].to_broadcast([P, 1])).then_inc(self.landed, 16)

    def square(self, dve):
        v = self.nc.vector
        dve.wait_ge(self.landed, 64)
        v.tensor_tensor(self.sq[:, :, :, :], self.w[:, :, :, :], self.w[:, :, :, :], ALU.mult).then_inc(self.steps, 1)
        dve.wait_ge(self.steps, 1)
        v.tensor_reduce(self.f[:, :, :], self.sq[:, :, :, :].rearrange("p k n s -> p k s n"), AX.X, ALU.add).then_inc(self.steps, 1)

    def root(self, act):
        act.wait_ge(self.steps, 2)
        self.nc.scalar.activation(self.g[:, :, :], self.f[:, :, :], ACT.Sqrt).then_inc(self.rooted, 1)

    def divide(self, dve):
        v = self.nc.vector
        dve.wait_ge(self.rooted, 1)
        v.tensor_scalar(self.f[:, :, :], self.g[:, :, :], 1e-6, None, ALU.add).then_inc(self.steps, 1)
        dve.wait_ge(self.steps, 3)
        v.reciprocal(self.g[:, :, :], self.f[:, :, :]).then_inc(self.steps, 1)
        dve.wait_ge(self.steps, 4)
        v.tensor_scalar(self.f[:, :, :], self.g[:, :, :], self.scale[:, 0:1], None, ALU.mult).then_inc(self.steps, 1)
        dve.wait_ge(self.steps, 5)
        for at in range(2):
            last = v.tensor_tensor(self.sq[:, at], self.w[:, at], self.f[:, at:at + 1, :].to_broadcast([P, NSLOT, PSLOT]), ALU.mult)
        last.then_inc(self.steps, 1)
        made = self.sq[:, :, :, :].rearrange("p k n s -> p k (n s)")
        dve.wait_ge(self.steps, 6)
        v.tensor_copy(self.high[:, :, :], made).then_inc(self.steps, 1)
        dve.wait_ge(self.steps, 7)
        v.tensor_tensor(self.low[:, :, :], made, self.high[:, :, :].bitcast(F32), ALU.subtract).then_inc(self.steps, 1)


def slot_mixture(nc, k, slots, mlp, splits):
    B_TOK, B_D, B_X, B_XT = 4, 5, 6, 7
    B_H, B_Y = B_TOK, B_D
    wd, wu, bd, bu = mlp["wd"], mlp["wu"], mlp["bd"], mlp["bu"]
    logitT = k.sb("slot_logitT", [NP, S])
    dT = k.sb("d_weightT", [NP, S])
    dw = k.sb("d_weight", [P, NT, NP])
    cw = k.sb("c_weight", [P, NT, NP])
    row1 = k.sb("c_row1", [P, NT])
    row2 = k.sb("c_row2", [P, NT])
    bank_max = k.sb("d_bank_max", [NP, NQ])
    neg_max = k.sb("d_neg_max", [NP, 1])
    xt = k.sb("x_tilde", [NP, D])
    dsum = k.sb("d_sum", [NP, 1])
    xtT = k.sb("x_tildeT", [KH, 2, NP])
    hid = k.sb("hid", [HDOWN, NP])
    hact = k.sb("hact", [HDOWN, NP])
    yT = k.sb("y_tildeT", [KH, 2, NP])
    y = k.sb("y_tilde", [NP, D])
    cT = k.sb("c_T", [NP, S])
    logit_made = k.sem("slot_logit_made")
    logit_kept = k.sem("slot_logit_kept")
    maxed = k.sem("slot_maxed")
    dv = k.sem("ffn0_vector")
    ac = k.sem("ffn0_scalar")
    pe = k.sem("ffn0_tensor")
    c_turned = k.sem("c_turned")
    c_kept = k.sem("c_kept")
    made = k.sem("ffn0_out_made")
    added = k.sem("ffn0_out_added")
    V_RMAX, V_LC, V_RSUM, V_RINV, V_C, V_DINV, V_XT, V_HB, V_YB = range(1, 10)
    A_DEXP, A_CEXP, A_DW, A_XTT, A_GELU, A_Y = range(1, 7)
    T_TOK, T_D, T_X, T_XT, T_H, T_YT, T_Y = range(1, 8)
    with nc.Block() as block:
        @block.gpsimd
        def _(pool):
            for x in splits:
                x.split(pool)

        @block.vector
        def _(dve):
            v = nc.vector
            for c in range(NQ):
                dve.wait_ge(logit_kept, c + 1)
                v.tensor_reduce(bank_max[:, c:c + 1], logitT[:, c * QW:(c + 1) * QW], AX.X, ALU.max).then_inc(maxed, 1)
            dve.wait_ge(maxed, NQ)
            v.tensor_reduce(neg_max[:, :], bank_max[:, :], AX.X, ALU.max, negate=True).then_inc(maxed, 1)
            tok = k.PS[:, B_TOK, :].rearrange("p (t n) -> p t n", t=NT)
            dve.wait_ge(pe, T_TOK)
            v.tensor_reduce(row1[:, :], tok, AX.X, ALU.max).then_inc(dv, 1)
            dve.wait_ge(dv, V_RMAX)
            v.tensor_tensor(cw[:, :, :], tok, row1[:, :].unsqueeze(2).to_broadcast([P, NT, NP]), ALU.subtract).then_inc(dv, 1)
            dve.wait_ge(ac, A_CEXP)
            v.tensor_reduce(row1[:, :], cw[:, :, :], AX.X, ALU.add).then_inc(dv, 1)
            dve.wait_ge(dv, V_RSUM)
            v.reciprocal(row2[:, :], row1[:, :]).then_inc(dv, 1)
            dve.wait_ge(dv, V_RINV)
            v.tensor_tensor(cw[:, :, :], cw[:, :, :], row2[:, :].unsqueeze(2).to_broadcast([P, NT, NP]), ALU.mult).then_inc(dv, 1)
            dve.wait_ge(pe, T_X)
            v.reciprocal(dsum[:, :], k.PS[0:NP, B_X, D:D + 1]).then_inc(dv, 1)
            dve.wait_ge(dv, V_DINV)
            v.tensor_scalar(xt[:, :], k.PS[0:NP, B_X, 0:D], dsum[:, 0:1], None, ALU.mult).then_inc(dv, 1)
            mlp["loads"].wait(dve)
            dve.wait_ge(pe, T_H)
            v.tensor_tensor(hid[:, :].rearrange("p (n s) -> p n s", n=NSLOT), k.PS[0:HDOWN, B_H, 0:NP].rearrange("p (n s) -> p n s", n=NSLOT),
                            bd[:, :].unsqueeze(2).to_broadcast([HDOWN, NSLOT, PSLOT]), ALU.add).then_inc(dv, 1)
            dve.wait_ge(pe, T_YT)
            v.tensor_tensor(yT[:, :, :].rearrange("p k (n s) -> p (k n) s", n=NSLOT),
                            k.PS[0:KH, B_Y, 0:2 * NP].rearrange("p (n s) -> p n s", n=2 * NSLOT),
                            bu[:, :, :].rearrange("p k n -> p (k n)").unsqueeze(2).to_broadcast([KH, 2 * NSLOT, PSLOT]),
                            ALU.add).then_inc(dv, 1)
            for t in range(NT):
                dve.wait_ge(made, t + 1)
                v.tensor_tensor(k.h[:, t, :], k.PS[:, t % 8, 0:D], k.h[:, t, :], ALU.add).then_inc(added, 1)
                if t >= 1:
                    k.stat(dve, t - 1, added, t)
            k.stat(dve, NT - 1, added, NT)

        @block.scalar
        def _(act):
            for c in range(NQ):
                act.wait_ge(logit_made, c + 1)
                nc.scalar.activation(logitT[:, c * QW:(c + 1) * QW], k.PS[0:NP, c, :], ACT.Copy).then_inc(logit_kept, 1)
            act.wait_ge(maxed, NQ + 1)
            act.wait_ge(logit_kept, NQ)
            nc.scalar.activation(dT[:, :], logitT[:, :], ACT.Exp, bias=neg_max[:, 0:1]).then_inc(ac, 1)
            act.wait_ge(dv, V_LC)
            nc.scalar.activation(cw[:, :, :], cw[:, :, :], ACT.Exp).then_inc(ac, 1)
            act.wait_ge(pe, T_D)
            nc.scalar.activation(dw[:, :, :], k.PS[:, B_D, :].rearrange("p (t n) -> p t n", t=NT), ACT.Copy).then_inc(ac, 1)
            for b in range(2):
                act.wait_ge(c_turned, b + 1)
                nc.scalar.activation(cT[:, b * 512:(b + 1) * 512], k.PS[0:NP, b, :], ACT.Copy).then_inc(c_kept, 1)
            act.wait_ge(pe, T_XT)
            nc.scalar.activation(xtT[:, :, :], k.PS[0:KH, B_XT, 0:2 * NP].rearrange("p (k n) -> p k n", k=2), ACT.Copy).then_inc(ac, 1)
            act.wait_ge(dv, V_HB)
            nc.scalar.activation(hact[:, :], hid[:, :], ACT.Gelu).then_inc(ac, 1)
            for b in range(2, 4):
                act.wait_ge(c_turned, b + 1)
                nc.scalar.activation(cT[:, b * 512:(b + 1) * 512], k.PS[0:NP, b, :], ACT.Copy).then_inc(c_kept, 1)
            act.wait_ge(pe, T_Y)
            nc.scalar.activation(y[:, :], k.PS[0:NP, B_XT, 0:D], ACT.Copy).then_inc(ac, 1)

        @block.tensor
        def _(te):
            mm = nc.tensor.matmul

            def turn_c(b):
                for i in range(4):
                    last = nc.tensor.transpose(k.PS[0:NP, b, i * P:(i + 1) * P], cw[:, 4 * b + i, :], k.ident)
                last.then_inc(c_turned, 1)

            for c in range(NQ):
                product_wx(nc, k.PS[0:NP, c, :], slots.high, slots.low, slice(0, NP),
                           k.xT, k.xl, slice(c * QW, (c + 1) * QW)).then_inc(logit_made, 1)
            small_ident = k.cst[0:NP, C_ID:C_ID + NP]
            te.wait_ge(logit_kept, NQ)
            for t in range(NT):
                last = nc.tensor.transpose(k.PS[:, B_TOK, t * NP:(t + 1) * NP], logitT[:, t * P:(t + 1) * P], small_ident)
            last.then_inc(pe, 1)
            te.wait_ge(ac, A_DEXP)
            for t in range(NT):
                last = nc.tensor.transpose(k.PS[:, B_D, t * NP:(t + 1) * NP], dT[:, t * P:(t + 1) * P], small_ident)
            last.then_inc(pe, 1)
            te.wait_ge(ac, A_DW)
            for t in range(NT):
                mm(k.PS[0:NP, B_X, 0:D], dw[:, t, :], k.xn[:, t, :], start=t == 0, stop=t == NT - 1, skip_group_check=True)
                last = mm(k.PS[0:NP, B_X, D:D + 1], dw[:, t, :], k.cst[:, C_ONE:C_ONE + 1], start=False, stop=t == NT - 1, skip_group_check=True)
            last.then_inc(pe, 1)
            te.wait_ge(dv, V_C)
            turn_c(0)
            turn_c(1)
            te.wait_ge(dv, V_XT)
            for half in range(2):
                last = nc.tensor.transpose(k.PS[0:KH, B_XT, half * NP:(half + 1) * NP], xt[:, half * KH:(half + 1) * KH], small_ident)
            last.then_inc(pe, 1)
            mlp["loads"].wait(te)
            te.wait_ge(ac, A_XTT)
            for n in range(NSLOT):
                for half in range(2):
                    last = mm(k.PS[0:HDOWN, B_H, n * PSLOT:(n + 1) * PSLOT], wd[:, half, n, :],
                              xtT[:, half, n * PSLOT:(n + 1) * PSLOT], start=half == 0, stop=half == 1)
            last.then_inc(pe, 1)
            turn_c(2)
            turn_c(3)
            te.wait_ge(ac, A_GELU)
            for half in range(2):
                for n in range(NSLOT):
                    last = mm(k.PS[0:KH, B_Y, half * NP + n * PSLOT:half * NP + (n + 1) * PSLOT],
                              wu[:, n, half * KH:(half + 1) * KH], hact[:, n * PSLOT:(n + 1) * PSLOT], start=True, stop=True)
            last.then_inc(pe, 1)
            te.wait_ge(dv, V_YB)
            for half in range(2):
                last = nc.tensor.transpose(k.PS[0:NP, B_XT, half * KH:(half + 1) * KH], yT[:, half, :], k.cst[0:KH, C_ID:C_ID + KH])
            last.then_inc(pe, 1)
            te.wait_ge(ac, A_Y)
            te.wait_ge(c_kept, 4)
            for t in range(NT):
                if t >= 8:
                    te.wait_ge(added, t - 7)
                mm(k.PS[:, t % 8, 0:D], cT[:, t * P:(t + 1) * P], y[:, :], start=True, stop=True).then_inc(made, 1)


def linear_project(nc, k, w, lin, loads):
    expx = k.sb("exp_x", [P, 2, QW])
    relu = k.sb("relu_x", [P, 2, QW])
    made = k.sem("lin_made")
    mapped = k.sem("mapped")
    joined = k.sem("joined")
    kept = k.sem("lin_kept")
    v_ones = k.sem("v_ones")
    units = [(m, pair, c) for m in "kq" for pair in range(NPAIR) for c in range(NQ)]
    NU = len(units)
    rest = [(what, t) for what in ("turn", "v", "gate") for t in range(NT)]
    with nc.Block() as block:
        @block.sync
        def _(sp):
            for x in loads:
                x.load(sp)

        @block.gpsimd
        def _(pool):
            nc.gpsimd.memset(lin["v"][:, :, :, D1:D1 + 1], 1.0)

        @block.tensor
        def _(te):
            for n, (m, pair, c) in enumerate(units):
                te.wait_ge(w[m].parts, 2)
                if n >= 8:
                    te.wait_ge(mapped, n - 7)
                product_wx(nc, k.PS[:, n % 8, :], w[m].high, w[m].low, slice(pair * P, (pair + 1) * P),
                           k.xT, k.xl, slice(c * QW, (c + 1) * QW)).then_inc(made, 1)
            for i, (what, t) in enumerate(rest):
                if i < 8:
                    te.wait_ge(mapped, NU - 7 + i)
                else:
                    te.wait_ge(kept, i - 7)
                bank = i % 8
                if what == "turn":
                    te.wait_ge(joined, NPAIR * NQ)
                    for pair in range(NPAIR):
                        last = nc.tensor.transpose(k.PS[:, bank, pair * P:(pair + 1) * P],
                                                   lin["kT"][:, pair, t * P:(t + 1) * P], k.ident)
                else:
                    n, m = (DIM1, "v") if what == "v" else (D, "g")
                    te.wait_ge(w[m].parts, 2)
                    last = product_xw(nc, k.PS[:, bank, 0:n], w[m].high, w[m].low, slice(0, n),
                                      k.xT, k.xl, slice(t * P, (t + 1) * P))
                last.then_inc(made, 1)

        @block.vector
        def _(dve):
            for n, (m, pair, c) in enumerate(units):
                dve.wait_ge(mapped, n + 1)
                nc.vector.scalar_tensor_tensor(lin[m + "T"][:, pair, c * QW:(c + 1) * QW], expx[:, n % 2, :], 1.0,
                                               relu[:, n % 2, :], ALU.min, ALU.add).then_inc(joined, 1)

        @block.scalar
        def _(act):
            for n in range(NU):
                act.wait_ge(made, n + 1)
                if n >= 2:
                    act.wait_ge(joined, n - 1)
                nc.scalar.activation(expx[:, n % 2, :], k.PS[:, n % 8, :], ACT.Exp)
                nc.scalar.activation(relu[:, n % 2, :], k.PS[:, n % 8, :], ACT.Relu).then_inc(mapped, 1)
            for i, (what, t) in enumerate(rest):
                act.wait_ge(made, NU + i + 1)
                ps = k.PS[:, i % 8, :]
                if what == "turn":
                    last = nc.scalar.activation(lin["k"][:, t, :], ps[:, 0:DIM1], ACT.Copy)
                elif what == "v":
                    last = nc.scalar.activation(lin["v"][:, t, :, 0:D1], ps[:, 0:DIM1].rearrange("p (h d) -> p h d", d=D1), ACT.Copy)
                else:
                    last = nc.scalar.activation(lin["gate"][:, t, :], ps[:, 0:D], ACT.Sigmoid)
                last.then_inc(kept, 1)


def linear_attention(nc, k, wo_loads, lin, loads):
    B_A, B_N, B_S, B_T, B_Y = 0, 2, 4, 5, 6
    STATES = 2
    HW = D1 + 1
    wo = lin["wo"]
    at = k.sb("lin_scores", [P, 2, 2, NPAIR, P])
    den = k.sb("lin_den", [P, 2, H1])
    inv = k.sb("lin_inv", [P, 2, H1])
    on = k.sb("lin_out", [P, 2, H1, D1])
    oT = k.sb("lin_outT", [P, 2, NPAIR, P])
    gated = k.sb("gated", [P, 2, D])
    states = k.sb("lin_states", [P, STATES, NPAIR, 2, HW])
    cleared = k.sem("lin_states_cleared")
    scored = k.sem("lin_scored")
    masked = k.sem("lin_masked")
    numed = k.sem("lin_numed")
    stated = k.sem("lin_stated")
    copied = k.sem("lin_state_copied")
    dened = k.sem("lin_dened")
    inved = k.sem("lin_inved")
    normed = k.sem("lin_normed")
    turned = k.sem("lin_turned")
    kept = k.sem("lin_outT_kept")
    made = k.sem("lin_y_made")
    gates = k.sem("lin_gated")
    added = k.sem("lin_added")
    ROUNDS = NT + 3
    with nc.Block() as block:
        @block.sync
        def _(sp):
            for x in loads:
                x.load(sp)

        @block.gpsimd
        def _(pool):
            nc.gpsimd.memset(states[:, :, :, :, :], 0.0).then_inc(cleared, 1)

        @block.tensor
        def _(te):
            mm = nc.tensor.matmul
            for r in range(ROUNDS):
                if r < NT:
                    c = r
                    if c >= 1:
                        te.wait_ge(masked, c)
                    for odd in range(2):
                        rows = slice(odd * D1, (odd + 1) * D1)
                        for pair in range(NPAIR):
                            last = mm(k.PS[:, B_A + odd, pair * P:(pair + 1) * P], lin["kT"][rows, pair, c * P:(c + 1) * P],
                                      lin["qT"][rows, pair, c * P:(c + 1) * P], start=True, stop=True)
                    last.then_inc(scored, 1)
                if r >= 3:
                    c = r - 3
                    if c == 0:
                        wo_loads.wait(te)
                    te.wait_ge(kept, c + 1)
                    if c >= 2:
                        te.wait_ge(gates, c - 1)
                    for pair in range(NPAIR):
                        last = mm(k.PS[:, B_Y + c % 2, 0:D], oT[:, c % 2, pair, :], wo[:, pair, :], start=pair == 0, stop=pair == NPAIR - 1)
                    last.then_inc(made, 1)
                if 1 <= r < NT:
                    c = r - 1
                    if c >= 1:
                        te.wait_ge(copied, c)
                    for pair in range(NPAIR):
                        last = mm(k.PS[:, B_S, pair * 2 * HW:(pair + 1) * 2 * HW], lin["k"][:, c, pair * P:(pair + 1) * P],
                                  lin["v"][:, c, 2 * pair:2 * pair + 2, :].rearrange("p o d -> p (o d)"), start=c == 0 and pair == 0,
                                  stop=pair == NPAIR - 1, skip_group_check=True)
                    last.then_inc(stated, 1)
                if 1 <= r < NT + 1:
                    c = r - 1
                    te.wait_ge(masked, c + 1)
                    if c >= 1:
                        te.wait_ge(copied, c)
                    if c >= 2:
                        te.wait_ge(normed, c - 1)
                    for pair in range(NPAIR):
                        out = k.PS[:, B_N + c % 2, pair * 2 * HW:(pair + 1) * 2 * HW]
                        if c:
                            mm(out, lin["qT"][:, pair, c * P:(c + 1) * P], states[:, (c - 1) % STATES, pair].rearrange("p o d -> p (o d)"),
                               start=pair == 0, stop=False, skip_group_check=True)
                        for odd in range(2):
                            last = mm(out[:, odd * HW:(odd + 1) * HW], at[:, c % 2, odd, pair, :], lin["v"][:, c, 2 * pair + odd, :],
                                      start=c == 0 and pair + odd == 0, stop=pair == NPAIR - 1 and odd == 1, skip_group_check=True)
                    last.then_inc(numed, 1)
                if 2 <= r < NT + 2:
                    c = r - 2
                    te.wait_ge(normed, c + 1)
                    if c >= 1:
                        te.wait_ge(kept, c)
                    for pair in range(NPAIR):
                        last = nc.tensor.transpose(k.PS[:, B_T, pair * P:(pair + 1) * P],
                                                   on[:, c % 2, 2 * pair:2 * pair + 2, :].rearrange("p o d -> p (o d)"), k.ident)
                    last.then_inc(turned, 1)

        @block.vector
        def _(dve):
            v = nc.vector
            for r in range(ROUNDS):
                if r < NT:
                    c = r
                    dve.wait_ge(scored, c + 1)
                    if c >= 2:
                        dve.wait_ge(numed, c - 1)
                    for odd in range(2):
                        last = v.tensor_tensor(at[:, c % 2, odd], k.PS[:, B_A + odd, 0:NPAIR * P].rearrange("p (q n) -> p q n", q=NPAIR),
                                               k.tri.unsqueeze(1).to_broadcast([P, NPAIR, P]), ALU.mult)
                    last.then_inc(masked, 1)
                if r >= 3:
                    c = r - 3
                    dve.wait_ge(made, c + 1)
                    v.tensor_tensor(gated[:, c % 2, :], k.PS[:, B_Y + c % 2, 0:D], lin["gate"][:, c, :], ALU.mult).then_inc(gates, 1)
                if 1 <= r < NT + 1:
                    c = r - 1
                    num = k.PS[:, B_N + c % 2, 0:H1 * HW].rearrange("p (h d) -> p h d", h=H1)
                    dve.wait_ge(numed, c + 1)
                    v.tensor_scalar(den[:, c % 2, :], num[:, :, D1], 1e-6, None, ALU.max).then_inc(dened, 1)
                    dve.wait_ge(dened, c + 1)
                    v.reciprocal(inv[:, c % 2, :], den[:, c % 2, :]).then_inc(inved, 1)
                    dve.wait_ge(inved, c + 1)
                    if c >= 2:
                        dve.wait_ge(turned, c - 1)
                    v.tensor_tensor(on[:, c % 2], num[:, :, 0:D1], inv[:, c % 2, :].unsqueeze(2).to_broadcast([P, H1, D1]),
                                    ALU.mult).then_inc(normed, 1)
                if r >= 3:
                    c = r - 3
                    dve.wait_ge(gates, c + 1)
                    v.tensor_tensor(k.h[:, c, :], k.h[:, c, :], gated[:, c % 2, :], ALU.add).then_inc(added, 1)
                if r >= 4:
                    k.stat(dve, r - 4, added, r - 3)
            k.stat(dve, NT - 1, added, NT)

        @block.scalar
        def _(act):
            for r in range(ROUNDS):
                if r >= 1 and r < NT:
                    c = r - 1
                    act.wait_ge(stated, c + 1)
                    if c == 0:
                        act.wait_ge(cleared, 1)
                    if c >= STATES:
                        act.wait_ge(numed, c - STATES + 2)
                    for odd in range(2):
                        rows = slice(odd * D1, (odd + 1) * D1)
                        last = nc.scalar.activation(states[rows, c % STATES, :, odd, :],
                                                    k.PS[rows, B_S, 0:NPAIR * 2 * HW].rearrange("p (q o d) -> p q o d", q=NPAIR, o=2)[:, :, odd, :],
                                                    ACT.Copy)
                    last.then_inc(copied, 1)
                if 2 <= r < NT + 2:
                    c = r - 2
                    act.wait_ge(turned, c + 1)
                    if c >= 2:
                        act.wait_ge(made, c - 1)
                    nc.scalar.activation(oT[:, c % 2], k.PS[:, B_T, 0:NPAIR * P].rearrange("p (q n) -> p q n", q=NPAIR),
                                         ACT.Copy).then_inc(kept, 1)


def route(nc, k, a, wr, moe):
    t1 = k.sb("route1", [P, NT, E])
    t2 = k.sb("route2", [P, NT, E])
    prob = k.sb("prob", [P, NT, E])
    row = k.sb("route_row", [P, 2, NT])
    mask = k.sb("mask", [P, NT, 2, E])
    maskb = k.sb("maskb", [P, NT, 2, E], BF16)
    place = k.sb("place", [P, NT, 2, E])
    B_LOG = 2
    logitT = k.sb("router_logitT", [E, S])
    logit_made = k.sem("router_logit_made")
    logit_kept = k.sem("router_logit_kept")
    made = k.sem("router_made")
    high_made = k.sem("xn_high_made")
    low_made = k.sem("xn_low_made")
    xh, xl = moe["xn_high"], moe["xn_low"]

    def columns(x, tiles):
        return x[:, tiles, 0:P], x[:, tiles, P:2 * P].rearrange("p t (c d) -> p t c d", c=2)

    def rows_of(tiles):
        return k.xn[:, tiles, 0:P], k.xn[:, tiles, P:D].unsqueeze(2).to_broadcast([P, TPG, 2, DB])

    def high_rows(g):
        tiles = slice(g * TPG, (g + 1) * TPG)
        for dst, src in zip(columns(xh, tiles), rows_of(tiles)):
            last = nc.scalar.activation(dst, src, ACT.Copy)
        last.then_inc(high_made, 1)

    dv = k.sem("route_vector")
    ac = k.sem("route_scalar")
    with nc.Block() as block:
        @block.sync
        def _(sp):
            load_expert(sp, a, moe, 0)

        @block.tensor
        def _(te):
            te.wait_ge(wr.parts, 2)
            for c in range(NQ):
                product_wx(nc, k.PS[0:E, B_LOG + c, :], wr.high, wr.low, slice(0, E),
                           k.xT, k.xl, slice(c * QW, (c + 1) * QW)).then_inc(logit_made, 1)
            for c in range(NQ):
                te.wait_ge(logit_kept, c + 1)
                for t in range(TPQ * c, TPQ * (c + 1)):
                    last = nc.tensor.transpose(k.PS[:, 0, t * E:(t + 1) * E], logitT[:, t * P:(t + 1) * P], k.cst[0:E, C_ID:C_ID + E])
            last.then_inc(made, 1)
            te.wait_ge(dv, MASKED_AT)
            nc.tensor.matmul(k.PS[:, 1, 0:2 * NT * E], k.trib[:, :], maskb[:, :, :, :].rearrange("p t c e -> p (t c e)"),
                             start=True, stop=False, skip_group_check=True)
            count = k.PS[:, 1, 0:2 * NT * E].rearrange("p (g i c e) -> p g i c e", i=TPG, c=2, e=E)
            by_group = maskb[:, :, :, :].rearrange("p (g i) c e -> p g i c e", i=TPG)
            for c in range(2):
                nc.tensor.matmul(count[:, :, 1, c, :], k.oneb[:, :], by_group[:, :, 0, c, :], start=False, stop=False, skip_group_check=True)
            for i in range(TPG):
                for other in range(TPG):
                    last = nc.tensor.matmul(count[:, :, i, 1, :], k.oneb[:, :], by_group[:, :, other, 0, :], start=False,
                                            stop=i + other == 2 * TPG - 2, skip_group_check=True)
            last.then_inc(made, 1)

        @block.scalar
        def _(act):
            for c in range(NQ):
                act.wait_ge(logit_made, c + 1)
                nc.scalar.activation(logitT[:, c * QW:(c + 1) * QW], k.PS[0:E, B_LOG + c, :], ACT.Copy).then_inc(logit_kept, 1)
                high_rows(c)
            act.wait_ge(dv, 2)
            nc.scalar.activation(t2[:, :, :], t1[:, :, :], ACT.Exp).then_inc(ac, 1)
            for g in range(NQ, GRP):
                high_rows(g)
            moe["sel_loads"].wait(act)
            nc.scalar.activation(moe["sel"][:, :, :], moe["sel_raw"][:, :, :], ACT.Copy)
            act.wait_ge(moe["wi_landed"], 48)
            nc.scalar.activation(moe["wih"][:, 0], moe["wi"][:, :, :], ACT.Copy).then_inc(moe["wi_high"], 1)

        @block.gpsimd
        def _(pool):
            for g in range(GRP):
                tiles = slice(g * TPG, (g + 1) * TPG)
                for n, (dst, src, high) in enumerate(zip(columns(xl, tiles), rows_of(tiles), columns(xh, tiles))):
                    pool.wait_ge(high_made, g + 1)
                    nc.gpsimd.tensor_tensor(dst, src, high.bitcast(F32), ALU.subtract).then_inc(low_made, 1)
            pool.wait_ge(moe["wi_high"], 1)
            nc.gpsimd.tensor_tensor(moe["wil"][:, 0], moe["wi"][:, :, :], moe["wih"][:, 0].bitcast(F32), ALU.subtract).then_inc(moe["wi_low"], 1)

        @block.vector
        def _(dve):
            v = nc.vector
            steps = [0]

            def wide(x):
                return x.unsqueeze(2).to_broadcast([P, NT, E])

            def then(ins):
                steps[0] += 1
                ins.then_inc(dv, 1)
                dve.wait_ge(dv, steps[0])

            logits = k.PS[:, 0, 0:NT * E].rearrange("p (t e) -> p t e", t=NT)
            dve.wait_ge(made, 1)
            then(v.tensor_reduce(row[:, 0, :], logits, AX.X, ALU.max))
            then(v.tensor_tensor(t1[:, :, :], logits, wide(row[:, 0, :]), ALU.subtract))
            dve.wait_ge(ac, 1)
            then(v.tensor_reduce(row[:, 0, :], t2[:, :, :], AX.X, ALU.add))
            then(v.reciprocal(row[:, 1, :], row[:, 0, :]))
            then(v.tensor_tensor(prob[:, :, :], t2[:, :, :], wide(row[:, 1, :]), ALU.mult))
            rank = k.cst[:, C_RANK:C_RANK + E].unsqueeze(1).to_broadcast([P, NT, E])
            for c in range(2):
                src = prob if c == 0 else t2
                then(v.tensor_reduce(row[:, 0, :], src[:, :, :], AX.X, ALU.max))
                then(v.tensor_tensor(t1[:, :, :], src[:, :, :], wide(row[:, 0, :]), ALU.is_equal))
                then(v.tensor_tensor(t1[:, :, :], t1[:, :, :], rank, ALU.mult))
                then(v.tensor_reduce(row[:, 1, :], t1[:, :, :], AX.X, ALU.max))
                then(v.tensor_tensor(mask[:, :, c, :], t1[:, :, :], wide(row[:, 1, :]), ALU.is_equal))
                if c == 0:
                    then(v.scalar_tensor_tensor(t2[:, :, :], mask[:, :, 0, :], -2.0, prob[:, :, :], ALU.mult, ALU.add))
            then(v.tensor_copy(maskb[:, :, :, :], mask[:, :, :, :]))
            assert steps[0] == MASKED_AT
            then(v.tensor_tensor(t1[:, :, :], mask[:, :, 0, :], mask[:, :, 1, :], ALU.add))
            then(v.tensor_tensor(moe["gate"][:, :, :], t1[:, :, :], prob[:, :, :], ALU.mult))
            dve.wait_ge(made, 2)
            then(v.tensor_tensor(place[:, :, :, :], k.PS[:, 1, 0:2 * NT * E].rearrange("p (t c e) -> p t c e", c=2, e=E),
                                 mask[:, :, :, :], ALU.mult))
            then(v.tensor_tensor(t1[:, :, :], place[:, :, 0, :], place[:, :, 1, :], ALU.add))
            then(v.tensor_scalar(moe["place"][:, :, :], t1[:, :, :], -1.0, None, ALU.add))


MASKED_AT = 17


def dispatch(nc, k, moe):
    disp = k.sb("disp", [P, 2, TPG, E, CAP], F32R)
    xh, xl = moe["xn_high"], moe["xn_low"]
    routes = k.sb("routes", [P, NT, 4, E], BF16)
    rest = k.sb("gate_rest", [P, NT, E])
    listed = k.sem("disp_listed")
    made = k.sem("disp_made")
    kept = k.sem("disp_kept")
    parted = k.sem("routes_parted")
    turned = k.sem("routes_turned")
    with nc.Block() as block:
        @block.vector
        def _(dve):
            for g in range(GRP):
                if g >= 2:
                    dve.wait_ge(made, 4 * (g - 1))
                for i in range(TPG):
                    t = g * TPG + i
                    last = nc.vector.tensor_tensor(disp[:, g % 2, i], k.cst[:, C_IOTA:C_IOTA + CAP].unsqueeze(1).to_broadcast([P, E, CAP]),
                                                   moe["place"][:, t, :].unsqueeze(2).to_broadcast([P, E, CAP]), ALU.is_equal)
                last.then_inc(listed, 1)
            nc.vector.tensor_copy(routes[:, :, 0, :], moe["place"][:, :, :]).then_inc(parted, 1)
            nc.vector.tensor_copy(routes[:, :, 1, :], moe["gate"][:, :, :]).then_inc(parted, 1)
            dve.wait_ge(parted, 2)
            nc.vector.tensor_tensor(rest[:, :, :], moe["gate"][:, :, :], routes[:, :, 1, :], ALU.subtract).then_inc(parted, 1)
            dve.wait_ge(parted, 3)
            nc.vector.tensor_copy(routes[:, :, 2, :], rest[:, :, :]).then_inc(parted, 1)
            dve.wait_ge(parted, 4)
            nc.vector.tensor_tensor(routes[:, :, 3, :], rest[:, :, :], routes[:, :, 2, :], ALU.subtract).then_inc(parted, 1)
            dve.wait_ge(turned, 2)
            nc.vector.tensor_copy(moe["routesT"][:, 8 * P:16 * P], k.PS[:, 1, :].bitcast(BF16)[0:4 * E, 0:8 * P])

        @block.tensor
        def _(te):
            n = 0
            for g in range(GRP):
                te.wait_ge(listed, g + 1)
                for at in range(2):
                    for eh in range(2):
                        if n >= 8:
                            te.wait_ge(kept, n - 7)
                        for x in (xh, xl):
                            for i in range(TPG):
                                last = nc.tensor.matmul(k.PS[:, n % 8, 0:EHALF], x[:, g * TPG + i, at * P:(at + 1) * P],
                                                        disp[:, g % 2, i, eh * 4:(eh + 1) * 4, :].rearrange("p e c -> p (e c)"),
                                                        start=x is xh and i == 0, stop=x is xl and i == TPG - 1)
                        last.then_inc(made, 1)
                        n += 1
            te.wait_ge(parted, 5)
            for b in range(2):
                te.wait_ge(kept, n - 7 + b)
                for i in range(8):
                    last = nc.tensor.transpose(k.PS[:, b, :].bitcast(BF16)[0:4 * E, i * P:(i + 1) * P],
                                               routes[:, 8 * b + i].rearrange("p r e -> p (r e)"), k.identb[:, :])
                last.then_inc(turned, 1)

        @block.scalar
        def _(act):
            n = 0
            for g in range(GRP):
                for at in range(2):
                    for eh in range(2):
                        act.wait_ge(made, n + 1)
                        nc.scalar.activation(moe["xin"][:, eh * 4:(eh + 1) * 4, at, :, g, :],
                                             k.PS[:, n % 8, 0:EHALF].rearrange("p (e s c) -> p e s c", s=ST, c=CT), ACT.Copy).then_inc(kept, 1)
                        n += 1
            act.wait_ge(turned, 1)
            nc.scalar.activation(moe["routesT"][:, 0:8 * P], k.PS[:, 0, :].bitcast(BF16)[0:4 * E, 0:8 * P], ACT.Copy)


def load_expert(sp, a, moe, e):
    for rows, at, where in ((slice(0, P), 0, slice(0, P)), (slice(P, D), 1, slice(0, DB)), (slice(P, D), 1, slice(DB, P))):
        sp.dma_start(moe["wi"][where, at, :], a["L1_ffn_wi"][e, rows, :]).then_inc(moe["wi_landed"], 16)
    if e >= 1:
        sp.wait_ge(moe["wo_parts"], 3 * e)
    sp.dma_start(moe["wo"][:, :, :], a["L1_ffn_wo"][e].rearrange("(f p) d -> p f d", p=P)).then_inc(moe["wo_landed"], 16)


def load_slots(sp, moe, kt):
    for e in range(kt * P // CAP, ((kt + 1) * P - 1) // CAP + 1):
        sp.wait_ge(moe["stored"][e % 2], 16 * ST * (e // 2 + 1))
    sp.dma_start(moe["eo"][:, kt, :, :], moe["scratch"].rearrange("g e c d -> g (e c) d")[:, kt * P:(kt + 1) * P, :]
                 .rearrange("g p d -> p g d")).then_inc(moe["eo_loaded"][kt], 16)


def experts(nc, k, a, moe):
    HALVES = 2
    SH = SLOTS // HALVES
    wi, wo = moe["wi"], moe["wo"]
    wih, wil = moe["wih"], moe["wil"]
    xh = k.sb("xin_high", [P, 2, 2, SLOTS], F32R)
    xl = k.sb("xin_low", [P, 2, SLOTS], F32R)
    wop = k.sb("wo_parts", [P, NF, 2, D], F32R)
    hh, hl = (k.sb(f"hid_{x}", [P, NF, SLOTS], F32R) for x in ("high", "low"))
    eo = k.sb("expert_out", [P, 2, ST, D])
    wi_landed, wo_landed, wo_parts = moe["wi_landed"], moe["wo_landed"], moe["wo_parts"]
    x_high = k.sem("xin_high_made")
    x_low = k.sem("xin_low_made")
    wi_high, wi_low = moe["wi_high"], moe["wi_low"]
    made = k.sem("expert_made")
    hid_high = k.sem("hid_high_made")
    hid_low = k.sem("hid_low_made")
    outed = k.sem("expert_outed")
    halved = k.sem("expert_halved")
    kept = k.sem("expert_kept")
    stored = moe["stored"]
    spread = k.sem("routes_spread")
    matched = k.sem("slots_matched")
    weighed = k.sem("slots_weighed")
    UN = NF * HALVES
    RING, ORING = 4, 2
    B_O, B_PLACE, B_GATE = RING, RING + ORING, RING + ORING + 1
    SPLIT_WO, SPLIT_X = (1, 3), (5, 8)
    SPREADS = [(0, -1), (0, -1)] + [(e, u) for e in range(E - 2) for u in (2, 7, UN + 1)]
    KT_OF = [(kt, q) for q in range(NQ) for kt in range(ST)]
    assert len(SPREADS) == len(KT_OF)

    def f(x):
        return x.bitcast(F32)

    def spreads_behind(e, u):
        return [w for w, where in enumerate(SPREADS) if where == (e, u)]

    with nc.Block() as block:
        @block.sync
        def _(sp):
            for e in range(E):
                if e + 1 < E:
                    sp.wait_ge(wi_low, e + 1)
                    load_expert(sp, a, moe, e + 1)
                for kt in range(ST):
                    if ((kt + 1) * P - 1) // CAP == e - 1:
                        load_slots(sp, moe, kt)
                for s in range(ST):
                    sp.wait_ge(kept, ST * e + s + 1)
                    sp.dma_start(moe["scratch"][:, e, s * CT:(s + 1) * CT, :], eo[:, e % 2, s, :]).then_inc(stored[e % 2], 16)

        @block.gpsimd
        def _(pool):
            for e in range(E):
                pool.wait_ge(wo_parts, 3 * e + 2)
                nc.gpsimd.tensor_tensor(wop[:, :, 1, :], wo[:, :, :], f(wop[:, :, 0, :]), ALU.subtract).then_inc(wo_parts, 1)
                if e + 1 < E:
                    if e >= 1:
                        pool.wait_ge(made, UN * e)
                    pool.wait_ge(wi_landed, 48 * (e + 2))
                    nc.gpsimd.tensor_copy(wih[:, (e + 1) % 2], wi[:, :, :]).then_inc(wi_high, 1)
                    pool.wait_ge(wi_high, e + 2)
                    nc.gpsimd.tensor_tensor(wil[:, (e + 1) % 2], wi[:, :, :], f(wih[:, (e + 1) % 2]), ALU.subtract).then_inc(wi_low, 1)

        @block.tensor
        def _(te):
            mm = nc.tensor.matmul

            def spread_routes(e, u):
                for w in spreads_behind(e, u):
                    kt, q = KT_OF[w]
                    if w:
                        te.wait_ge(weighed, w)
                    for i, bank in enumerate((B_PLACE, B_GATE)):
                        last = mm(k.PS[:, bank, :], moe["sel"][:, i, kt * P:(kt + 1) * P], moe["routesT"][:, q * QW:(q + 1) * QW],
                                  start=True, stop=True)
                    last.then_inc(spread, 1)

            n = m = 0
            for e in range(E):
                spread_routes(e, -1)
                te.wait_ge(x_low, e + 1)
                te.wait_ge(wi_low, e + 1)
                for u in range(UN):
                    s, t = u // NF, u % NF
                    if n >= RING:
                        te.wait_ge(hid_low, n - RING + 1)
                    product_wx(nc, k.PS[:, n % RING, 0:SH], wih[:, e % 2], wil[:, e % 2], slice(t * P, (t + 1) * P),
                               xh[:, e % 2], xl[:, e % 2], slice(s * SH, (s + 1) * SH)).then_inc(made, 1)
                    n += 1
                    spread_routes(e, u)
                te.wait_ge(wo_parts, 3 * (e + 1))
                for s in range(ST):
                    te.wait_ge(hid_low, UN * e + (NF if (s + 1) * P <= SH else UN))
                    if m >= ORING:
                        te.wait_ge(kept, m - ORING + 1)
                    out = k.PS[:, B_O + m % ORING, 0:2 * D]
                    rows = slice(s * P, (s + 1) * P)
                    for t in range(NF):
                        mm(out, hh[:, t, rows], wop[:, t].rearrange("p k d -> p (k d)"), start=t == 0, stop=False, skip_group_check=True)
                        last = mm(out[:, 0:D], hl[:, t, rows], wop[:, t, 0, :], start=False, stop=t == NF - 1, skip_group_check=True)
                    last.then_inc(outed, 1)
                    m += 1
                    spread_routes(e, UN + s)

        @block.vector
        def _(dve):
            def low_x(e):
                dve.wait_ge(x_high, 2 * (e + 1))
                x = moe["xin"][:, e].rearrange("p k s g c -> p k (s g c)")
                high = xh[:, e % 2]
                nc.vector.tensor_tensor(xl[:, e % 2], x[:, 0], f(high[:, 0, :]), ALU.subtract)
                nc.vector.tensor_tensor(high[DB:P, 1, :], x[DB:P, 1], f(high[DB:P, 1, :]), ALU.subtract).then_inc(x_low, 1)

            def keep(e, s):
                n = ST * e + s
                dve.wait_ge(halved, n + 1)
                nc.vector.tensor_tensor(eo[:, e % 2, s, :], k.PS[:, B_O + n % ORING, D:2 * D], eo[:, e % 2, s, :], ALU.add).then_inc(kept, 1)

            def weigh(e, u):
                for w in spreads_behind(e, u):
                    kt, q = KT_OF[w]
                    part = moe["combT"][:, kt, q * QW:(q + 1) * QW]
                    dve.wait_ge(spread, w + 1)
                    nc.vector.tensor_scalar(part, k.PS[:, B_PLACE, :], k.cst[:, C_CROW + kt:C_CROW + kt + 1], None, ALU.is_equal).then_inc(matched, 1)
                    dve.wait_ge(matched, w + 1)
                    nc.vector.tensor_tensor(part, part, k.PS[:, B_GATE, :], ALU.mult).then_inc(weighed, 1)

            low_x(0)
            for e in range(E):
                weigh(e, -1)
                for u in range(UN):
                    s, t = u // NF, u % NF
                    n = UN * e + u
                    dve.wait_ge(hid_high, n + 1)
                    nc.vector.scalar_tensor_tensor(hl[:, t, s * SH:(s + 1) * SH], k.PS[:, n % RING, 0:SH], 0.0, f(hh[:, t, s * SH:(s + 1) * SH]),
                                                   ALU.max, ALU.subtract).then_inc(hid_low, 1)
                    weigh(e, u)
                for s in range(ST):
                    keep(e, s)
                    weigh(e, UN + s)
                    if s == 0 and e + 1 < E:
                        low_x(e + 1)

        @block.scalar
        def _(act):
            def high_x(e, at):
                if e >= 2:
                    act.wait_ge(made, UN * (e - 1))
                nc.scalar.activation(xh[:, e % 2, at], moe["xin"][:, e, at].rearrange("p s g c -> p (s g c)"), ACT.Copy).then_inc(x_high, 1)

            def high_wo(e, piece):
                if e:
                    act.wait_ge(outed, ST * e)
                act.wait_ge(wo_landed, 16 * (e + 1))
                tiles = slice(piece * NF // 2, (piece + 1) * NF // 2)
                nc.scalar.activation(wop[:, tiles, 0, :], wo[:, tiles, :], ACT.Copy).then_inc(wo_parts, 1)

            def keep(e, s):
                n = ST * e + s
                act.wait_ge(outed, n + 1)
                if s == 0 and e >= 2:
                    act.wait_ge(stored[e % 2], 16 * ST * (e // 2))
                nc.scalar.activation(eo[:, e % 2, s, :], k.PS[:, B_O + n % ORING, 0:D], ACT.Copy).then_inc(halved, 1)

            high_x(0, 0)
            high_x(0, 1)
            for e in range(E):
                for u in range(UN):
                    s, t = u // NF, u % NF
                    n = UN * e + u
                    act.wait_ge(made, n + 1)
                    if e and t == 0:
                        act.wait_ge(outed, ST * (e - 1) + (SH // P + 1 if s == 0 else ST))
                    nc.scalar.activation(hh[:, t, s * SH:(s + 1) * SH], k.PS[:, n % RING, 0:SH], ACT.Relu).then_inc(hid_high, 1)
                    if u in SPLIT_WO:
                        high_wo(e, SPLIT_WO.index(u))
                    if u in SPLIT_X and e + 1 < E:
                        high_x(e + 1, SPLIT_X.index(u))
                for s in range(ST):
                    keep(e, s)


def combine(nc, k, moe, out):
    FIRST = 6
    made = k.sem("comb_made")
    added = k.sem("comb_added")
    stored = k.sem("stored")
    with nc.Block() as block:
        @block.vector
        def _(dve):
            for t in range(NT):
                dve.wait_ge(made, t + 1)
                nc.vector.tensor_tensor(k.h[:, t, :], k.PS[:, t % 8, 0:D], k.h[:, t, :], ALU.add).then_inc(added, 1)

        @block.tensor
        def _(te):
            def product(t, kt):
                return nc.tensor.matmul(k.PS[:, t % 8, 0:D], moe["combT"][:, kt, t * P:(t + 1) * P], moe["eo"][:, kt, t // TPG, :],
                                        start=kt == 0, stop=kt == ST - 1)

            for t in range(FIRST):
                for kt in range(ST - 1):
                    if t == 0:
                        te.wait_ge(moe["eo_loaded"][kt], 16)
                    product(t, kt)
            te.wait_ge(moe["eo_loaded"][ST - 1], 16)
            for t in range(NT):
                if t >= 8:
                    te.wait_ge(added, t - 7)
                for kt in range(ST - 1 if t < FIRST else 0, ST):
                    last = product(t, kt)
                last.then_inc(made, 1)

        @block.sync
        def _(sp):
            load_slots(sp, moe, ST - 1)
            view = out.rearrange("(q t p) d -> q p t d", p=P, t=4)
            for q in range(NT // 4):
                sp.wait_ge(added, 4 * q + 4)
                sp.dma_start(view[q], k.h[:, 4 * q:4 * q + 4, :]).then_inc(stored, 16)
            sp.wait_ge(stored, 16 * (NT // 4))


def program(nc, a, out):
    with ExitStack() as ctx:
        k = Core(nc, ctx)
        w_router = Weights(nc, k, "w_router", a["L1_ffn_w_router"])
        with k.room():
            slots = Slots(nc, k, a)
            mlp = mlp_weights(k, a)
            with k.room():
                att = {
                    "scratch": nc.dram_tensor("qk_parts", [2, 3, D, S], BF16, kind="Internal").ap(),
                    "o": k.sb("o0", [P, NG, S]),
                    "v": k.sb("v0", [P, NT, H0, HROW]),
                    "ks": k.sb("ks", [P, 2, HG, S], BF16),
                    "qm": k.sb("qm", [P, 2, HG // 2, S], BF16),
                    "km": k.sb("km", [P, 2, HG // 2, S], BF16),
                    "stored": [k.sem(f"parts_stored{i}") for i in range(4)],
                    "m_loaded": [[k.sem(f"mstack_loaded_{m}{g}") for g in range(NG)] for m in "qk"],
                    "s_loaded": [[k.sem(f"stack_loaded_{m}{g}") for g in range(NG)] for m in "qk"],
                    "wo": k.sb("wo0", [P, NG, D]),
                }
                att["wo_loads"] = Loads(k.nc, k.sem("wo0_landed"), [
                    (att["wo"][HROW * j:HROW * j + DK0, :, :], a["wo0"].rearrange("(g j r) o -> j r g o", j=HG, r=DK0)[j])
                    for j in range(HG)])
                with k.room():
                    k.rows(0)
                    w = [Weights(nc, k, f"w0_{m}", a[f"w{m}0"]) for m in "qkv"]
                    with k.room():
                        embed(nc, k, a, att, loads=w)
                    layernorm(nc, k, splits=w)
                    with k.room():
                        softmax_qkv(nc, k, w, att)
                with k.room():
                    att["qs"] = k.sb("qs", [P, 2, HG, S], BF16)
                    softmax_attention(nc, k, a, att)
                softmax_out(nc, k, att, loads=[slots, mlp["loads"]])
            k.rows(1)
            w = {m: Weights(nc, k, f"w1_{m}", a[f"L1_attn_W{m}"]) for m in "kqvg"}
            layernorm(nc, k, loads=w.values(), slots=slots, l2=True)
            with k.room():
                slot_mixture(nc, k, slots, mlp, splits=w.values())
            layernorm(nc, k)
            with k.room():
                lin = {
                    "qT": k.sb("lin_qT", [P, NPAIR, S]),
                    "kT": k.sb("lin_kT", [P, NPAIR, S]),
                    "k": k.sb("lin_k", [P, NT, DIM1]),
                    "v": k.sb("lin_v", [P, NT, H1, D1 + 1]),
                    "gate": k.sb("lin_gate", [P, NT, D]),
                    "wo": k.sb("wo1", [P, NPAIR, D]),
                }
                wo_loads = Loads(k.nc, k.sem("wo1_landed"), [(lin["wo"][:, :, :], a["L1_attn_Wo"].rearrange("(k p) o -> p k o", p=P))])
                with k.room():
                    linear_project(nc, k, w, lin, loads=[wo_loads])
                with k.room():
                    linear_attention(nc, k, wo_loads, lin, loads=[w_router])
        slots = k.sb("moe_slots", [P, E * 2 * SLOTS])
        moe = {
            "gate": k.sb("moe_gate", [P, NT, E]),
            "place": k.sb("moe_place", [P, NT, E]),
            "sel": k.sb("moe_sel", [4 * E, 2, E * CAP], BF16),
            "routesT": k.sb("moe_routesT", [4 * E, S], BF16),
            "xin": slots[:, :].rearrange("p (e k s g c) -> p e k s g c", e=E, k=2, s=ST, g=GRP),
            "eo": slots[:, 0:ST * GRP * D].rearrange("p (k g d) -> p k g d", k=ST, g=GRP),
            "wi": k.sb("wi", [P, 2, F]),
            "wo": k.sb("wo2", [P, NF, D]),
            "wih": k.sb("wi_high", [P, 2, 2, F], F32R),
            "wil": k.sb("wi_low", [P, 2, 2, F], F32R),
            "stored": [k.sem(f"expert_stored{i}") for i in range(2)],
            "wi_landed": k.sem("wi_landed"),
            "wi_high": k.sem("wi_high_made"),
            "wi_low": k.sem("wi_low_made"),
            "wo_landed": k.sem("wo_landed"),
            "wo_parts": k.sem("wo_parts_made"),
            "eo_loaded": [k.sem(f"eo_loaded{kt}") for kt in range(ST)],
            "scratch": nc.dram_tensor("expert_rows", [GRP, E, CAP, D], F32, kind="Internal").ap(),
        }
        with k.room():
            k.rows(2)
            moe["sel_raw"] = k.sb("sel", [4 * E, 2, E * CAP])
            moe["sel_loads"] = Loads(k.nc, k.sem("sel_landed"), [(moe["sel_raw"][:, :, :], a["sel"])])
            moe["xn_high"] = k.sb("xn_high", [P, NT, 2 * P], F32R)
            moe["xn_low"] = k.sb("xn_low", [P, NT, 2 * P], F32R)
            layernorm(nc, k, loads=[moe["sel_loads"]], splits=[w_router])
            with k.room():
                route(nc, k, a, w_router, moe)
            with k.room():
                dispatch(nc, k, moe)
        with k.room():
            moe["combT"] = k.sb("combT", [P, ST, S])
            with k.room():
                experts(nc, k, a, moe)
            combine(nc, k, moe, out)


_HOST = {
    "L0_attn_Wq": "wq0", "L0_attn_Wk": "wk0", "L0_attn_Wv": "wv0", "L0_attn_Wo": "wo0",
}


def laid_out(inputs):
    arrays = {}
    for name, x in inputs.items():
        x = np.asarray(x)
        arrays[_HOST.get(name, name)] = np.ascontiguousarray(x.T) if name in _HOST else np.ascontiguousarray(x)
    arrays["L0_ffn_scale"] = arrays["L0_ffn_scale"].reshape(1, 1)
    arrays["consts"], arrays["pe"], arrays["sel"] = constants()
    return arrays


def kernel(**inputs):
    import concourse.bacc as _bacc
    from concourse.bass_utils import run_bass_kernel_spmd as _run

    nc = _bacc.Bacc("TRN2", target_bir_lowering=False, num_devices=1)
    arrays, a = {}, {}
    for name, x in laid_out(inputs).items():
        arrays[f"in_{name}"] = x
        a[name] = nc.dram_tensor(f"in_{name}", x.shape, mybir.dt.from_np(x.dtype), kind="ExternalInput").ap()
    out = nc.dram_tensor("out_0", (S, D), F32, kind="ExternalOutput").ap()
    program(nc, a, out)
    r = _run(nc, [arrays], core_ids=[0])
    return r.results[0]["out_0"].reshape(1, S, D)
```
